# Optimizing a Trainium2 kernel written in Bass

```python
import numpy as np
import jax
import jax.numpy as jnp

def _softmax(x, axis=-1):
    return jax.nn.softmax(x, axis=axis)

def _gelu(x):
    return jax.nn.gelu(x, approximate=True)

def _silu(x):
    return jax.nn.silu(x)

def _sigmoid(x):
    return jax.nn.sigmoid(x)

def _layernorm(x, axis=-1, eps=1e-05):
    m = jnp.mean(x, axis=axis, keepdims=True)
    v = jnp.var(x, axis=axis, keepdims=True)
    return (x - m) / jnp.sqrt(v + eps)

def _scatter_add(tgt, idx, src, axis=0):
    return tgt.at[idx].add(src)

def _segment_sum(src, seg, n):
    return jax.ops.segment_sum(src, seg, n)
kernel_name = 'mk_conv_attn_hybrid_d4_conv_nhwc256_r4_d57b45'

def setup_inputs(seed: int=0):
    np.random.seed(seed)
    _w = jnp.asarray

    def _rec_inputs():
        import jax
        import jax.numpy as jnp
        _gk = jax.random.key(seed)
        x = -0.000125 + 0.9999 * jax.random.normal(jax.random.fold_in(_gk, 1), (32, 16, 16, 64), jnp.float32)
        return x
    x = _rec_inputs()

    def _L0_conv_setup():
        import jax, jax.numpy as jnp
        import numpy as np
        WS, SS, HEADS = (8, 4, 8)

        def _static_consts(H, W):
            ws, ss = (WS, SS)
            r = np.arange(-(ws - 1), ws, dtype=np.float32)
            tbl = np.stack(np.meshgrid(r, r, indexing='ij'), axis=-1)
            tbl = tbl / (ws - 1) * 8.0
            tbl = np.sign(tbl) * np.log2(np.abs(tbl) + 1.0) / np.log2(8.0)
            tbl = tbl.reshape(-1, 2)
            c = np.stack(np.meshgrid(np.arange(ws), np.arange(ws), indexing='ij')).reshape(2, -1)
            rel = (c[:, :, None] - c[:, None, :]).transpose(1, 2, 0).copy()
            rel[..., 0] += ws - 1
            rel[..., 1] += ws - 1
            rel[..., 0] *= 2 * ws - 1
            idx = rel.sum(-1)
            img = np.zeros((H, W), dtype=np.int32)
            cnt = 0
            for hs in (slice(0, -ws), slice(-ws, -ss), slice(-ss, None)):
                for wsl in (slice(0, -ws), slice(-ws, -ss), slice(-ss, None)):
                    img[hs, wsl] = cnt
                    cnt += 1
            mw = img.reshape(H // ws, ws, W // ws, ws).transpose(0, 2, 1, 3).reshape(-1, ws * ws)
            mask = np.where(mw[:, None, :] != mw[:, :, None], -100.0, 0.0).astype(np.float32)
            return (jnp.asarray(tbl), jnp.asarray(idx), jnp.asarray(mask))

        def _fwd(x, Wq, bq, Wk, bk, Wv, bv, Wo, bo, logit_scale, cpb_w1, cpb_b1, cpb_w2):
            B, H, W, C = x.shape
            ws, ss, h = (WS, SS, HEADS)
            N, dh = (ws * ws, C // HEADS)
            tbl, idx, mask = _static_consts(H, W)
            xs = jnp.roll(x, (-ss, -ss), axis=(1, 2))
            nh, nw = (H // ws, W // ws)
            xw = xs.reshape(B, nh, ws, nw, ws, C).transpose(0, 1, 3, 2, 4, 5).reshape(B * nh * nw, N, C)

            def proj(t, Wm, bm):
                return (t @ Wm.T + bm).reshape(-1, N, h, dh).transpose(0, 2, 1, 3)
            q, k, v = (proj(xw, Wq, bq), proj(xw, Wk, bk), proj(xw, Wv, bv))
            qn = q / jnp.maximum(jnp.linalg.norm(q, axis=-1, keepdims=True), 1e-12)
            kn = k / jnp.maximum(jnp.linalg.norm(k, axis=-1, keepdims=True), 1e-12)
            scale = jnp.exp(jnp.minimum(logit_scale, jnp.log(100.0)))
            attn = jnp.einsum('whnd,whmd->whnm', qn, kn) * scale[None]
            bias = 16.0 * jax.nn.sigmoid(jax.nn.relu(tbl @ cpb_w1.T + cpb_b1) @ cpb_w2.T)
            attn = attn + bias[idx].transpose(2, 0, 1)[None]
            attn = attn.reshape(B, nh * nw, h, N, N) + mask[None, :, None]
            attn = jax.nn.softmax(attn, axis=-1).reshape(B * nh * nw, h, N, N)
            out = jnp.einsum('whnm,whmd->whnd', attn, v).transpose(0, 2, 1, 3).reshape(-1, N, C)
            out = out @ Wo.T + bo
            out = out.reshape(B, nh, nw, ws, ws, C).transpose(0, 1, 3, 2, 4, 5).reshape(B, H, W, C)
            return jnp.roll(out, (ss, ss), axis=(1, 2))
        key = jax.random.key(seed)
        ks = jax.random.split(key, 12)
        B, H, W, C = (32, 16, 16, 64)
        p = lambda i, shp, s=0.05: jax.random.normal(ks[i], shp, dtype=jnp.float32) * s
        return {'x': p(0, (B, H, W, C), 1.0), 'Wq': p(1, (C, C)), 'bq': p(2, (C,)), 'Wk': p(3, (C, C)), 'bk': p(4, (C,)), 'Wv': p(5, (C, C)), 'bv': p(6, (C,)), 'Wo': p(7, (C, C)), 'bo': p(8, (C,)), 'logit_scale': jnp.full((HEADS, 1, 1), jnp.log(10.0), dtype=jnp.float32), 'cpb_w1': p(9, (128, 2)), 'cpb_b1': p(10, (128,)), 'cpb_w2': p(11, (HEADS, 128))}
    _L0_conv_all = _L0_conv_setup()
    _L0_conv_in = {k: v for k, v in _L0_conv_all.items() if k in ('Wq', 'bq', 'Wk', 'bk', 'Wv', 'bv', 'Wo', 'bo', 'logit_scale', 'cpb_w1', 'cpb_b1', 'cpb_w2')}
    del _L0_conv_all

    def _L1_conv_setup():
        import jax, jax.numpy as jnp
        import numpy as np
        F = 64
        K = 3
        G = 16
        RR = 4
        BN_EPS = 0.001
        key = jax.random.key(seed)
        ks = jax.random.split(key, 8)
        C = 64
        Cr = F // RR
        KKG = K * K * G
        s = lambda k, sh, fan: jax.random.normal(k, sh, jnp.float32) * (1.0 / np.sqrt(fan))
        return {'x': jax.random.normal(ks[0], (4, 32, 32, C), jnp.float32), 'Wr': s(ks[1], (C, Cr), C), 'br': jnp.zeros((Cr,), jnp.float32), 'gamma': jnp.ones((Cr,), jnp.float32), 'beta': jnp.zeros((Cr,), jnp.float32), 'mean': jax.random.normal(ks[2], (Cr,), jnp.float32) * 0.1, 'var': jax.random.uniform(ks[3], (Cr,), jnp.float32, 0.5, 1.5), 'Ws': s(ks[4], (Cr, KKG), Cr), 'bs': jnp.zeros((KKG,), jnp.float32), 'Wi': s(ks[5], (C, F), C), 'bi': jnp.zeros((F,), jnp.float32)}
    _L1_conv_all = _L1_conv_setup()
    _L1_conv_in = {k: v for k, v in _L1_conv_all.items() if k in ('Wr', 'br', 'gamma', 'beta', 'mean', 'var', 'Ws', 'bs', 'Wi', 'bi')}
    del _L1_conv_all

    def _L2_attn_setup():
        import math
        import jax, jax.numpy as jnp
        import numpy as np
        EPS_DIV = 1e-07
        EPS_NORM = 1e-12

        def _l2_normalize(x, axis):
            n = jnp.sqrt(jnp.sum(x * x, axis=axis, keepdims=True))
            return x / jnp.maximum(n, EPS_NORM)
        key = jax.random.key(seed)
        ks = jax.random.split(key, 5)
        b, N, C = (8, 1024, 64)
        x = jax.random.normal(ks[0], (b, N, C), dtype=jnp.float32)
        W_qkv = jax.random.normal(ks[1], (C, 3 * C), dtype=jnp.float32) * (1.0 / math.sqrt(C))
        b_qkv = jax.random.normal(ks[2], (3 * C,), dtype=jnp.float32) * 0.02
        W_out = jax.random.normal(ks[3], (C, C), dtype=jnp.float32) * (1.0 / math.sqrt(C))
        b_out = jax.random.normal(ks[4], (C,), dtype=jnp.float32) * 0.02
        return {'x': x, 'W_qkv': W_qkv, 'b_qkv': b_qkv, 'W_out': W_out, 'b_out': b_out}
    _L2_attn_all = _L2_attn_setup()
    _L2_attn_in = {k: v for k, v in _L2_attn_all.items() if k in ('W_qkv', 'b_qkv', 'W_out', 'b_out')}
    del _L2_attn_all

    def _L2_ffn_setup():
        import math
        import jax, jax.numpy as jnp
        import numpy as np
        CAPACITY_FACTOR = 1.25
        TOP_K = 2
        LN_EPS = 1e-05

        def _layer_norm(x, gamma, beta):
            mu = jnp.mean(x, axis=-1, keepdims=True)
            var = jnp.var(x, axis=-1, keepdims=True)
            return (x - mu) * jax.lax.rsqrt(var + LN_EPS) * gamma + beta
        key = jax.random.key(seed)
        ks = jax.random.split(key, 4)
        B, S, D, F, E = (8, 1024, 64, 128, 8)
        x = jax.random.normal(ks[0], (B, S, D), dtype=jnp.float32)
        Wr = jax.random.normal(ks[1], (D, E), dtype=jnp.float32) / np.sqrt(D)
        br = jnp.zeros((E,), jnp.float32)
        W1 = jax.random.normal(ks[2], (E, D, F), dtype=jnp.float32) / np.sqrt(D)
        b1 = jnp.zeros((E, F), jnp.float32)
        W2 = jax.random.normal(ks[3], (E, F, D), dtype=jnp.float32) / np.sqrt(F)
        b2 = jnp.zeros((E, D), jnp.float32)
        gamma = jnp.ones((D,), jnp.float32)
        beta = jnp.zeros((D,), jnp.float32)
        return {'x': x, 'Wr': Wr, 'br': br, 'W1': W1, 'b1': b1, 'W2': W2, 'b2': b2, 'gamma': gamma, 'beta': beta}
    _L2_ffn_all = _L2_ffn_setup()
    _L2_ffn_in = {k: v for k, v in _L2_ffn_all.items() if k in ('Wr', 'br', 'W1', 'b1', 'W2', 'b2', 'gamma', 'beta')}
    del _L2_ffn_all

    def _L3_attn_setup():
        import jax, jax.numpy as jnp
        import numpy as np
        EPS_NORM = 1e-06
        EPS_ATTN = 1e-06
        HEADS = 8

        def rmsnorm(x, w):
            ms = jnp.mean(x * x, axis=-1, keepdims=True)
            return w * (x * jax.lax.rsqrt(ms + EPS_NORM))

        def linear_attention(x, w_qkv, w_out, b_out):
            B, N, D = x.shape
            hd = D // HEADS
            qkv = (x @ w_qkv).reshape(B, N, 3, HEADS, hd)
            q, k, v = (qkv[:, :, 0], qkv[:, :, 1], qkv[:, :, 2])
            q = jax.nn.elu(q) + 1.0
            k = jax.nn.elu(k) + 1.0
            kv = jnp.einsum('bnhd,bnhm->bhdm', k, v)
            z = 1.0 / (jnp.einsum('bnhd,bhd->bnh', q, k.sum(axis=1)) + EPS_ATTN)
            out = jnp.einsum('bnhd,bhdm,bnh->bnhm', q, kv, z)
            out = out.reshape(B, N, D)
            return out @ w_out + b_out
        key = jax.random.key(seed)
        ks = jax.random.split(key, 4)
        B, N, D = (16, 2048, 64)
        x = jax.random.normal(ks[0], (B, N, D), dtype=jnp.float32)
        w_norm1 = jnp.ones((D,), dtype=jnp.float32)
        w_qkv = jax.random.normal(ks[1], (D, 3 * D), dtype=jnp.float32) * 0.02
        w_out = jax.random.normal(ks[2], (D, D), dtype=jnp.float32) * 0.02
        b_out = jnp.zeros((D,), dtype=jnp.float32)
        w_norm2 = jnp.ones((D,), dtype=jnp.float32)
        return {'x': x, 'w_norm1': w_norm1, 'w_qkv': w_qkv, 'w_out': w_out, 'b_out': b_out, 'w_norm2': w_norm2}
    _L3_attn_all = _L3_attn_setup()
    _L3_attn_in = {k: v for k, v in _L3_attn_all.items() if k in ('w_norm1', 'w_qkv', 'w_out', 'b_out', 'w_norm2')}
    del _L3_attn_all

    def _L3_ffn_setup():
        import jax, jax.numpy as jnp
        import numpy as np
        N_EXPERTS = 8
        TOP_K = 2
        key = jax.random.key(seed)
        ks = jax.random.split(key, 5)
        B, T, C, E, H = (8, 512, 64, 8, 682)
        scale = 1.0 / np.sqrt(C)
        return {'x': jax.random.normal(ks[0], (B, T, C), dtype=jnp.float32), 'router_w': jax.random.normal(ks[1], (E, C), dtype=jnp.float32) * scale, 'w1': jax.random.normal(ks[2], (E, H, C), dtype=jnp.float32) * scale, 'w2': jax.random.normal(ks[3], (E, C, H), dtype=jnp.float32) * (1.0 / np.sqrt(H)), 'w3': jax.random.normal(ks[4], (E, H, C), dtype=jnp.float32) * scale}
    _L3_ffn_all = _L3_ffn_setup()
    _L3_ffn_in = {k: v for k, v in _L3_ffn_all.items() if k in ('router_w', 'w1', 'w2', 'w3')}
    del _L3_ffn_all
    return {'x': x, 'L0_conv_Wq': _L0_conv_in['Wq'], 'L0_conv_bq': _L0_conv_in['bq'], 'L0_conv_Wk': _L0_conv_in['Wk'], 'L0_conv_bk': _L0_conv_in['bk'], 'L0_conv_Wv': _L0_conv_in['Wv'], 'L0_conv_bv': _L0_conv_in['bv'], 'L0_conv_Wo': _L0_conv_in['Wo'], 'L0_conv_bo': _L0_conv_in['bo'], 'L0_conv_logit_scale': _L0_conv_in['logit_scale'], 'L0_conv_cpb_w1': _L0_conv_in['cpb_w1'], 'L0_conv_cpb_b1': _L0_conv_in['cpb_b1'], 'L0_conv_cpb_w2': _L0_conv_in['cpb_w2'], 'L1_conv_Wr': _L1_conv_in['Wr'], 'L1_conv_br': _L1_conv_in['br'], 'L1_conv_gamma': _L1_conv_in['gamma'], 'L1_conv_beta': _L1_conv_in['beta'], 'L1_conv_mean': _L1_conv_in['mean'], 'L1_conv_var': _L1_conv_in['var'], 'L1_conv_Ws': _L1_conv_in['Ws'], 'L1_conv_bs': _L1_conv_in['bs'], 'L1_conv_Wi': _L1_conv_in['Wi'], 'L1_conv_bi': _L1_conv_in['bi'], 'L2_attn_W_qkv': _L2_attn_in['W_qkv'], 'L2_attn_b_qkv': _L2_attn_in['b_qkv'], 'L2_attn_W_out': _L2_attn_in['W_out'], 'L2_attn_b_out': _L2_attn_in['b_out'], 'L2_ffn_Wr': _L2_ffn_in['Wr'], 'L2_ffn_br': _L2_ffn_in['br'], 'L2_ffn_W1': _L2_ffn_in['W1'], 'L2_ffn_b1': _L2_ffn_in['b1'], 'L2_ffn_W2': _L2_ffn_in['W2'], 'L2_ffn_b2': _L2_ffn_in['b2'], 'L2_ffn_gamma': _L2_ffn_in['gamma'], 'L2_ffn_beta': _L2_ffn_in['beta'], 'L3_attn_w_norm1': _L3_attn_in['w_norm1'], 'L3_attn_w_qkv': _L3_attn_in['w_qkv'], 'L3_attn_w_out': _L3_attn_in['w_out'], 'L3_attn_b_out': _L3_attn_in['b_out'], 'L3_attn_w_norm2': _L3_attn_in['w_norm2'], 'L3_ffn_router_w': _L3_ffn_in['router_w'], 'L3_ffn_w1': _L3_ffn_in['w1'], 'L3_ffn_w2': _L3_ffn_in['w2'], 'L3_ffn_w3': _L3_ffn_in['w3']}

def reference(x, L0_conv_Wq, L0_conv_bq, L0_conv_Wk, L0_conv_bk, L0_conv_Wv, L0_conv_bv, L0_conv_Wo, L0_conv_bo, L0_conv_logit_scale, L0_conv_cpb_w1, L0_conv_cpb_b1, L0_conv_cpb_w2, L1_conv_Wr, L1_conv_br, L1_conv_gamma, L1_conv_beta, L1_conv_mean, L1_conv_var, L1_conv_Ws, L1_conv_bs, L1_conv_Wi, L1_conv_bi, L2_attn_W_qkv, L2_attn_b_qkv, L2_attn_W_out, L2_attn_b_out, L2_ffn_Wr, L2_ffn_br, L2_ffn_W1, L2_ffn_b1, L2_ffn_W2, L2_ffn_b2, L2_ffn_gamma, L2_ffn_beta, L3_attn_w_norm1, L3_attn_w_qkv, L3_attn_w_out, L3_attn_b_out, L3_attn_w_norm2, L3_ffn_router_w, L3_ffn_w1, L3_ffn_w2, L3_ffn_w3):
    import jax
    import jax.numpy as jnp

    def _L0_conv_ref(x, Wq, bq, Wk, bk, Wv, bv, Wo, bo, logit_scale, cpb_w1, cpb_b1, cpb_w2):
        import jax, jax.numpy as jnp
        import numpy as np
        WS, SS, HEADS = (8, 4, 8)

        def _static_consts(H, W):
            ws, ss = (WS, SS)
            r = np.arange(-(ws - 1), ws, dtype=np.float32)
            tbl = np.stack(np.meshgrid(r, r, indexing='ij'), axis=-1)
            tbl = tbl / (ws - 1) * 8.0
            tbl = np.sign(tbl) * np.log2(np.abs(tbl) + 1.0) / np.log2(8.0)
            tbl = tbl.reshape(-1, 2)
            c = np.stack(np.meshgrid(np.arange(ws), np.arange(ws), indexing='ij')).reshape(2, -1)
            rel = (c[:, :, None] - c[:, None, :]).transpose(1, 2, 0).copy()
            rel[..., 0] += ws - 1
            rel[..., 1] += ws - 1
            rel[..., 0] *= 2 * ws - 1
            idx = rel.sum(-1)
            img = np.zeros((H, W), dtype=np.int32)
            cnt = 0
            for hs in (slice(0, -ws), slice(-ws, -ss), slice(-ss, None)):
                for wsl in (slice(0, -ws), slice(-ws, -ss), slice(-ss, None)):
                    img[hs, wsl] = cnt
                    cnt += 1
            mw = img.reshape(H // ws, ws, W // ws, ws).transpose(0, 2, 1, 3).reshape(-1, ws * ws)
            mask = np.where(mw[:, None, :] != mw[:, :, None], -100.0, 0.0).astype(np.float32)
            return (jnp.asarray(tbl), jnp.asarray(idx), jnp.asarray(mask))

        def _fwd(x, Wq, bq, Wk, bk, Wv, bv, Wo, bo, logit_scale, cpb_w1, cpb_b1, cpb_w2):
            B, H, W, C = x.shape
            ws, ss, h = (WS, SS, HEADS)
            N, dh = (ws * ws, C // HEADS)
            tbl, idx, mask = _static_consts(H, W)
            xs = jnp.roll(x, (-ss, -ss), axis=(1, 2))
            nh, nw = (H // ws, W // ws)
            xw = xs.reshape(B, nh, ws, nw, ws, C).transpose(0, 1, 3, 2, 4, 5).reshape(B * nh * nw, N, C)

            def proj(t, Wm, bm):
                return (t @ Wm.T + bm).reshape(-1, N, h, dh).transpose(0, 2, 1, 3)
            q, k, v = (proj(xw, Wq, bq), proj(xw, Wk, bk), proj(xw, Wv, bv))
            qn = q / jnp.maximum(jnp.linalg.norm(q, axis=-1, keepdims=True), 1e-12)
            kn = k / jnp.maximum(jnp.linalg.norm(k, axis=-1, keepdims=True), 1e-12)
            scale = jnp.exp(jnp.minimum(logit_scale, jnp.log(100.0)))
            attn = jnp.einsum('whnd,whmd->whnm', qn, kn) * scale[None]
            bias = 16.0 * jax.nn.sigmoid(jax.nn.relu(tbl @ cpb_w1.T + cpb_b1) @ cpb_w2.T)
            attn = attn + bias[idx].transpose(2, 0, 1)[None]
            attn = attn.reshape(B, nh * nw, h, N, N) + mask[None, :, None]
            attn = jax.nn.softmax(attn, axis=-1).reshape(B * nh * nw, h, N, N)
            out = jnp.einsum('whnm,whmd->whnd', attn, v).transpose(0, 2, 1, 3).reshape(-1, N, C)
            out = out @ Wo.T + bo
            out = out.reshape(B, nh, nw, ws, ws, C).transpose(0, 1, 3, 2, 4, 5).reshape(B, H, W, C)
            return jnp.roll(out, (ss, ss), axis=(1, 2))
        return _fwd(x, Wq, bq, Wk, bk, Wv, bv, Wo, bo, logit_scale, cpb_w1, cpb_b1, cpb_w2)

    def _L1_conv_ref(x, Wr, br, gamma, beta, mean, var, Ws, bs, Wi, bi):
        import jax, jax.numpy as jnp
        import numpy as np
        F = 64
        K = 3
        G = 16
        RR = 4
        BN_EPS = 0.001
        B, H, W, _ = x.shape
        KK = K * K
        r = jnp.einsum('bhwc,cd->bhwd', x, Wr) + br
        r = jax.nn.relu((r - mean) * jax.lax.rsqrt(var + BN_EPS) * gamma + beta)
        w = jnp.einsum('bhwd,dk->bhwk', r, Ws) + bs
        w = w.reshape(B, H, W, G, KK)[:, :, :, :, None, :]
        xi = jnp.einsum('bhwc,cf->bhwf', x, Wi) + bi
        pad = (K - 1) // 2
        xp = jnp.pad(xi, ((0, 0), (pad, pad), (pad, pad), (0, 0)))
        patches = jnp.stack([xp[:, i:i + H, j:j + W, :] for i in range(K) for j in range(K)], axis=3)
        patches = patches.reshape(B, H, W, G, F // G, KK)
        out = jnp.sum(w * patches, axis=-1)
        return out.reshape(B, H, W, F)

    def _L2_attn_ref(x, W_qkv, b_qkv, W_out, b_out):
        import math
        import jax, jax.numpy as jnp
        import numpy as np
        EPS_DIV = 1e-07
        EPS_NORM = 1e-12

        def _l2_normalize(x, axis):
            n = jnp.sqrt(jnp.sum(x * x, axis=axis, keepdims=True))
            return x / jnp.maximum(n, EPS_NORM)
        b, N, C = x.shape
        qkv = x @ W_qkv + b_qkv
        q, k, v = jnp.split(qkv, 3, axis=2)
        q = q - jnp.mean(q, axis=2, keepdims=True)
        k = k - jnp.mean(k, axis=2, keepdims=True)
        q2 = q * q
        k2 = k * k
        q2s = jnp.sum(q2, axis=2, keepdims=True)
        k2s = jnp.sum(k2, axis=2, keepdims=True)
        k2 = _l2_normalize(k2 / (k2s + EPS_DIV), axis=-2)
        q2 = _l2_normalize(q2 / (q2s + EPS_DIV), axis=-1)
        kv = jnp.einsum('bnc,bnd->bcd', k2, v)
        t2 = jnp.einsum('bnc,bcd->bnd', q2, kv) / math.sqrt(N)
        attn = v + t2
        return attn @ W_out + b_out

    def _L2_ffn_ref(x, Wr, br, W1, b1, W2, b2, gamma, beta):
        import math
        import jax, jax.numpy as jnp
        import numpy as np
        CAPACITY_FACTOR = 1.25
        TOP_K = 2
        LN_EPS = 1e-05

        def _layer_norm(x, gamma, beta):
            mu = jnp.mean(x, axis=-1, keepdims=True)
            var = jnp.var(x, axis=-1, keepdims=True)
            return (x - mu) * jax.lax.rsqrt(var + LN_EPS) * gamma + beta
        B, S, D = x.shape
        E = Wr.shape[1]
        N = B * S
        K = TOP_K
        logits = jnp.mean(x, axis=1) @ Wr + br
        routing_weights = jax.nn.softmax(logits, axis=-1)
        capacity = float(math.ceil(N * CAPACITY_FACTOR / E))
        expected_loads = routing_weights.sum(axis=0) * (N / B)
        scale = jnp.where(expected_loads > capacity, capacity / expected_loads, 1.0)
        routing_weights = jax.nn.softmax(routing_weights * scale, axis=-1)
        rw_tok = jnp.broadcast_to(routing_weights[:, None, :], (B, S, E)).reshape(N, E)
        top_w, top_i = jax.lax.top_k(rw_tok, K)
        top_w = jax.nn.softmax(top_w, axis=-1)
        xf = x.reshape(N, D)
        h = jax.nn.gelu(jnp.einsum('nd,edf->enf', xf, W1) + b1[:, None, :], approximate=False)
        y = jnp.einsum('enf,efd->end', h, W2) + b2[:, None, :]
        w_dense = jnp.zeros((N, E), x.dtype).at[jnp.arange(N)[:, None], top_i].add(top_w)
        out = jnp.einsum('ne,end->nd', w_dense, y).reshape(B, S, D)
        out = _layer_norm(out + x, gamma, beta)
        return out

    def _L3_attn_ref(x, w_norm1, w_qkv, w_out, b_out, w_norm2):
        import jax, jax.numpy as jnp
        import numpy as np
        EPS_NORM = 1e-06
        EPS_ATTN = 1e-06
        HEADS = 8

        def rmsnorm(x, w):
            ms = jnp.mean(x * x, axis=-1, keepdims=True)
            return w * (x * jax.lax.rsqrt(ms + EPS_NORM))

        def linear_attention(x, w_qkv, w_out, b_out):
            B, N, D = x.shape
            hd = D // HEADS
            qkv = (x @ w_qkv).reshape(B, N, 3, HEADS, hd)
            q, k, v = (qkv[:, :, 0], qkv[:, :, 1], qkv[:, :, 2])
            q = jax.nn.elu(q) + 1.0
            k = jax.nn.elu(k) + 1.0
            kv = jnp.einsum('bnhd,bnhm->bhdm', k, v)
            z = 1.0 / (jnp.einsum('bnhd,bhd->bnh', q, k.sum(axis=1)) + EPS_ATTN)
            out = jnp.einsum('bnhd,bhdm,bnh->bnhm', q, kv, z)
            out = out.reshape(B, N, D)
            return out @ w_out + b_out
        h = x + linear_attention(rmsnorm(x, w_norm1), w_qkv, w_out, b_out)
        return h + rmsnorm(h, w_norm2)

    def _L3_ffn_ref(x, router_w, w1, w2, w3):
        import jax, jax.numpy as jnp
        import numpy as np
        N_EXPERTS = 8
        TOP_K = 2
        B, T, C = x.shape
        flat = x.reshape(-1, C)
        logits = flat @ router_w.T
        probs = jax.nn.softmax(logits, axis=-1)
        topk_probs, topk_idx = jax.lax.top_k(probs, TOP_K)
        topk_probs = topk_probs / (jnp.sum(topk_probs, axis=-1, keepdims=True) + 1e-09)
        onehot = jax.nn.one_hot(topk_idx, N_EXPERTS, dtype=flat.dtype)
        gates = jnp.einsum('nk,nke->ne', topk_probs, onehot)
        h1 = jnp.einsum('nc,ehc->neh', flat, w1)
        h3 = jnp.einsum('nc,ehc->neh', flat, w3)
        h = jax.nn.silu(h1) * h3
        y = jnp.einsum('neh,ech->nec', h, w2)
        out = jnp.einsum('ne,nec->nc', gates, y)
        return out.reshape(B, T, C)

    def _gn(v, G=32, eps=1e-05):
        B_, H_, W_, C_ = v.shape
        g = v.reshape(B_, H_, W_, G, C_ // G)
        m = jnp.mean(g, axis=(1, 2, 4), keepdims=True)
        s = jnp.var(g, axis=(1, 2, 4), keepdims=True)
        return ((g - m) / jnp.sqrt(s + eps)).reshape(v.shape)

    def _ln_c(v, eps=1e-06):
        m = jnp.mean(v, axis=-1, keepdims=True)
        s = jnp.var(v, axis=-1, keepdims=True)
        return (v - m) / jnp.sqrt(s + eps)

    def _ln_t(v, eps=1e-05):
        m = jnp.mean(v, axis=-1, keepdims=True)
        s = jnp.var(v, axis=-1, keepdims=True)
        return (v - m) / jnp.sqrt(s + eps)

    def _to_tokens(v):
        B_, H_, W_, C_ = v.shape
        return v.reshape(B_, H_ * W_, C_)

    def _from_tokens(t, like):
        return t.reshape(like.shape)
    x = x + _L0_conv_ref(_gn(x), L0_conv_Wq, L0_conv_bq, L0_conv_Wk, L0_conv_bk, L0_conv_Wv, L0_conv_bv, L0_conv_Wo, L0_conv_bo, L0_conv_logit_scale, L0_conv_cpb_w1, L0_conv_cpb_b1, L0_conv_cpb_w2)
    x = x + _L1_conv_ref(_gn(x), L1_conv_Wr, L1_conv_br, L1_conv_gamma, L1_conv_beta, L1_conv_mean, L1_conv_var, L1_conv_Ws, L1_conv_bs, L1_conv_Wi, L1_conv_bi)
    t = _to_tokens(x)
    t = t + _L2_attn_ref(_ln_t(t), L2_attn_W_qkv, L2_attn_b_qkv, L2_attn_W_out, L2_attn_b_out)
    t = t + _L2_ffn_ref(_ln_t(t), L2_ffn_Wr, L2_ffn_br, L2_ffn_W1, L2_ffn_b1, L2_ffn_W2, L2_ffn_b2, L2_ffn_gamma, L2_ffn_beta)
    t = t + _L3_attn_ref(_ln_t(t), L3_attn_w_norm1, L3_attn_w_qkv, L3_attn_w_out, L3_attn_b_out, L3_attn_w_norm2)
    t = t + _L3_ffn_ref(_ln_t(t), L3_ffn_router_w, L3_ffn_w1, L3_ffn_w2, L3_ffn_w3)
    x = _from_tokens(t, x)
    return x

_drawn_inputs = setup_inputs


def setup_inputs(seed=0):
    import zlib

    import numpy as np

    out = dict(_drawn_inputs(seed))
    spreads = {'L0_conv_logit_scale': (2.3025851249694824, 0.2),
     'L1_conv_br': (0.0, 0.1),
     'L1_conv_gamma': (1.0, 0.2),
     'L1_conv_beta': (0.0, 0.1),
     'L1_conv_bs': (0.0, 0.1),
     'L1_conv_bi': (0.0, 0.1),
     'L2_ffn_br': (0.0, 0.1),
     'L2_ffn_b1': (0.0, 0.504),
     'L2_ffn_b2': (0.0, 0.359),
     'L2_ffn_gamma': (1.0, 0.2),
     'L2_ffn_beta': (0.0, 0.29),
     'L3_attn_w_norm1': (1.0, 0.6),
     'L3_attn_b_out': (0.0, 0.1),
     'L3_attn_w_norm2': (1.0, 0.2)}
    factors = {'L0_conv_cpb_w1': 8.0,
     'L0_conv_cpb_b1': 8.0,
     'L0_conv_cpb_w2': 8.0,
     'L2_attn_b_out': 3.277,
     'L3_attn_w_qkv': 8.0,
     'L3_attn_w_out': 8.0}
    for name, (base, spread) in spreads.items():
        noise = np.random.default_rng([zlib.crc32(name.encode()), seed]).standard_normal(out[name].shape)
        drawn = base * np.exp(spread * noise) if base else spread * noise
        out[name] = jnp.asarray(drawn.astype(out[name].dtype))
    for name, factor in factors.items():
        out[name] = (out[name] * factor).astype(out[name].dtype)
    return out
```

```python
import concourse.bass as bass
from concourse import mybir
from contextlib import ExitStack
import numpy as np

F32 = mybir.dt.float32
ALU = mybir.AluOpType
ACT = mybir.ActivationFunctionType
AX = mybir.AxisListType.X

STOP_AFTER = 5

B, HH, WW, C = 32, 16, 16, 64
HALF = B // 2
N = HH * WW
P = 2 * C
COLS = HALF * N
CHUNK = 512
NCH = COLS // CHUNK
WS, SS, HEADS, DH = 8, 4, 8, 8
WT = WS * WS
NWIN = N // WT
PAIRS = COLS // WT
HP = HEADS // 2
VW = 34
RR, KK, PH = 16, 9, HH + 2
E, FH = 8, 128
HB, NHB = 114, 6
TILES = COLS // 128

MATS = ["ident", "mean", "centre", "pair", "head", "sum", "stack",
        "wq0", "wk0", "wv0", "wo0", "wi1", "wr1", "wq2t", "wk2t", "wv2", "wo2",
        "wq4", "wk4", "wv4", "wo4", "rt3", "rt5"]
VECS = (["bq0", "bk0", "bv0", "bo0", "ls0", "bi1", "br1", "ga1", "be1", "mu1", "va1",
         "bq2", "bk2", "bv2", "bo2", "ga3", "be3", "n14", "bo4", "n24", "cb1",
         "eps6", "eps5", "eps3", "tiny", "ln20", "ln16", "guard", "one", "par0", "par1", "half0", "half1"]
        + [f"w2c{h}" for h in range(HEADS)] + [f"b1_{e}" for e in range(E)]
        + [f"b2_{e}" for e in range(E)] + [f"brr{k}" for k in range(2 * E)]
        + [f"rank{e}" for e in range(E)])
M = {n: i for i, n in enumerate(MATS)}
V = {n: i for i, n in enumerate(VECS)}

STEPS = {
    "pe_projected": [("q_proj", 8), ("k_proj", 8), ("v_proj", 16), ("l0_wo", 8), ("r_proj", 8), ("xi_proj", 8),
                     ("w2_centred", 5), ("k2_proj", 8), ("v2_proj", 8), ("q2_proj", 8), ("t2", 8), ("o2_proj", 8),
                     ("k4_proj", 8), ("v4_proj", 8), ("q4_proj", 8), ("o4_proj", 8)],
    "pe_summed": [("bias_hid", 16), ("bias_z", 1), ("g0_grp", 1), ("q_ssq", 8), ("k_ssq", 8), ("g1_grp", 1),
                  ("k2_norm", 1), ("kv2", 16), ("q2_s1", 8), ("r3_logits", 1), ("r3_load", 1), ("r3_gates", 1),
                  ("kv4", 16), ("ks4", 1), ("num4", 8)],
    "pe_mean": [("q2_s2", 8), ("n4_ms", 8), ("den4", 8), ("m4_ms", 8)],
    "ln_centred": [("a2_cen", 8), ("a3_cen", 8), ("l3_cen", 8), ("a4_cen", 8), ("a5_cen", 8)],
    "ln_variance": [("a2_var", 8), ("a3_var", 8), ("l3_var", 8), ("a4_var", 8), ("a5_var", 8)],
    "act_first": [("bias_relu", 16), ("q_sq", 8), ("k_sq", 8), ("r_ready", 8), ("xi_kept", 8), ("a2_sq", 8),
                  ("k2_sq", 8), ("k2_fourth", 8), ("k2_ln", 1), ("k2_rs", 1), ("q2_sq", 8), ("t2_kept", 8),
                  ("a3_sq", 8), ("l3_sq", 8), ("a4_sq", 8), ("n4_sq", 8), ("k4_exp", 8), ("q4_exp", 8),
                  ("z4_ln", 8), ("m4_sq", 8), ("a5_sq", 8)],
    "act_second": [("bias_exp", 1), ("qscale", 1), ("g0_sd", 1), ("q_len", 8), ("k_len", 8), ("g1_sd", 1),
                   ("bn_sd", 1), ("a2_ln", 8), ("q2_ln", 8), ("a3_ln", 8), ("sm1_exp", 1), ("sm2_exp", 1),
                   ("sm3_exp", 1), ("l3_ln", 8), ("a4_ln", 8), ("n4_ln", 8), ("z4", 8), ("m4_ln", 8), ("a5_ln", 8)],
    "act_rstd": [("a2_rstd", 8), ("q2_rs", 8), ("a3_rstd", 8), ("l3_rstd", 8), ("a4_rstd", 8), ("n4_rstd", 8),
                 ("m4_rstd", 8), ("a5_rstd", 8)],
    "l0_vector": [("hmask", 1), ("lsc", 1), ("vx_ones", 2), ("g0_stats", 16), ("g0_aggr", 16)],
    "l0_norms": [("bias_v", 3), ("bm_ready", 4), ("q_biased", 8), ("q_clip", 8), ("q_rlen", 8), ("q_norm", 8),
                 ("k_biased", 8), ("k_clip", 8), ("k_rlen", 8), ("k_norm", 8), ("v_ready", 32)],
    "l1_vector": [("l0_res", 8), ("x1_ready", 9), ("g1_stats", 16), ("g1_aggr", 16)],
    "l2_vector": [("a2", 8), ("w2_kept", 5), ("k2_biased", 8), ("v2_kept", 8), ("k2_sum", 9), ("k2_inv", 1),
                  ("k2_ready", 8), ("k2_clip", 1), ("kv2_kept", 16), ("q2_clip", 8), ("x3_ready", 8),
                  ("a3", 8), ("r3_mean", 8), ("sm1_in", 1), ("r3_rw", 1), ("sm2_in", 1), ("sm3_in", 1),
                  ("r3_diag", 1), ("gates2", 1), ("b2_prod", 2), ("y3_kept", 16), ("l3", 8), ("x4_part", 8),
                  ("x4_ready", 8)],
    "l3_vector": [("a4", 8), ("n4", 8), ("k4_neg", 8), ("v4_kept", 8), ("q4_neg", 8),
                  ("o4", 8), ("h4", 8), ("x5_part", 8), ("m4", 8), ("x5_ready", 8), ("a5", 8)],
    "vector_second": [("q2_ready", 8), ("k4_elu", 8), ("kv4_kept", 8), ("q4_elu", 8)],
}
PLACE = {}
for _group, _steps in STEPS.items():
    _base = 0
    for _step, _n in _steps:
        PLACE[_step] = _group, _base
        _base += _n


def network(nc, xw_d, xi_d, mats_d, vecs_d, feats_d, cw1_d, wmask_d, taps_d, wexp_d,
            w1l2_d, w2l2_d, w1l3_d, w3l3_d, w2l3_d, out_d, stop):
    with ExitStack() as ctx:
        def sb(name, shape):
            return ctx.enter_context(nc.sbuf_tensor(name, shape, F32))

        sems = {}

        def S(step):
            name = PLACE.get(step, (step, 0))[0]
            if name not in sems:
                sems[name] = nc.alloc_semaphore(name)
            return sems[name]

        def when(step, n):
            return S(step), PLACE.get(step, (step, 0))[1] + n

        X = sb("X", [P, COLS])
        A = sb("A", [P, COLS])
        T1 = sb("T1", [P, COLS])
        T2 = sb("T2", [P, COLS])
        T34 = sb("T34", [P, 2 * COLS])
        T3, T4 = T34[:, 0:COLS], T34[:, COLS:2 * COLS]
        big = sb("big", [P, 11264])
        KVS = sb("KVS", [P, HALF, 128])
        KSS = sb("KSS", [P, HALF, 128])
        up2 = sb("up2", [P, 2, E, FH])
        w2l2 = sb("w2l2", [FH, E, C])
        rows = sb("rows", [P, 2, 128])
        mats = sb("mats", [P, len(MATS), 128])
        vecs = sb("vecs", [P, len(VECS)])
        small = sb("small", [P, 1024])
        bank = [ctx.enter_context(nc.psum_tensor(f"bank{i}", [P, CHUNK], F32)) for i in range(NCH)]

        def mat(name):
            return mats[:, M[name], :]

        def vec(name, n=1):
            return vecs[:, V[name]:V[name] + n]

        def ch(t, c, p0=0, p1=P):
            return t[p0:p1, c * CHUNK:(c + 1) * CHUNK]

        VX = big[:, 0:PAIRS * HP * VW].rearrange("p (n w) -> p n w", w=VW)
        o = PAIRS * HP * VW
        BM = big[:, o:o + NWIN * 512].rearrange("p (w h k) -> p w h k", w=NWIN, h=HEADS)
        o += NWIN * 512
        wmask = big[:, o:o + NWIN * WT].rearrange("p (w k) -> p w k", w=NWIN)
        o += NWIN * WT
        cw1 = big[0:2, o:o + 128]
        PAD = big[:, 0:HALF * PH * PH].rearrange("p (b r c) -> p b r c", b=HALF, r=PH)
        o = HALF * PH * PH
        taps = big[:, o:o + KK * 128].rearrange("p (t n) -> p t n", t=KK)
        o += KK * 128
        wexp = big[0:33, o:o + KK * 128].rearrange("p (t n) -> p t n", t=KK)
        o += KK * 128
        stage = sb("stage", [P, 4608])
        QB = [stage[:, s * 128:(s + 1) * 128] for s in range(2)]
        OB = [stage[:, 256 + s * 128:256 + (s + 1) * 128] for s in range(2)]
        KX = [stage[:, 512 + s * 512:1024 + s * 512] for s in range(2)]
        SC = [stage[:, 1536 + s * 512:2048 + s * 512] for s in range(2)]
        PR = [stage[:, 2560 + s * 512:3072 + s * 512] for s in range(2)]
        PT = [stage[:, 3584 + s * 512:4096 + s * 512] for s in range(2)]
        PROD = [stage[:, s * 512:(s + 1) * 512] for s in range(4)]
        stats = small[:, 0:96].rearrange("p (b s) -> p b s", s=6)
        mv = small[:, 96:128].rearrange("p (b s) -> p b s", s=2)
        gst = small[:, 128:160]
        grp = small[:, 160:192]
        gvar = small[:, 192:208]
        gsq = small[:, 208:224]
        gsd = small[:, 224:240]
        grs = small[:, 240:256]
        qscale = small[:, 256:257]
        lsc = small[:, 257:258]
        rowmax = [small[:, 272 + 8 * s:280 + 8 * s] for s in range(2)]
        rden = [small[:, 288 + 8 * s:296 + 8 * s] for s in range(2)]
        rmask = [small[:, 304 + 16 * s:320 + 16 * s] for s in range(2)]
        ksum = small[:, 368:432]
        kinv = small[:, 432:496]
        knorm = small[:, 496:512]
        kln = small[:, 512:528]
        krs = small[:, 528:544]
        bqc = small[:, 544:545]
        xmean = small[:, 552:568]
        y2b = small[:, 568:584]
        gates2 = small[:, 600:856]
        bnv = small[:, 336:344]

        hmask = small[:, 352:360]
        ident2 = mats[:, M["stack"], 0:64]
        pmask = mats[:, M["stack"], 64:96]

        xw3 = T1[:, :].rearrange("p (b n) -> p b n", n=N)
        X3 = X[:, :].rearrange("p (b n) -> p b n", n=N)
        A3 = A[:, :].rearrange("p (b n) -> p b n", n=N)


        def gn_vector(dve, t, src, src_sem, src_val):
            for b in range(HALF):
                if b % 2 == 0:
                    dve.wait_ge(*when(src_sem, src_val(b // 2)))
                nc.vector.bn_stats(stats[:, b, :], src[:, b, :]).then_inc(S(t + "_stats"), 1)
            for b in range(HALF):
                dve.wait_ge(*when(t + "_stats", b + 1))
                nc.vector.bn_aggr(mv[:, b, :], stats[:, b, :]).then_inc(S(t + "_aggr"), 1)
            dve.wait_ge(*when(t + "_aggr", HALF))
            nc.vector.tensor_copy(gst[:, 0:16], mv[:, :, 0]).then_inc(S(t + "_gst"), 1)
            nc.vector.tensor_tensor(gsq, mv[:, :, 0], mv[:, :, 0], ALU.mult).then_inc(S(t + "_sq"), 1)
            dve.wait_ge(*when(t + "_sq", 1))
            nc.vector.tensor_tensor(gst[:, 16:32], gsq, mv[:, :, 1], ALU.add).then_inc(S(t + "_gst"), 1)
            dve.wait_ge(*when(t + "_grp", 1))
            nc.vector.tensor_copy(grp, bank[0][:, 0:32]).then_inc(S(t + "_grpc"), 1)
            dve.wait_ge(*when(t + "_grpc", 1))
            nc.vector.tensor_tensor(gsq, grp[:, 0:16], grp[:, 0:16], ALU.mult).then_inc(S(t + "_grpc"), 1)
            dve.wait_ge(*when(t + "_grpc", 2))
            nc.vector.tensor_tensor(gvar, grp[:, 16:32], gsq, ALU.subtract).then_inc(S(t + "_var"), 1)
            dve.wait_ge(*when(t + "_sd", 1))
            nc.vector.reciprocal(grs, gsd).then_inc(S(t + "_rs"), 1)
            dve.wait_ge(*when(t + "_rs", 1))
            for b in range(HALF):
                nc.vector.tensor_scalar(A3[:, b, :], src[:, b, :], grp[:, b:b + 1], grs[:, b:b + 1],
                                        ALU.subtract, ALU.mult).then_inc(S(t + "_norm"), 1)

        def gn_tensor(pe, t):
            pe.wait_ge(*when(t + "_gst", 2))
            nc.tensor.matmul(bank[0][:, 0:32], mat("pair"), gst, start=True, stop=True).then_inc(S(t + "_grp"), 1)

        def gn_scalar(act, t):
            act.wait_ge(*when(t + "_var", 1))
            nc.scalar.activation(gsd, gvar, ACT.Sqrt, bias=vec("eps5")).then_inc(S(t + "_sd"), 1)

        def ln_tensor(pe, t, src, ready, val, left=None):
            def var(c):
                pe.wait_ge(*when(t + "_sq", c + 1))
                if c >= 4:
                    pe.wait_ge(*when(t + "_ln", c - 3))
                else:
                    pe.wait_ge(*when(ready, left or val(4 + c)))
                nc.tensor.matmul(bank[4 + c % 4][:, :], mat("mean"), ch(T2, c), start=True, stop=True) \
                    .then_inc(S(t + "_var"), 1)

            for c in range(NCH):
                pe.wait_ge(*when(ready, val(c)))
                if c >= 4:
                    pe.wait_ge(*when(t, c - 3))
                nc.tensor.matmul(bank[c % 4][:, :], mat("centre"), ch(src, c), start=True, stop=True) \
                    .then_inc(S(t + "_cen"), 1)
                if c >= 2:
                    var(c - 2)
            var(NCH - 2)
            var(NCH - 1)

        def ln_scalar(act, t, eps):
            def rstd(c):
                act.wait_ge(*when(t + "_var", c + 1))
                nc.scalar.activation(ch(T2, c), bank[4 + c % 4][:, :], ACT.Ln, bias=vec(eps)).then_inc(S(t + "_ln"), 1)
                act.wait_ge(*when(t + "_ln", c + 1))
                nc.scalar.activation(ch(T2, c), ch(T2, c), ACT.Exp, scale=-0.5).then_inc(S(t + "_rstd"), 1)

            for c in range(NCH):
                act.wait_ge(*when(t + "_cen", c + 1))
                nc.scalar.activation(ch(T2, c), bank[c % 4][:, :], ACT.Square).then_inc(S(t + "_sq"), 1)
                if c >= 3:
                    rstd(c - 3)
            for c in range(NCH - 3, NCH):
                rstd(c)

        def ln_vector(dve, t, dst):
            for c in range(NCH):
                dve.wait_ge(*when(t + "_rstd", c + 1))
                nc.vector.tensor_tensor(ch(dst, c), bank[c % 4][:, :], ch(T2, c), ALU.mult).then_inc(S(t), 1)

        def rms_scalar(act, t, src, ready, eps):
            for c in range(NCH):
                act.wait_ge(*when(ready, c + 1))
                nc.scalar.activation(ch(T2, c), ch(src, c), ACT.Square).then_inc(S(t + "_sq"), 1)
            for c in range(NCH):
                act.wait_ge(*when(t + "_ms", c + 1))
                nc.scalar.activation(ch(T2, c), bank[c][:, :], ACT.Ln, bias=vec(eps)).then_inc(S(t + "_ln"), 1)
                act.wait_ge(*when(t + "_ln", c + 1))
                nc.scalar.activation(ch(T2, c), ch(T2, c), ACT.Exp, scale=-0.5).then_inc(S(t + "_rstd"), 1)

        def rms_tensor(pe, t):
            for c in range(NCH):
                pe.wait_ge(*when(t + "_sq", c + 1))
                nc.tensor.matmul(bank[c][:, :], mat("mean"), ch(T2, c), start=True, stop=True) \
                    .then_inc(S(t + "_ms"), 1)

        def steps(eng, f, last):
            for k in range(NWIN):
                f(k, k)
            with eng.Fori(1, HALF) as b:
                for w in range(NWIN):
                    f(b * NWIN + w, w)
            for k in range(PAIRS, PAIRS + last):
                f(k, k % NWIN)

        def at(k, lag):
            n = k - lag
            return n if not isinstance(k, int) or 0 <= n < PAIRS else None

        def reused(eng, name, n, per=1):
            if not isinstance(n, int) or n >= 2:
                eng.wait_ge(*when(name, (n - 1) * per))

        def steps2(eng, f, last):
            for k in range(2):
                f(k, k)
            with eng.Fori(1, HALF // 2) as b:
                for p in range(2):
                    f(b * 2 + p, p)
            for k in range(HALF, HALF + last):
                f(k, k % 2)

        def at2(k, lag):
            n = k - lag
            return n if not isinstance(k, int) or 0 <= n < HALF else None

        def finish(dve, ready):
            dve.wait_ge(*when(ready, NCH))
            for c in range(NCH):
                nc.vector.tensor_copy(ch(X, c), ch(X, c)).then_inc(S("final"), 1)

        route = sb("route", [HALF, 512])
        lg, lc, ld, wk, o1, o2 = (route[:, 16 * i:16 * i + 16] for i in range(6))
        lg3, wk3, o13, o23 = (v.rearrange("p (h e) -> p h e", e=E) for v in (lg, wk, o1, o2))
        s2a, s2b, s2f = route[:, 96:98], route[:, 98:100], route[:, 100:102]
        gdiag = route[:, 256:512]
        lg5, wk5, o15, o25 = (ch(T1, i).rearrange("p (n e) -> p n e", e=E) for i in range(4))
        s5a, s5b, s5f = (T1[:, 2048 + 64 * i:2112 + 64 * i] for i in range(3))
        gates5 = ch(T1, 0)
        up1w = big[:, 0:E * HB * NHB].rearrange("p (e n) -> p e n", e=E)
        up3w = big[:, E * HB * NHB:2 * E * HB * NHB].rearrange("p (e n) -> p e n", e=E)
        downw = T3[0:HB, 0:E * NHB * C].rearrange("p (e k n) -> p e k n", e=E, k=NHB)
        XM = [T4[:, CHUNK * i:CHUNK * i + CHUNK] for i in range(2)]
        GC = T4[:, 3072:3136]
        G5 = [T4[:, 1024 + CHUNK * i:1536 + CHUNK * i] for i in range(2)]
        Y5 = [T4[:, 2048 + CHUNK * i:2560 + CHUNK * i] for i in range(2)]
        S5 = [stage[0:HB, 512 * i:512 * i + 512] for i in range(2)]
        H5 = [stage[0:HB, 1024 + 512 * i:1536 + 512 * i] for i in range(2)]
        HID = [stage[:, 512 * i:512 * i + 512] for i in range(4)]
        W2G = [stage[:, 2048 + 1024 * i:3072 + 1024 * i] for i in range(2)]
        CAPACITY = float(-(-B * N * 5 // 4 // E))

        block = ctx.enter_context(nc.Block())

        @block.sync
        def _(sp):
            sp.dma_start(T1[:, :], xw_d).then_inc(S("loaded_xw"), 16)
            sp.dma_start(mats[:, :, :], mats_d).then_inc(S("loaded_mats"), 16)
            sp.dma_start(vecs[:, :], vecs_d).then_inc(S("loaded_vecs"), 16)
            sp.dma_start(T2[0:2, :], feats_d).then_inc(S("loaded_feats"), 16)
            sp.dma_start(cw1, cw1_d).then_inc(S("loaded_feats"), 16)
            sp.dma_start(wmask, wmask_d).then_inc(S("loaded_wmask"), 16)
            sp.dma_start(X[:, :], xi_d).then_inc(S("loaded_xi"), 16)
            sp.wait_ge(*when("l0_obd", PAIRS))
            sp.wait_ge(*when("l0_pv", PAIRS))
            sp.dma_start(taps, taps_d).then_inc(S("loaded_taps"), 16)
            sp.dma_start(wexp, wexp_d).then_inc(S("loaded_taps"), 16)
            sp.wait_ge(*when("loaded_taps", 32))
            sp.dma_start(up2[:, :, :, :], w1l2_d).then_inc(S("loaded_l2"), 16)
            sp.dma_start(w2l2[:, :, :], w2l2_d).then_inc(S("loaded_l2"), 16)
            sp.wait_ge(*when("loaded_l2", 32))
            if stop == 5:
                sp.wait_ge(*when("tap_summed", NCH * KK))
                sp.dma_start(up1w, w1l3_d).then_inc(S("loaded_l3"), 16)
                sp.dma_start(up3w, w3l3_d).then_inc(S("loaded_l3"), 16)
                sp.wait_ge(*when("z4", NCH))
                sp.wait_ge(*when("o4", NCH))
                sp.dma_start(downw, w2l3_d).then_inc(S("loaded_l3"), 16)
                sp.wait_ge(*when("loaded_l3", 48))
            for c in range(NCH):
                sp.wait_ge(*when("final", c + 1))
                sp.dma_start(ch(out_d, c), ch(X, c)).then_inc(S("stored"), 16)
            sp.wait_ge(*when("stored", 16 * NCH))

        @block.gpsimd
        def _(pool):
            nc.gpsimd.memset(big[:, 0:PAIRS * HP * VW], 0.0).then_inc(S("vx_zero"), 1)
            def stage_keys(k, w):
                n, s = at(k, 0), w % 2
                if n is None:
                    return
                pool.wait_ge(*when("q_norm", (NCH if not isinstance(n, int) else n // NWIN // 2 + 1)))
                pool.wait_ge(*when("k_norm", (NCH if not isinstance(n, int) else n // NWIN // 2 + 1)))
                reused(pool, "l0_scores", n)
                nc.gpsimd.tensor_tensor(QB[s].rearrange("p (h q) -> p h q", h=2),
                                        T1[:, bass.ds(n * WT, WT)].unsqueeze(1).broadcast_to([P, 2, WT]),
                                        vec("half0", 2).unsqueeze(2).broadcast_to([P, 2, WT]),
                                        ALU.mult).then_inc(S("l0_staged"), 1)
                nc.gpsimd.tensor_tensor(KX[s].rearrange("p (h k) -> p h k", h=HEADS),
                                        T2[:, bass.ds(n * WT, WT)].unsqueeze(1).broadcast_to([P, HEADS, WT]),
                                        hmask.unsqueeze(2).broadcast_to([P, HEADS, WT]),
                                        ALU.mult).then_inc(S("l0_staged"), 1)

            pool.wait_ge(*when("hmask", 1))
            steps(pool, stage_keys, 0)

            pool.wait_ge(*when("l0_pv", PAIRS))
            nc.gpsimd.memset(big[:, 0:HALF * PH * PH], 0.0).then_inc(S("pad_zero"), 1)

            if stop < 3:
                return
            pool.wait_ge(*when("gates2", 1))
            pool.wait_ge(*when("loaded_l2", 32))

            def gate_w2(k, p):
                b = at2(k, 0)
                if b is None:
                    return
                if not isinstance(b, int) or b >= 2:
                    pool.wait_ge(*when("down3", E * (b - 1)))
                for h in range(2):
                    nc.gpsimd.tensor_tensor(
                        W2G[p][:, 512 * h:512 * h + 512].rearrange("p (e c) -> p e c", e=E), w2l2[:, :, :],
                        gates2[:, bass.ds(b * 16 + 8 * h, E)].unsqueeze(2).broadcast_to([P, E, C]), ALU.mult) \
                        .then_inc(S("w2_gated"), 1)

            steps2(pool, gate_w2, 0)

        @block.vector
        def _(dve):
            dve.wait_ge(*when("loaded_mats", 16))
            dve.wait_ge(*when("loaded_vecs", 16))
            nc.vector.tensor_tensor(hmask, mats[:, M["head"], 0:64:8], mats[:, M["head"], 64:128:8],
                                    ALU.add).then_inc(S("hmask"), 1)
            nc.vector.tensor_scalar(lsc, vec("ls0"), float(np.log(np.float32(100.0))), None, ALU.min) \
                .then_inc(S("lsc"), 1)
            dve.wait_ge(*when("vx_zero", 1))
            for j in range(2):
                nc.vector.tensor_copy(VX[:, :, 32 + j], vec(f"par{j}").broadcast_to([P, PAIRS * HP])) \
                    .then_inc(S("vx_ones"), 1)
            gn_vector(dve, "g0", xw3, "loaded_xw", lambda c: 16)
            dve.wait_ge(*when("bias_exp", 1))
            bz = ch(T3, 1)
            nc.vector.tensor_scalar(bz, ch(T3, 0), 1.0, None, ALU.add).then_inc(S("bias_v"), 1)
            dve.wait_ge(*when("bias_v", 1))
            nc.vector.reciprocal(ch(T3, 2), bz).then_inc(S("bias_v"), 1)
            dve.wait_ge(*when("bias_v", 2))
            nc.vector.tensor_scalar(ch(T3, 3).rearrange("p (h k) -> p k h", h=HEADS),
                                    ch(T3, 2).rearrange("p (k h) -> p k h", h=HEADS), 16.0, None, ALU.mult) \
                .then_inc(S("bias_v"), 1)
            dve.wait_ge(*when("bias_v", 3))
            dve.wait_ge(*when("loaded_wmask", 16))
            for w in range(NWIN):
                nc.vector.tensor_tensor(BM[:, w, :, :], ch(T3, 3).rearrange("p (h k) -> p h k", h=HEADS),
                                        wmask[:, w, :].unsqueeze(1).broadcast_to([P, HEADS, WT]),
                                        ALU.add).then_inc(S("bm_ready"), 1)
            dve.wait_ge(*when("bm_ready", NWIN))
            for t, T in (("q", T1), ("k", T2)):
                for c in range(NCH):
                    dve.wait_ge(*when(t + "_proj", c + 1))
                    nc.vector.tensor_scalar(ch(T, c), bank[c][:, :], vec(f"b{t}0"), None, ALU.add) \
                        .then_inc(S(t + "_biased"), 1)
                for c in range(NCH):
                    dve.wait_ge(*when(t + "_ssq", c + 1))
                    nc.vector.tensor_scalar(ch(T3, c), bank[c][:, :], 1e-24, None, ALU.max) \
                        .then_inc(S(t + "_clip"), 1)
                for c in range(NCH):
                    dve.wait_ge(*when(t + "_len", c + 1))
                    nc.vector.reciprocal(ch(T3, c), ch(T3, c)).then_inc(S(t + "_rlen"), 1)
                if t == "q":
                    dve.wait_ge(*when("qscale", 1))
                for c in range(NCH):
                    dve.wait_ge(*when(t + "_rlen", c + 1))
                    nc.vector.scalar_tensor_tensor(ch(T, c), ch(T3, c), qscale if t == "q" else 1.0, ch(T, c),
                                                   ALU.mult, ALU.mult).then_inc(S(t + "_norm"), 1)
            dve.wait_ge(*when("vx_zero", 1))
            for g in range(PAIRS // 4):
                dve.wait_ge(*when("v_proj", g + 1))
                for x in range(2):
                    nc.vector.tensor_copy(
                        VX[64 * x:64 * x + 64, g * 16:g * 16 + 16, 0:32]
                        .rearrange("p n (h x d) -> p n h x d", h=2, x=2)[:, :, :, x, :],
                        bank[g % NCH][64 * x:64 * x + 64, 0:256].rearrange("p (n h d) -> p n h d", h=2, d=DH)) \
                        .then_inc(S("v_ready"), 1)

            def softmax_and_out(k, w):
                n, s = at(k, 0), w % 2
                if n is not None:
                    sc = SC[s].rearrange("p (h k) -> p h k", h=HEADS)
                    dve.wait_ge(*when("l0_scores", n + 1))
                    reused(dve, "l0_exp", n)
                    nc.vector.tensor_tensor(sc, bank[s][:, :].rearrange("p (h k) -> p h k", h=HEADS),
                                            BM[:, w, :, :], ALU.add).then_inc(S("l0_biased"), 1)
                    dve.wait_ge(*when("l0_biased", n + 1))
                    nc.vector.tensor_reduce(rowmax[s], sc, AX, ALU.max).then_inc(S("l0_max"), 1)
                    dve.wait_ge(*when("l0_max", n + 1))
                    nc.vector.tensor_tensor(sc, sc, rowmax[s].unsqueeze(2).broadcast_to([P, HEADS, WT]),
                                            ALU.subtract).then_inc(S("l0_shifted"), 1)
                n = at(k, 2)
                if n is not None:
                    ob = bank[4 + s][:, 0:HP * VW].rearrange("p (g v) -> p g v", v=VW)
                    dve.wait_ge(*when("l0_pv", n + 1))
                    nc.vector.reciprocal(rden[s].rearrange("p (g x) -> p g x", x=2), ob[:, :, 32:34]) \
                        .then_inc(S("l0_rden"), 1)
                    dve.wait_ge(*when("l0_rden", n + 1))
                    rd = rden[s].rearrange("p (g x) -> p g x", x=2)
                    for h in range(2):
                        nc.vector.tensor_scalar(rmask[s].rearrange("p (g h x) -> p g h x", h=2, x=2)[:, :, h, :],
                                                rd, vec(f"half{h}"), None, ALU.mult).then_inc(S("l0_rmask"), 1)
                    dve.wait_ge(*when("l0_rmask", (n + 1) * 2))
                    reused(dve, "l0_ot", n)
                    nc.vector.tensor_tensor(OB[s].rearrange("p (g y d) -> p g y d", g=HP, d=DH),
                                            ob[:, :, 0:32].rearrange("p g (y d) -> p g y d", d=DH),
                                            rmask[s].rearrange("p (g y) -> p g y", g=HP).unsqueeze(3)
                                            .broadcast_to([P, HP, 4, DH]), ALU.mult).then_inc(S("l0_obd"), 1)

            dve.wait_ge(*when("v_ready", PAIRS // 2))
            steps(dve, softmax_and_out, 2)
            for c in range(NCH):
                dve.wait_ge(*when("l0_wo", c + 1))
                nc.vector.tensor_scalar(ch(T4, c), bank[c][:, :], vec("bo0"), None, ALU.add) \
                    .then_inc(S("l0_res"), 1)
            dve.wait_ge(*when("l0_res", NCH))
            dve.wait_ge(*when("loaded_xi", 16))
            Xi = X[:, :].rearrange("p (b r c) -> p b r c", r=HH, c=WW)
            Tw = T4[:, :].rearrange("p (b w i j) -> p b w i j", w=NWIN, i=WS, j=WS)
            runs = [(0, 0, SS, WS), (1, 0, SS + WS, WS - SS), (1, WS - SS, 0, SS)]
            for wy, iy, r, nr in runs:
                for wx, ix, q, nq in runs:
                    xv = Xi[:, :, r:r + nr, q:q + nq]
                    nc.vector.tensor_tensor(xv, xv, Tw[:, :, 2 * wy + wx, iy:iy + nr, ix:ix + nq], ALU.add) \
                        .then_inc(S("x1_ready"), 1)
            if stop == 0:
                dve.wait_ge(*when("x1_ready", 9))
                for c in range(NCH):
                    nc.vector.tensor_copy(ch(X, c), ch(X, c)).then_inc(S("final"), 1)
                return

            gn_vector(dve, "g1", X3, "x1_ready", lambda c: 9)
            sc_, sh_ = bnv[:, 3:4], bnv[:, 5:6]
            dve.wait_ge(*when("bn_sd", 1))
            nc.vector.reciprocal(bnv[:, 2:3], bnv[:, 1:2]).then_inc(S("bn_v"), 1)
            nc.vector.tensor_tensor(bnv[:, 4:5], vec("br1"), vec("mu1"), ALU.subtract).then_inc(S("bn_v"), 1)
            dve.wait_ge(*when("bn_v", 2))
            nc.vector.tensor_tensor(sc_, bnv[:, 2:3], vec("ga1"), ALU.mult).then_inc(S("bn_v"), 1)
            dve.wait_ge(*when("bn_v", 3))
            nc.vector.scalar_tensor_tensor(sh_, bnv[:, 4:5], sc_, vec("be1"), ALU.mult, ALU.add) \
                .then_inc(S("bn_v"), 1)
            nc.vector.memset(T1[32:33, :], 1.0).then_inc(S("r_one"), 1)
            for c in range(NCH):
                dve.wait_ge(*when("xi_kept", min(c + 1, NCH)))
                for t in range(KK):
                    k, i, j = c * KK + t, t // 3, t % 3
                    dve.wait_ge(*when("tap_w", k + 1))
                    if k >= 4:
                        dve.wait_ge(*when("tap_summed", k - 3))
                    nc.vector.tensor_tensor(
                        PROD[k % 4].rearrange("p (b r c) -> p b r c", r=HH, c=WW),
                        bank[k % 4][:, :].rearrange("p (b r c) -> p b r c", r=HH, c=WW),
                        PAD[:, 2 * c:2 * c + 2, i:i + HH, j:j + WW], ALU.mult).then_inc(S("tap_prod"), 1)
                    if t == 3 and c:
                        dve.wait_ge(*when("tap_summed", c * KK))
                        nc.vector.tensor_tensor(ch(X, c - 1), ch(X, c - 1), bank[4 + (c - 1) % 2][:, :], ALU.add) \
                            .then_inc(S("x2_ready"), 1)
            dve.wait_ge(*when("tap_summed", NCH * KK))
            nc.vector.tensor_tensor(ch(X, NCH - 1), ch(X, NCH - 1), bank[4 + (NCH - 1) % 2][:, :], ALU.add) \
                .then_inc(S("x2_ready"), 1)
            if stop == 1:
                finish(dve, "x2_ready")
                return

            ln_vector(dve, "a2", A)
            for i in range(2):
                dve.wait_ge(*when("w2_centred", i + 1))
                nc.vector.tensor_copy(mat(("wq2t", "wk2t")[i]), bank[i][:, 0:128]).then_inc(S("w2_kept"), 1)
            for i in range(2):
                dve.wait_ge(*when("w2_centred", i + 3))
                nc.vector.tensor_copy(rows[:, i, :], bank[2 + i][:, 0:128]).then_inc(S("w2_kept"), 1)
            dve.wait_ge(*when("w2_centred", 5))
            nc.vector.tensor_copy(bqc, bank[4][:, 0:1]).then_inc(S("w2_kept"), 1)
            dve.wait_ge(*when("w2_kept", 5))
            for c in range(NCH):
                dve.wait_ge(*when("k2_proj", c + 1))
                nc.vector.tensor_tensor(ch(T1, c).rearrange("p (j n) -> p j n", n=128),
                                        bank[c][:, :].rearrange("p (j n) -> p j n", n=128),
                                        rows[:, 0, :].unsqueeze(1).broadcast_to([P, 4, 128]), ALU.add) \
                    .then_inc(S("k2_biased"), 1)
            for c in range(NCH):
                dve.wait_ge(*when("v2_proj", c + 1))
                nc.vector.tensor_tensor(ch(T3, c).rearrange("p (j n) -> p j n", n=128),
                                        bank[c][:, :].rearrange("p (j n) -> p j n", n=128),
                                        rows[:, 1, :].unsqueeze(1).broadcast_to([P, 4, 128]), ALU.add) \
                    .then_inc(S("v2_kept"), 1)
            for c in range(NCH):
                dve.wait_ge(*when("k2_sq", c + 1))
                nc.vector.tensor_reduce(ksum[:, 8 * c:8 * c + 8], ch(T1, c).rearrange("p (j n) -> p j n", n=64),
                                        AX, ALU.add).then_inc(S("k2_sum"), 1)
            dve.wait_ge(*when("k2_sum", NCH))
            nc.vector.tensor_scalar(ksum, ksum, 1e-7, None, ALU.add).then_inc(S("k2_sum"), 1)
            dve.wait_ge(*when("k2_sum", NCH + 1))
            nc.vector.reciprocal(kinv, ksum).then_inc(S("k2_inv"), 1)
            dve.wait_ge(*when("k2_inv", 1))
            for c in range(NCH):
                k = ch(T1, c).rearrange("p (j n) -> p j n", n=64)
                nc.vector.tensor_tensor(k, k, kinv[:, 8 * c:8 * c + 8].unsqueeze(2).broadcast_to([P, 8, 64]),
                                        ALU.mult).then_inc(S("k2_ready"), 1)
            dve.wait_ge(*when("k2_norm", 1))
            nc.vector.tensor_scalar(knorm, bank[4][:, 0:HALF], 1e-24, 2.0 ** 40, ALU.max, ALU.mult) \
                .then_inc(S("k2_clip"), 1)
            dve.wait_ge(*when("k2_rs", 1))
            for b in range(HALF):
                dve.wait_ge(*when("kv2", 4 * (b // 4 + 1)))
                nc.vector.scalar_tensor_tensor(KVS[:, b, :], bank[b // 4][:, (b % 4) * 128:(b % 4 + 1) * 128],
                                               krs[:, b:b + 1], mat("sum"), ALU.mult, ALU.mult) \
                    .then_inc(S("kv2_kept"), 1)
            for c in range(NCH):
                dve.wait_ge(*when("q2_guard", c + 1))
                dve.wait_ge(*when("q2_s2", c + 1))
                nc.vector.scalar_tensor_tensor(ch(T1, c), bank[4 + c % 4][:, :], 2.0 ** 40, ch(T1, c),
                                               ALU.mult, ALU.max).then_inc(S("q2_clip"), 1)
                if c >= 2:
                    dve.wait_ge(*when("q2_rs", c - 1))
                    nc.vector.tensor_tensor(ch(T2, c - 2), ch(T2, c - 2), ch(T1, c - 2), ALU.mult) \
                        .then_inc(S("q2_ready"), 1)
            for c in range(NCH - 2, NCH):
                dve.wait_ge(*when("q2_rs", c + 1))
                nc.vector.tensor_tensor(ch(T2, c), ch(T2, c), ch(T1, c), ALU.mult).then_inc(S("q2_ready"), 1)
            for c in range(NCH):
                dve.wait_ge(*when("o2_proj", c + 1))
                nc.vector.scalar_tensor_tensor(ch(X, c), bank[c][:, :], vec("bo2"), ch(X, c), ALU.add, ALU.add) \
                    .then_inc(S("x3_ready"), 1)
            if stop == 2:
                finish(dve, "x3_ready")
                return

            ln_vector(dve, "a3", A)
            for c in range(NCH):
                dve.wait_ge(*when("a3", c + 1))
                nc.vector.tensor_reduce(xmean[:, 2 * c:2 * c + 2], ch(A, c).rearrange("p (b n) -> p b n", n=N),
                                        AX, ALU.add).then_inc(S("r3_mean"), 1)
            links = [0]

            def link(instruction):
                links[0] += 1
                instruction.then_inc(S("link"), 1)
                dve.wait_ge(*when("link", links[0]))

            def top2(p, n, probs, work, one1, one2, max1, max2, first):
                def spread(v):
                    return v.unsqueeze(2).broadcast_to([p, n, E])
                rank = vec("rank0", E)[0:p, :].unsqueeze(1).broadcast_to([p, n, E])
                for one, best, src in ((one1, max1, probs), (one2, max2, work)):
                    link(nc.vector.tensor_reduce(best, src, AX, ALU.max))
                    link(nc.vector.tensor_tensor(one, src, spread(best), ALU.is_ge))
                    link(nc.vector.tensor_tensor(one, one, rank, ALU.mult))
                    link(nc.vector.tensor_reduce(first, one, AX, ALU.max))
                    link(nc.vector.tensor_tensor(one, rank, spread(first), ALU.is_equal))
                    if one is one1:
                        link(nc.vector.scalar_tensor_tensor(work, one, -4.0, probs, ALU.mult, ALU.add))

            def softmax_vector(p, n, z, m, t):
                link(nc.vector.tensor_reduce(m, z, AX, ALU.max))
                nc.vector.tensor_tensor(z, z, m.unsqueeze(2).broadcast_to([p, n, E]), ALU.subtract) \
                    .then_inc(S(t + "_in"), 1)
                dve.wait_ge(*when(t + "_exp", 1))
                link(nc.vector.tensor_reduce(m, z, AX, ALU.add))
                link(nc.vector.reciprocal(m, m))
                link(nc.vector.tensor_tensor(z, z, m.unsqueeze(2).broadcast_to([p, n, E]), ALU.mult))

            dve.wait_ge(*when("r3_logits", 1))
            link(nc.vector.scalar_tensor_tensor(lg, bank[0][0:HALF, 0:16], 1.0 / N,
                                                vecs[0:HALF, V["brr0"]:V["brr0"] + 16], ALU.mult, ALU.add))
            softmax_vector(HALF, 2, lg3, s2a, "sm1")
            nc.vector.tensor_copy(lc, lg).then_inc(S("r3_rw"), 1)
            dve.wait_ge(*when("r3_load", 1))
            link(nc.vector.tensor_copy(ld, bank[1][0:HALF, 0:16]))
            link(nc.vector.tensor_tensor(ld[:, 0:8], ld[:, 0:8], ld[:, 8:16], ALU.add))
            link(nc.vector.reciprocal(ld[:, 8:16], ld[:, 0:8]))
            link(nc.vector.tensor_scalar(ld[:, 8:16], ld[:, 8:16], CAPACITY / N, 1.0, ALU.mult, ALU.min))
            link(nc.vector.tensor_tensor(lg3, lg3, ld[:, 8:16].unsqueeze(1).broadcast_to([HALF, 2, E]), ALU.mult))
            softmax_vector(HALF, 2, lg3, s2a, "sm2")
            top2(HALF, 2, lg3, wk3, o13, o23, s2a, s2b, s2f)
            nc.vector.tensor_tensor(s2b, s2b, s2a, ALU.subtract).then_inc(S("sm3_in"), 1)
            dve.wait_ge(*when("sm3_exp", 1))
            link(nc.vector.tensor_scalar(s2a, s2b, 1.0, None, ALU.add))
            link(nc.vector.reciprocal(s2a, s2a))
            link(nc.vector.tensor_tensor(s2b, s2a, s2b, ALU.mult))
            link(nc.vector.tensor_tensor(o13, o13, s2a.unsqueeze(2).broadcast_to([HALF, 2, E]), ALU.mult))
            link(nc.vector.tensor_tensor(o23, o23, s2b.unsqueeze(2).broadcast_to([HALF, 2, E]), ALU.mult))
            link(nc.vector.tensor_tensor(o13, o13, o23, ALU.add))
            nc.vector.tensor_tensor(gdiag.rearrange("p (b g) -> p b g", g=16),
                                    mats[0:HALF, M["ident"], 0:HALF].unsqueeze(2).broadcast_to([HALF, HALF, 16]),
                                    o1.unsqueeze(1).broadcast_to([HALF, HALF, 16]), ALU.mult) \
                .then_inc(S("r3_diag"), 1)
            dve.wait_ge(*when("r3_gates", 1))
            nc.vector.tensor_copy(gates2, bank[2][:, 0:256]).then_inc(S("gates2"), 1)
            dve.wait_ge(*when("gates2", 1))
            g4 = gates2.rearrange("p (b h e) -> p b h e", h=2, e=E)
            tb = ch(T4, 0)[:, 0:128].rearrange("p (b e) -> p b e", e=E)
            for h in range(2):
                q = slice(64 * h, 64 * h + 64)
                nc.vector.tensor_tensor(tb[q], g4[q, :, h, :],
                                        vec("b2_0", E)[q, :].unsqueeze(1).broadcast_to([64, HALF, E]), ALU.mult) \
                    .then_inc(S("b2_prod"), 1)
            dve.wait_ge(*when("b2_prod", 2))
            link(nc.vector.tensor_reduce(y2b, tb, AX, ALU.add))

            def mix2(k, p):
                b = at2(k, 1)
                if b is not None:
                    dve.wait_ge(*when("down3", E * (b + 1)))
                    nc.vector.scalar_tensor_tensor(T1[:, bass.ds(b * N, N)], bank[4 + (p + 1) % 2][:, 0:N],
                                                   y2b[:, bass.ds(b, 1)], A[:, bass.ds(b * N, N)], ALU.add, ALU.add) \
                        .then_inc(S("y3_kept"), 1)

            steps2(dve, mix2, 1)
            ln_vector(dve, "l3", T3)
            for c in range(NCH):
                dve.wait_ge(*when("l3", c + 1))
                nc.vector.scalar_tensor_tensor(ch(X, c), ch(T3, c), vec("ga3"), ch(X, c), ALU.mult, ALU.add) \
                    .then_inc(S("x4_part"), 1)
            for c in range(NCH):
                dve.wait_ge(*when("x4_part", c + 1))
                nc.vector.tensor_scalar(ch(X, c), ch(X, c), vec("be3"), None, ALU.add).then_inc(S("x4_ready"), 1)
            if stop == 3:
                finish(dve, "x4_ready")
                return

            ln_vector(dve, "a4", A)
            for c in range(NCH):
                dve.wait_ge(*when("n4_rstd", c + 1))
                nc.vector.scalar_tensor_tensor(ch(T1, c), ch(T2, c), vec("n14"), ch(A, c), ALU.mult, ALU.mult) \
                    .then_inc(S("n4"), 1)
            for t, T in (("k", T3), ("q", T2)):
                for c in range(NCH):
                    dve.wait_ge(*when(t + "4_proj", c + 1))
                    nc.vector.tensor_scalar(ch(T, c), bank[c][:, :], 0.0, None, ALU.min).then_inc(S(t + "4_neg"), 1)
                    if c >= 2:
                        dve.wait_ge(*when(t + "4_exp", c - 1))
                        nc.vector.scalar_tensor_tensor(ch(T, c - 2), bank[c - 2][:, :], 0.0, ch(T, c - 2),
                                                       ALU.max, ALU.add).then_inc(S(t + "4_elu"), 1)
                for c in range(NCH - 2, NCH):
                    dve.wait_ge(*when(t + "4_exp", c + 1))
                    nc.vector.scalar_tensor_tensor(ch(T, c), bank[c][:, :], 0.0, ch(T, c),
                                                   ALU.max, ALU.add).then_inc(S(t + "4_elu"), 1)
                if t == "k":
                    for c in range(NCH):
                        dve.wait_ge(*when("v4_proj", c + 1))
                        nc.vector.tensor_copy(ch(T4, c), bank[c][:, :]).then_inc(S("v4_kept"), 1)
                    for c in range(4):
                        dve.wait_ge(*when("kv4", 4 * (c + 1)))
                        nc.vector.tensor_tensor(KVS[:, 4 * c:4 * c + 4, :],
                                                bank[c][:, :].rearrange("p (b n) -> p b n", n=128),
                                                mat("head").unsqueeze(1).broadcast_to([P, 4, 128]), ALU.mult) \
                            .then_inc(S("kv4_kept"), 1)
                    dve.wait_ge(*when("ks4", 1))
                    nc.vector.tensor_copy(krs, bank[4][:, 0:HALF]).then_inc(S("ks4_kept"), 1)
                    dve.wait_ge(*when("ks4_kept", 1))
                    for c in range(4):
                        nc.vector.tensor_tensor(KSS[:, 4 * c:4 * c + 4, :],
                                                krs[:, 4 * c:4 * c + 4].unsqueeze(2).broadcast_to([P, 4, 128]),
                                                mat("head").unsqueeze(1).broadcast_to([P, 4, 128]), ALU.mult) \
                            .then_inc(S("kv4_kept"), 1)
            for c in range(NCH):
                dve.wait_ge(*when("z4", c + 1))
                dve.wait_ge(*when("num4", c + 1))
                nc.vector.tensor_tensor(ch(T1, c), bank[4 + c % 4][:, :], ch(T3, c), ALU.mult).then_inc(S("o4"), 1)
            for c in range(NCH):
                dve.wait_ge(*when("o4_proj", c + 1))
                nc.vector.scalar_tensor_tensor(ch(T4, c), bank[c][:, :], vec("bo4"), ch(A, c), ALU.add, ALU.add) \
                    .then_inc(S("h4"), 1)
            for c in range(NCH):
                dve.wait_ge(*when("h4", c + 1))
                nc.vector.tensor_tensor(ch(X, c), ch(X, c), ch(T4, c), ALU.add).then_inc(S("x5_part"), 1)
            for c in range(NCH):
                dve.wait_ge(*when("m4_rstd", c + 1))
                nc.vector.scalar_tensor_tensor(ch(T4, c), ch(T4, c), vec("n24"), ch(T2, c), ALU.mult, ALU.mult) \
                    .then_inc(S("m4"), 1)
            for c in range(NCH):
                dve.wait_ge(*when("m4", c + 1))
                nc.vector.tensor_tensor(ch(X, c), ch(X, c), ch(T4, c), ALU.add).then_inc(S("x5_ready"), 1)
            if stop == 4:
                finish(dve, "x5_ready")
                return

            ln_vector(dve, "a5", A)
            dve.wait_ge(*when("r5_logits", 1))
            link(nc.vector.tensor_copy(gates5, bank[0][:, :]))
            softmax_vector(P, 2 * TILES, lg5, s5a, "sm4")
            top2(P, 2 * TILES, lg5, wk5, o15, o25, s5a, s5b, s5f)
            link(nc.vector.tensor_tensor(s5f, s5a, s5b, ALU.add))
            link(nc.vector.tensor_scalar(s5f, s5f, 1e-9, None, ALU.add))
            link(nc.vector.reciprocal(s5f, s5f))
            link(nc.vector.tensor_tensor(o15, o15, o25, ALU.add))
            link(nc.vector.tensor_tensor(lg5, lg5, o15, ALU.mult))
            nc.vector.tensor_tensor(lg5, lg5, s5f.unsqueeze(2).broadcast_to([P, 2 * TILES, E]), ALU.mult) \
                .then_inc(S("gates5"), 1)

            def weigh5(u, e, h, c):
                s, q = e % 2, slice(64 * h, 64 * h + 64)
                dve.wait_ge(*when("down5", (u + 1) * NHB))
                dve.wait_ge(*when("g5_kept", u + 1))
                nc.vector.tensor_tensor(Y5[s][q, :], bank[6 + s][q, :], G5[s][q, :], ALU.mult) \
                    .then_inc(S("y5"), 1)
                dve.wait_ge(*when("y5", u + 1))
                if not isinstance(u, int) or u:
                    dve.wait_ge(*when("y5_added", u))
                xv = X[q, bass.ds(c * CHUNK, CHUNK)]
                nc.vector.tensor_tensor(xv, xv, Y5[s][q, :], ALU.add).then_inc(S("y5_added"), 1)

            def chunk5_vector(c):
                for h in range(2):
                    if not isinstance(c, int) or c:
                        dve.wait_ge(*when("up5", (2 * c + h - 1) * E * NHB))
                    nc.vector.tensor_tensor(XM[h], A[:, bass.ds(c * CHUNK, CHUNK)],
                                            vec(f"half{h}").broadcast_to([P, CHUNK]), ALU.mult) \
                        .then_inc(S("x5_masked"), 1)
                if not isinstance(c, int) or c:
                    dve.wait_ge(*when("g5_rows", 2 * c * E))
                nc.vector.tensor_copy(GC, gates5[:, bass.ds(c * 64, 64)]).then_inc(S("g5_chunk"), 1)
                for h in range(2):
                    for e in range(E):
                        u = (2 * c + h) * E + e
                        for k in range(NHB):
                            n, s = u * NHB + k, k % 2
                            dve.wait_ge(*when("silu5", n + 1))
                            if not isinstance(n, int) or n >= 2:
                                dve.wait_ge(*when("down5", n - 1))
                            nc.vector.tensor_tensor(H5[s], bank[2 + s][0:HB, :], S5[s], ALU.mult) \
                                .then_inc(S("hid5"), 1)
                        if e:
                            weigh5(u - 1, e - 1, h, c)
                        elif h:
                            weigh5(u - 1, E - 1, 0, c)
                weigh5((2 * c + 1) * E + E - 1, E - 1, 1, c)

            dve.wait_ge(*when("gates5", 1))
            chunk5_vector(0)
            with dve.Fori(1, NCH) as c:
                chunk5_vector(c)
            dve.wait_ge(*when("y5_added", NCH * 2 * E))
            for c in range(NCH):
                nc.vector.tensor_copy(ch(X, c), ch(X, c)).then_inc(S("final"), 1)

        @block.scalar
        def _(act):
            act.wait_ge(*when("loaded_vecs", 16))
            for c in range(2 * NCH):
                act.wait_ge(*when("bias_hid", c + 1))
                nc.scalar.activation(ch(T34, c), bank[c % NCH][:, :], ACT.Relu, bias=vec("cb1")) \
                    .then_inc(S("bias_relu"), 1)
            act.wait_ge(*when("bias_z", 1))
            nc.scalar.activation(ch(T3, 0), bank[0][:, :], ACT.Exp, scale=-1.0).then_inc(S("bias_exp"), 1)
            act.wait_ge(*when("lsc", 1))
            nc.scalar.activation(qscale, lsc, ACT.Exp).then_inc(S("qscale"), 1)
            gn_scalar(act, "g0")
            for t, T in (("q", T1), ("k", T2)):
                for c in range(NCH):
                    act.wait_ge(*when(t + "_biased", c + 1))
                    if t == "k":
                        act.wait_ge(*when("q_norm", c + 1))
                    nc.scalar.activation(ch(T3, c), ch(T, c), ACT.Square).then_inc(S(t + "_sq"), 1)
                for c in range(NCH):
                    act.wait_ge(*when(t + "_clip", c + 1))
                    nc.scalar.activation(ch(T3, c), ch(T3, c), ACT.Sqrt).then_inc(S(t + "_len"), 1)

            def exp_and_copies(k, w):
                n, s = at(k, 0), w % 2
                if n is not None:
                    act.wait_ge(*when("l0_shifted", n + 1))
                    reused(act, "l0_turned", n)
                    nc.scalar.activation(PR[s], SC[s], ACT.Exp).then_inc(S("l0_exp"), 1)
                n, s = at(k, 1), (w + 1) % 2
                if n is not None:
                    act.wait_ge(*when("l0_turned", n + 1))
                    reused(act, "l0_pv", n)
                    nc.scalar.activation(PT[s], bank[2 + s][:, :], ACT.Copy).then_inc(S("l0_pt"), 1)
                n = at(k, 3)
                if n is not None:
                    act.wait_ge(*when("l0_ot", n + 1))
                    nc.scalar.activation(T3[:, bass.ds(n * WT, WT)], bank[6 + s][:, 0:WT], ACT.Identity,
                                         bias=vec("bv0")).then_inc(S("l0_o"), 1)

            act.wait_ge(*when("k_norm", NCH))
            steps(act, exp_and_copies, 3)
            if stop == 0:
                return
            gn_scalar(act, "g1")
            nc.scalar.activation(bnv[:, 1:2], vec("va1"), ACT.Sqrt, bias=vec("eps3")).then_inc(S("bn_sd"), 1)
            act.wait_ge(*when("bn_v", 4))
            for c in range(NCH):
                act.wait_ge(*when("r_proj", c + 1))
                nc.scalar.activation(ch(T1, c, 0, 32), bank[c][0:32, :], ACT.Relu, bias=bnv[0:32, 5:6],
                                     scale=bnv[0:32, 3:4]).then_inc(S("r_ready"), 1)
            act.wait_ge(*when("pad_zero", 1))
            for c in range(NCH):
                act.wait_ge(*when("xi_proj", c + 1))
                nc.scalar.activation(PAD[:, 2 * c:2 * c + 2, 1:1 + HH, 1:1 + WW],
                                     bank[c][:, :].rearrange("p (b r c) -> p b r c", r=HH, c=WW),
                                     ACT.Identity, bias=vec("bi1")).then_inc(S("xi_kept"), 1)
            if stop == 1:
                return
            ln_scalar(act, "a2", "eps5")
            for c in range(NCH):
                act.wait_ge(*when("k2_biased", c + 1))
                nc.scalar.activation(ch(T1, c), ch(T1, c), ACT.Square).then_inc(S("k2_sq"), 1)
            for c in range(NCH):
                act.wait_ge(*when("k2_ready", c + 1))
                nc.scalar.activation(ch(T2, c), ch(T1, c), ACT.Square).then_inc(S("k2_fourth"), 1)
            act.wait_ge(*when("k2_clip", 1))
            nc.scalar.activation(kln, knorm, ACT.Ln).then_inc(S("k2_ln"), 1)
            act.wait_ge(*when("k2_ln", 1))
            nc.scalar.activation(krs, kln, ACT.Exp, scale=-0.5, bias=vec("ln16")).then_inc(S("k2_rs"), 1)
            act.wait_ge(*when("kv2", HALF))
            act.wait_ge(*when("k2_norm", 1))
            act.wait_ge(*when("w2_kept", 5))

            def q_rs(c):
                act.wait_ge(*when("q2_clip", c + 1))
                nc.scalar.activation(ch(T1, c), ch(T1, c), ACT.Ln, bias=vec("tiny")).then_inc(S("q2_ln"), 1)
                act.wait_ge(*when("q2_ln", c + 1))
                nc.scalar.activation(ch(T1, c), ch(T1, c), ACT.Exp, scale=-0.5, bias=vec("ln20")) \
                    .then_inc(S("q2_rs"), 1)

            for c in range(NCH):
                act.wait_ge(*when("q2_proj", c + 1))
                nc.scalar.activation(ch(T2, c), bank[c % 4][:, :], ACT.Square, bias=bqc).then_inc(S("q2_sq"), 1)
                act.wait_ge(*when("q2_sq", c + 1))
                nc.scalar.activation(ch(T4, c), ch(T2, c), ACT.Square).then_inc(S("q2_fourth"), 1)
                act.wait_ge(*when("q2_s1", c + 1))
                nc.scalar.activation(ch(T1, c), bank[c % 4][:, :], ACT.Square, scale=1e-12 * 2.0 ** 20,
                                     bias=vec("guard")).then_inc(S("q2_guard"), 1)
                if c >= 1:
                    q_rs(c - 1)
            q_rs(NCH - 1)
            for c in range(NCH):
                act.wait_ge(*when("t2", c + 1))
                nc.scalar.activation(ch(T1, c), bank[c][:, :], ACT.Identity, bias=vec("bv2")) \
                    .then_inc(S("t2_kept"), 1)
            if stop == 2:
                return
            ln_scalar(act, "a3", "eps5")
            for t in ("sm1", "sm2"):
                act.wait_ge(*when(t + "_in", 1))
                nc.scalar.activation(lg, lg, ACT.Exp).then_inc(S(t + "_exp"), 1)
            act.wait_ge(*when("sm3_in", 1))
            nc.scalar.activation(s2b, s2b, ACT.Exp).then_inc(S("sm3_exp"), 1)

            def gelu(k, p):
                b = at2(k, 0)
                if b is None:
                    return
                for e in range(E):
                    u = b * E + e
                    act.wait_ge(*when("up3", u + 1))
                    if not isinstance(u, int) or u >= 4:
                        act.wait_ge(*when("down3", u - 3))
                    nc.scalar.activation(HID[e % 4], bank[e % 4][:, :], ACT.Gelu, bias=vec(f"b1_{e}")) \
                        .then_inc(S("hid3"), 1)

            steps2(act, gelu, 0)
            ln_scalar(act, "l3", "eps5")
            if stop == 3:
                return
            ln_scalar(act, "a4", "eps5")
            rms_scalar(act, "n4", A, "a4", "eps6")
            for t, T in (("k", T3), ("q", T2)):
                for c in range(NCH):
                    act.wait_ge(*when(t + "4_neg", c + 1))
                    nc.scalar.activation(ch(T, c), ch(T, c), ACT.Exp).then_inc(S(t + "4_exp"), 1)
            for c in range(NCH):
                act.wait_ge(*when("den4", c + 1))
                nc.scalar.activation(ch(T3, c), bank[c % 4][:, :], ACT.Ln, bias=vec("eps6")).then_inc(S("z4_ln"), 1)
                act.wait_ge(*when("z4_ln", c + 1))
                nc.scalar.activation(ch(T3, c), ch(T3, c), ACT.Exp, scale=-1.0).then_inc(S("z4"), 1)
            rms_scalar(act, "m4", T4, "h4", "eps6")
            if stop == 4:
                return
            ln_scalar(act, "a5", "eps5")
            act.wait_ge(*when("sm4_in", 1))
            nc.scalar.activation(gates5, gates5, ACT.Exp).then_inc(S("sm4_exp"), 1)

            def chunk5_scalar(c):
                for h in range(2):
                    for e in range(E):
                        u = (2 * c + h) * E + e
                        act.wait_ge(*when("g5_rows", u + 1))
                        if not isinstance(u, int) or u >= 2:
                            act.wait_ge(*when("y5", u - 1))
                        nc.scalar.activation(G5[e % 2], bank[4 + e % 2][:, :], ACT.Copy).then_inc(S("g5_kept"), 1)
                        for k in range(NHB):
                            n, s = u * NHB + k, k % 2
                            act.wait_ge(*when("up5", n + 1))
                            if not isinstance(n, int) or n >= 2:
                                act.wait_ge(*when("hid5", n - 1))
                            nc.scalar.activation(S5[s], bank[s][0:HB, :], ACT.Silu).then_inc(S("silu5"), 1)

            chunk5_scalar(0)
            with act.Fori(1, NCH) as c:
                chunk5_scalar(c)

        @block.tensor
        def _(pe):
            pe.wait_ge(*when("loaded_mats", 16))
            pe.wait_ge(*when("loaded_vecs", 16))
            pe.wait_ge(*when("loaded_feats", 32))
            for c in range(2 * NCH):
                if c >= NCH:
                    pe.wait_ge(*when("bias_relu", c - NCH + 1))
                keys = T2[0:2, c * 4 * WT:(c + 1) * 4 * WT].rearrange("p (k q) -> p k q", k=4)
                nc.tensor.matmul(bank[c % NCH][:, :], cw1, keys.unsqueeze(2).broadcast_to([2, 4, 2, WT]),
                                 start=True, stop=True).then_inc(S("bias_hid"), 1)
            pe.wait_ge(*when("bias_relu", 2 * NCH))
            for key in range(WT):
                mm = nc.tensor.matmul(bank[0][:, key * HEADS:(key + 1) * HEADS],
                                      T34[:, key * 128:(key + 1) * 128],
                                      vec("w2c0", HEADS), start=True, stop=True)
            mm.then_inc(S("bias_z"), 1)
            pe.wait_ge(*when("bias_exp", 1))
            gn_tensor(pe, "g0")
            for t in ("q", "k"):
                for c in range(NCH):
                    if t == "q":
                        pe.wait_ge(*when("g0_norm", 2 * (c + 1)))
                        if c == 0:
                            pe.wait_ge(*when("g0_grpc", 1))
                    else:
                        pe.wait_ge(*when("q_clip", c + 1))
                    nc.tensor.matmul(bank[c][:, :], mat(f"w{t}0"), ch(A, c), start=True, stop=True) \
                        .then_inc(S(t + "_proj"), 1)
                for c in range(NCH):
                    pe.wait_ge(*when(t + "_sq", c + 1))
                    nc.tensor.matmul(bank[c][:, :], mat("head"), ch(T3, c), start=True, stop=True) \
                        .then_inc(S(t + "_ssq"), 1)
            for g in range(PAIRS // 4):
                if g < NCH:
                    pe.wait_ge(*when("k_clip", g + 1))
                else:
                    pe.wait_ge(*when("v_ready", 2 * (g - NCH + 1)))
                for i in range(4):
                    n = 4 * g + i
                    for x in range(2):
                        mm = nc.tensor.matmul(
                            bank[g % NCH][64 * x:64 * x + 64, i * 64:(i + 1) * 64], A[:, n * WT:(n + 1) * WT],
                            mat("wv0").rearrange("p (g x d) -> p g x d", x=2, d=DH)[:, :, x, :],
                            start=True, stop=True)
                mm.then_inc(S("v_proj"), 1)

            def attention(k, w):
                n, s = at(k, 0), w % 2
                if n is not None:
                    pe.wait_ge(*when("l0_staged", (n + 1) * 2))
                    reused(pe, "l0_biased", n)
                    nc.tensor.matmul(bank[s][:, :], QB[s], KX[s], start=True, stop=True).then_inc(S("l0_scores"), 1)
                n, s = at(k, 1), (w + 1) % 2
                if n is not None:
                    pe.wait_ge(*when("l0_exp", n + 1))
                    reused(pe, "l0_pt", n)
                    for g in range(HP):
                        mm = nc.tensor.transpose(bank[2 + s][:, g * 128:(g + 1) * 128],
                                                 PR[s][:, g * 128:(g + 1) * 128], mat("ident"))
                    mm.then_inc(S("l0_turned"), 1)
                n, s = at(k, 2), w % 2
                if n is not None:
                    pe.wait_ge(*when("l0_pt", n + 1))
                    reused(pe, "l0_obd", n)
                    for g in range(HP):
                        mm = nc.tensor.matmul(bank[4 + s][:, g * VW:(g + 1) * VW], PT[s][:, g * 128:(g + 1) * 128],
                                              VX[:, bass.ds(n * HP + g, 1), :].rearrange("p a v -> p (a v)"),
                                              start=True, stop=True)
                    mm.then_inc(S("l0_pv"), 1)
                n, s = at(k, 3), (w + 1) % 2
                if n is not None:
                    pe.wait_ge(*when("l0_obd", n + 1))
                    reused(pe, "l0_o", n)
                    nc.tensor.matmul(bank[6 + s][:, 0:WT], OB[s], ident2, start=True, stop=True) \
                        .then_inc(S("l0_ot"), 1)

            pe.wait_ge(*when("v_ready", PAIRS // 2))
            pe.wait_ge(*when("vx_ones", 2))
            steps(pe, attention, 3)
            for c in range(NCH):
                pe.wait_ge(*when("l0_o", PAIRS))
                nc.tensor.matmul(bank[c][:, :], mat("wo0"), ch(T3, c), start=True, stop=True) \
                    .then_inc(S("l0_wo"), 1)
            if stop == 0:
                return
            gn_tensor(pe, "g1")
            for c in range(NCH):
                pe.wait_ge(*when("g1_norm", 2 * (c + 1)))
                nc.tensor.matmul(bank[c][0:32, :], mat("wr1")[:, 0:32], ch(A, c), start=True, stop=True) \
                    .then_inc(S("r_proj"), 1)
            for c in range(NCH):
                pe.wait_ge(*when("r_ready", c + 1))
                nc.tensor.matmul(bank[c][:, :], mat("wi1"), ch(A, c), start=True, stop=True) \
                    .then_inc(S("xi_proj"), 1)
            pe.wait_ge(*when("xi_kept", NCH))
            pe.wait_ge(*when("loaded_taps", 32))
            pe.wait_ge(*when("r_one", 1))

            def tap_sum(k):
                c, t = k // KK, k % KK
                pe.wait_ge(*when("tap_prod", k + 1))
                if t == 0 and c >= 2:
                    pe.wait_ge(*when("x2_ready", c - 1))
                nc.tensor.matmul(bank[4 + c % 2][:, :], taps[:, t, :], PROD[k % 4], start=(t == 0),
                                 stop=(t == KK - 1)).then_inc(S("tap_summed"), 1)

            for k in range(NCH * KK):
                if k >= 4:
                    pe.wait_ge(*when("tap_prod", k - 3))
                nc.tensor.matmul(bank[k % 4][:, :], wexp[:, k % KK, :], ch(T1, k // KK, 0, 33),
                                 start=True, stop=True).then_inc(S("tap_w"), 1)
                if k >= 2:
                    tap_sum(k - 2)
            tap_sum(NCH * KK - 2)
            tap_sum(NCH * KK - 1)
            if stop == 1:
                return
            ln_tensor(pe, "a2", X, "x2_ready", lambda c: c + 1, left=NCH)
            pe.wait_ge(*when("a2", NCH))
            for i, (left, right) in enumerate(((mat("wq2t"), mat("centre")), (mat("wk2t"), mat("centre")),
                                               (vec("bk2").broadcast_to([P, 128]), mat("centre")),
                                               (vec("bv2").broadcast_to([P, 128]), mat("ident")))):
                nc.tensor.matmul(bank[i][:, 0:128], left, right, start=True, stop=True).then_inc(S("w2_centred"), 1)
            nc.tensor.matmul(bank[4][:, 0:1], mat("centre"), vec("bq2"), start=True, stop=True) \
                .then_inc(S("w2_centred"), 1)
            pe.wait_ge(*when("w2_kept", 5))
            for c in range(NCH):
                for j in range(4):
                    mm = nc.tensor.matmul(bank[c][:, j * 128:(j + 1) * 128],
                                          A[:, (4 * c + j) * 128:(4 * c + j + 1) * 128], mat("wk2t"),
                                          start=True, stop=True)
                mm.then_inc(S("k2_proj"), 1)
            for c in range(NCH):
                pe.wait_ge(*when("k2_biased", c + 1))
                for j in range(4):
                    mm = nc.tensor.matmul(bank[c][:, j * 128:(j + 1) * 128],
                                          A[:, (4 * c + j) * 128:(4 * c + j + 1) * 128], mat("wv2"),
                                          start=True, stop=True)
                mm.then_inc(S("v2_proj"), 1)
            pe.wait_ge(*when("v2_kept", NCH))
            for b in range(HALF):
                pe.wait_ge(*when("k2_fourth", b // 2 + 1))
                for j in range(2):
                    mm = nc.tensor.matmul(bank[4][:, b:b + 1], T2[:, (2 * b + j) * 128:(2 * b + j + 1) * 128],
                                          vec("one"), start=(j == 0), stop=(j == 1))
            mm.then_inc(S("k2_norm"), 1)
            for b in range(HALF):
                pe.wait_ge(*when("k2_ready", b // 2 + 1))
                for j in range(2):
                    tile = slice((2 * b + j) * 128, (2 * b + j + 1) * 128)
                    mm = nc.tensor.matmul(bank[b // 4][:, (b % 4) * 128:(b % 4 + 1) * 128], T1[:, tile], T3[:, tile],
                                          start=(j == 0), stop=(j == 1))
                mm.then_inc(S("kv2"), 1)

            def q_sums(c):
                pe.wait_ge(*when("q2_sq", c + 1))
                nc.tensor.matmul(bank[c % 4][:, :], mat("sum"), ch(T2, c), start=True, stop=True) \
                    .then_inc(S("q2_s1"), 1)
                pe.wait_ge(*when("q2_fourth", c + 1))
                if c >= 4:
                    pe.wait_ge(*when("q2_clip", c - 3))
                nc.tensor.matmul(bank[4 + c % 4][:, :], mat("sum"), ch(T4, c), start=True, stop=True) \
                    .then_inc(S("q2_s2"), 1)

            pe.wait_ge(*when("kv2_kept", HALF))
            pe.wait_ge(*when("k2_clip", 1))
            for c in range(NCH):
                if c >= 4:
                    pe.wait_ge(*when("q2_guard", c - 3))
                nc.tensor.matmul(bank[c % 4][:, :], mat("wq2t"), ch(A, c), start=True, stop=True) \
                    .then_inc(S("q2_proj"), 1)
                if c >= 1:
                    q_sums(c - 1)
            q_sums(NCH - 1)
            pe.wait_ge(*when("q2_clip", NCH))
            for c in range(NCH):
                pe.wait_ge(*when("q2_ready", c + 1))
                for i in range(2):
                    b = 2 * c + i
                    nc.tensor.matmul(bank[c][:, i * N:(i + 1) * N], mat("wv2"), A[:, b * N:(b + 1) * N],
                                     start=True, stop=False)
                    mm = nc.tensor.matmul(bank[c][:, i * N:(i + 1) * N], KVS[:, b, :], T2[:, b * N:(b + 1) * N],
                                          start=False, stop=True)
                mm.then_inc(S("t2"), 1)
            for c in range(NCH):
                pe.wait_ge(*when("t2_kept", c + 1))
                nc.tensor.matmul(bank[c][:, :], mat("wo2"), ch(T1, c), start=True, stop=True) \
                    .then_inc(S("o2_proj"), 1)
            if stop == 2:
                return
            ln_tensor(pe, "a3", X, "x3_ready", lambda c: c + 1)
            pe.wait_ge(*when("r3_mean", NCH))
            pe.wait_ge(*when("a3", NCH))
            nc.tensor.matmul(bank[0][0:HALF, 0:16], xmean, mat("rt3")[:, 0:16], start=True, stop=True) \
                .then_inc(S("r3_logits"), 1)
            pe.wait_ge(*when("r3_rw", 1))
            nc.tensor.matmul(bank[1][0:HALF, 0:16], vec("one")[0:HALF, :].broadcast_to([HALF, HALF]), lc,
                             start=True, stop=True).then_inc(S("r3_load"), 1)
            pe.wait_ge(*when("r3_diag", 1))
            nc.tensor.matmul(bank[2][:, 0:256], vec("one")[0:HALF, :].broadcast_to([HALF, 128]), gdiag,
                             start=True, stop=True).then_inc(S("r3_gates"), 1)
            pe.wait_ge(*when("gates2", 1))
            pe.wait_ge(*when("loaded_l2", 32))

            def down3(u, e, p):
                pe.wait_ge(*when("hid3", u + 1))
                for h in range(2):
                    mm = nc.tensor.matmul(bank[4 + p][64 * h:64 * h + 64, 0:N],
                                          W2G[p][:, 512 * h + C * e:512 * h + C * e + C],
                                          HID[e % 4][:, N * h:N * h + N], start=(e == 0), stop=(e == E - 1),
                                          skip_group_check=True)
                mm.then_inc(S("down3"), 1)

            def experts(k, p):
                b, done = at2(k, 0), at2(k, 1)
                for e in range(E):
                    if b is not None:
                        u = b * E + e
                        if not isinstance(u, int) or u >= 4:
                            pe.wait_ge(*when("hid3", u - 3))
                        for h in range(2):
                            mm = nc.tensor.matmul(bank[e % 4][:, N * h:N * h + N], up2[:, h, e, :],
                                                  A[:, bass.ds(b * N, N)], start=True, stop=True)
                        mm.then_inc(S("up3"), 1)
                    if e < 2:
                        if done is not None:
                            down3(done * E + e + E - 2, e + E - 2, (p + 1) % 2)
                    elif b is not None:
                        if e == 2:
                            pe.wait_ge(*when("w2_gated", 2 * (b + 1)))
                            if not isinstance(b, int) or b >= 2:
                                pe.wait_ge(*when("y3_kept", b - 1))
                        down3(b * E + e - 2, e - 2, p)

            steps2(pe, experts, 1)
            ln_tensor(pe, "l3", T1, "y3_kept", lambda c: 2 * (c + 1), left=HALF)
            if stop == 3:
                return
            ln_tensor(pe, "a4", X, "x4_ready", lambda c: c + 1)
            pe.wait_ge(*when("a4", NCH))
            rms_tensor(pe, "n4")
            for c in range(NCH):
                pe.wait_ge(*when("n4", c + 1))
                for j in range(4):
                    mm = nc.tensor.matmul(bank[c][:, j * 128:(j + 1) * 128],
                                          T1[:, (4 * c + j) * 128:(4 * c + j + 1) * 128], mat("wk4"),
                                          start=True, stop=True)
                mm.then_inc(S("k4_proj"), 1)
            for c in range(NCH):
                pe.wait_ge(*when("k4_elu", c + 1))
                for j in range(4):
                    mm = nc.tensor.matmul(bank[c][:, j * 128:(j + 1) * 128],
                                          T1[:, (4 * c + j) * 128:(4 * c + j + 1) * 128], mat("wv4"),
                                          start=True, stop=True)
                mm.then_inc(S("v4_proj"), 1)
            pe.wait_ge(*when("v4_kept", NCH))
            for b in range(HALF):
                for j in range(2):
                    tile = slice((2 * b + j) * 128, (2 * b + j + 1) * 128)
                    mm = nc.tensor.matmul(bank[b // 4][:, (b % 4) * 128:(b % 4 + 1) * 128], T3[:, tile], T4[:, tile],
                                          start=(j == 0), stop=(j == 1))
                mm.then_inc(S("kv4"), 1)
            for b in range(HALF):
                for j in range(2):
                    mm = nc.tensor.matmul(bank[4][:, b:b + 1], T3[:, (2 * b + j) * 128:(2 * b + j + 1) * 128],
                                          vec("one"), start=(j == 0), stop=(j == 1))
            mm.then_inc(S("ks4"), 1)
            pe.wait_ge(*when("kv4_kept", 4))
            pe.wait_ge(*when("ks4_kept", 1))
            for c in range(NCH):
                nc.tensor.matmul(bank[c][:, :], mat("wq4"), ch(T1, c), start=True, stop=True) \
                    .then_inc(S("q4_proj"), 1)
            pe.wait_ge(*when("kv4_kept", 8))
            pe.wait_ge(*when("q4_elu", NCH))
            for c in range(NCH):
                if c >= 4:
                    pe.wait_ge(*when("z4", c - 3))
                    pe.wait_ge(*when("o4", c - 3))
                for t, W, k in (("den4", KSS, 0), ("num4", KVS, 4)):
                    for i in range(2):
                        b = 2 * c + i
                        mm = nc.tensor.matmul(bank[k + c % 4][:, i * N:(i + 1) * N], W[:, b, :],
                                              T2[:, b * N:(b + 1) * N], start=True, stop=True)
                    mm.then_inc(S(t), 1)
            pe.wait_ge(*when("o4", NCH))
            for c in range(NCH):
                nc.tensor.matmul(bank[c][:, :], mat("wo4"), ch(T1, c), start=True, stop=True) \
                    .then_inc(S("o4_proj"), 1)
            rms_tensor(pe, "m4")
            if stop == 4:
                return
            ln_tensor(pe, "a5", X, "x5_ready", lambda c: c + 1)
            pe.wait_ge(*when("a5", NCH))
            for j in range(TILES):
                mm = nc.tensor.matmul(bank[0][:, 16 * j:16 * j + 16], A[:, j * 128:(j + 1) * 128],
                                      mat("rt5")[:, 0:16], start=True, stop=True)
            mm.then_inc(S("r5_logits"), 1)
            pe.wait_ge(*when("gates5", 1))
            pe.wait_ge(*when("loaded_l3", 48))

            def down5(n, h, e, k):
                pe.wait_ge(*when("hid5", n + 1))
                nc.tensor.matmul(bank[6 + e % 2][64 * h:64 * h + 64, :], downw[:, e, k, :], H5[k % 2],
                                 start=(k == 0), stop=(k == NHB - 1)).then_inc(S("down5"), 1)

            def chunk5_tensor(c):
                pe.wait_ge(*when("g5_chunk", c + 1))
                for h in range(2):
                    pe.wait_ge(*when("x5_masked", 2 * c + h + 1))
                    for e in range(E):
                        u = (2 * c + h) * E + e
                        if not isinstance(u, int) or u >= 2:
                            pe.wait_ge(*when("g5_kept", u - 1))
                        for j in range(4):
                            mm = nc.tensor.matmul(
                                bank[4 + e % 2][:, j * 128:(j + 1) * 128],
                                GC[:, j * 16 + h * E + e:j * 16 + h * E + e + 1].broadcast_to([P, 128]),
                                mat("ident"), start=True, stop=True)
                        mm.then_inc(S("g5_rows"), 1)
                        for k in range(NHB):
                            n = u * NHB + k
                            if not isinstance(n, int) or n >= 2:
                                pe.wait_ge(*when("hid5", n - 1))
                            nc.tensor.matmul(bank[k % 2][0:HB, :], up1w[:, e, k * HB:(k + 1) * HB], XM[h],
                                             start=True, stop=True)
                            nc.tensor.matmul(bank[2 + k % 2][0:HB, :], up3w[:, e, k * HB:(k + 1) * HB], XM[h],
                                             start=True, stop=True).then_inc(S("up5"), 1)
                            if k == 1 and (not isinstance(u, int) or u >= 2):
                                pe.wait_ge(*when("y5", u - 1))
                            if k:
                                down5(n - 1, h, e, k - 1)
                            elif e:
                                down5(n - 1, h, e - 1, NHB - 1)
                            elif h:
                                down5(n - 1, 0, E - 1, NHB - 1)
                down5(n, 1, E - 1, NHB - 1)

            chunk5_tensor(0)
            with pe.Fori(1, NCH) as c:
                chunk5_tensor(c)


def blocks(w):
    a, b = w.shape
    m = np.zeros((128, 128), np.float32)
    m[:a, :b] = w
    m[64:64 + a, b:2 * b] = w
    return m


def constants():
    eye = np.eye(128, dtype=np.float32)
    same = np.kron(np.eye(2), np.ones((64, 64))).astype(np.float32)
    pair = np.kron(np.eye(64), np.ones((2, 2))).astype(np.float32) / 2
    head = np.kron(np.eye(16), np.ones((8, 8))).astype(np.float32)
    stack = np.zeros((128, 128), np.float32)
    stack[:, 0:64] = np.concatenate([np.eye(64)] * 2, 0)
    par = (np.arange(32) // 8) % 2
    stack[:64, 64:96] = par == 0
    stack[64:, 64:96] = par == 1
    mats = {"ident": eye, "mean": same / 64, "centre": eye - same / 64, "pair": pair, "head": head,
            "sum": same, "stack": stack}
    ws = WS
    r = np.arange(-(ws - 1), ws, dtype=np.float32)
    tbl = np.stack(np.meshgrid(r, r, indexing="ij"), axis=-1)
    tbl = tbl / (ws - 1) * 8.0
    tbl = np.sign(tbl) * np.log2(np.abs(tbl) + 1.0) / np.log2(8.0)
    tbl = tbl.reshape(-1, 2).astype(np.float32)
    c = np.stack(np.meshgrid(np.arange(ws), np.arange(ws), indexing="ij")).reshape(2, -1)
    rel = c[:, :, None] - c[:, None, :] + (ws - 1)
    idx = rel[0] * (2 * ws - 1) + rel[1]
    feats = np.ascontiguousarray(tbl[idx.T].reshape(-1, 2).T)
    img = np.zeros((HH, WW), np.int32)
    cnt = 0
    for hs in (slice(0, -ws), slice(-ws, -SS), slice(-SS, None)):
        for wsl in (slice(0, -ws), slice(-ws, -SS), slice(-SS, None)):
            img[hs, wsl] = cnt
            cnt += 1
    mw = img.reshape(HH // ws, ws, WW // ws, ws).transpose(0, 2, 1, 3).reshape(-1, ws * ws)
    mask = np.where(mw[:, None, :] != mw[:, :, None], -100.0, 0.0).astype(np.float32)
    wmask = np.ascontiguousarray(np.concatenate([mask.transpose(1, 0, 2)] * 2, 0))
    taps = np.zeros((128, KK, 128), np.float32)
    m = np.arange(KK * C)
    for h in range(2):
        taps[64 * h + m % C, m // C, 64 * h + m // KK] = 1
    widx = (m // KK // 4) * KK + m % KK
    return mats, feats, wmask, taps, widx


def halves(x):
    return np.ascontiguousarray(x.reshape(2, HALF, N, C).transpose(0, 3, 1, 2).reshape(P, COLS))


_INS = ["xw", "xi", "mats", "vecs", "feats", "cw1", "wmask", "taps", "wexp", "w1l2", "w2l2", "w1l3", "w3l3", "w2l3"]
OUTPUT_NAMES = [("out_0", (P, COLS))]


def kernel(x, **w):
    import concourse.bacc as _bacc
    from concourse.bass_utils import run_bass_kernel_spmd as _run

    w = {k: np.asarray(v) for k, v in w.items()}
    x = np.asarray(x)
    mats, feats, wmask, taps, widx = constants()
    rolled = np.roll(x, (-SS, -SS), axis=(1, 2)).reshape(B, 2, WS, 2, WS, C).transpose(0, 1, 3, 2, 4, 5)
    arr = {"xw": halves(rolled.reshape(B, N, C)), "xi": halves(x.reshape(B, N, C))}
    hp, par, d = np.meshgrid(np.arange(HP), np.arange(2), np.arange(DH), indexing="ij")
    chan = (hp * 16 + par * 8 + d).ravel()
    wv0 = np.zeros((128, 128), np.float32)
    wo0 = np.zeros((128, 128), np.float32)
    bv0 = np.zeros(128, np.float32)
    for h in range(2):
        col = (hp * 32 + h * 16 + par * 8 + d).ravel()
        wv0[64 * h:64 * h + 64, col] = w["L0_conv_Wv"].T[:, chan]
        wo0[col, 64 * h:64 * h + 64] = w["L0_conv_Wo"].T[chan, :]
        bv0[col] = w["L0_conv_bv"][chan]
    qkv2, qkv4 = w["L2_attn_W_qkv"], w["L3_attn_w_qkv"]
    mats |= {"wq0": blocks(w["L0_conv_Wq"].T), "wk0": blocks(w["L0_conv_Wk"].T), "wv0": wv0, "wo0": wo0,
             "wi1": blocks(w["L1_conv_Wi"]), "wr1": blocks(w["L1_conv_Wr"]),
             "wq2t": blocks(qkv2[:, 0:64].T), "wk2t": blocks(qkv2[:, 64:128].T), "wv2": blocks(qkv2[:, 128:192]),
             "wo2": blocks(w["L2_attn_W_out"]), "wq4": blocks(qkv4[:, 0:64]), "wk4": blocks(qkv4[:, 64:128]),
             "wv4": blocks(qkv4[:, 128:192]), "wo4": blocks(w["L3_attn_w_out"]),
             "rt3": blocks(w["L2_ffn_Wr"]), "rt5": blocks(w["L3_ffn_router_w"].T)}
    arr["mats"] = np.ascontiguousarray(np.stack([mats[n] for n in MATS], 1))
    two = lambda v: np.concatenate([v, v])
    padded = lambda v: np.concatenate([v, v, np.zeros(96, np.float32)])
    vecs = {"bq0": two(w["L0_conv_bq"]), "bk0": two(w["L0_conv_bk"]), "bv0": bv0, "bo0": two(w["L0_conv_bo"]),
            "ls0": two(np.repeat(w["L0_conv_logit_scale"].reshape(-1), DH)), "bi1": two(w["L1_conv_bi"]),
            "br1": padded(w["L1_conv_br"]), "ga1": padded(w["L1_conv_gamma"]), "be1": padded(w["L1_conv_beta"]),
            "mu1": padded(w["L1_conv_mean"]), "va1": padded(w["L1_conv_var"]),
            "bq2": two(w["L2_attn_b_qkv"][0:64]), "bk2": two(w["L2_attn_b_qkv"][64:128]),
            "bv2": two(w["L2_attn_b_qkv"][128:192]), "bo2": two(w["L2_attn_b_out"]),
            "ga3": two(w["L2_ffn_gamma"]), "be3": two(w["L2_ffn_beta"]), "n14": two(w["L3_attn_w_norm1"]),
            "bo4": two(w["L3_attn_b_out"]), "n24": two(w["L3_attn_w_norm2"]), "cb1": w["L0_conv_cpb_b1"],
            "eps6": np.full(128, 1e-6), "eps5": np.full(128, 1e-5), "eps3": np.full(128, 1e-3),
            "tiny": np.full(128, 2.0 ** -60), "ln20": np.full(128, 20 * np.log(2)),
            "ln16": np.full(128, 20 * np.log(2) - np.log(16)), "guard": np.full(128, 1e-19 * 2.0 ** 20),
            "one": np.ones(128), "par0": np.arange(128) < 64, "par1": np.arange(128) >= 64,
            "half0": np.arange(128) < 64, "half1": np.arange(128) >= 64}
    for e in range(E):
        vecs[f"w2c{e}"] = w["L0_conv_cpb_w2"][e]
        vecs[f"b1_{e}"] = w["L2_ffn_b1"][e]
        vecs[f"b2_{e}"] = two(w["L2_ffn_b2"][e])
        vecs[f"rank{e}"] = np.full(128, E - e)
        for h in range(2):
            vecs[f"brr{h * E + e}"] = np.broadcast_to(w["L2_ffn_br"][e], (128,))
    arr["vecs"] = np.ascontiguousarray(np.stack([np.asarray(vecs[n], np.float32) for n in VECS], 1))
    arr["feats"], arr["wmask"], arr["taps"] = feats, wmask, taps
    arr["cw1"] = np.ascontiguousarray(w["L0_conv_cpb_w1"].T)
    wexp = np.zeros((33, KK, 128), np.float32)
    for h in range(2):
        for t in range(KK):
            wexp[16 * h:16 * h + 16, t, 64 * h:64 * h + 64] = w["L1_conv_Ws"][:, widx[64 * t:64 * t + 64]]
            wexp[32, t, 64 * h:64 * h + 64] = w["L1_conv_bs"][widx[64 * t:64 * t + 64]]
    arr["wexp"] = wexp
    up2 = np.zeros((128, 2, E, FH), np.float32)
    for h in range(2):
        up2[64 * h:64 * h + 64, h] = w["L2_ffn_W1"].transpose(1, 0, 2)
    arr["w1l2"] = up2
    arr["w2l2"] = np.ascontiguousarray(w["L2_ffn_W2"].transpose(1, 0, 2))
    hid = HB * NHB
    for name, key in (("w1l3", "L3_ffn_w1"), ("w3l3", "L3_ffn_w3")):
        up = np.zeros((128, E, hid), np.float32)
        for h in range(2):
            up[64 * h:64 * h + 64, :, :w[key].shape[1]] = w[key].transpose(2, 0, 1)
        arr[name] = up
    down = np.zeros((E, hid, C), np.float32)
    down[:, :w["L3_ffn_w2"].shape[2]] = w["L3_ffn_w2"].transpose(0, 2, 1)
    arr["w2l3"] = np.ascontiguousarray(down.reshape(E, NHB, HB, C).transpose(2, 0, 1, 3))

    nc = _bacc.Bacc("TRN2", target_bir_lowering=False, num_devices=1)
    args, arrays = [], {}
    for name in _INS:
        a = arr[name]
        arrays[f"in_{name}"] = a
        args.append(nc.dram_tensor(f"in_{name}", a.shape, F32, kind="ExternalInput").ap())
    args.append(nc.dram_tensor("out_0", (P, COLS), F32, kind="ExternalOutput").ap())
    network(nc, *args, STOP_AFTER)
    r = _run(nc, [arrays], core_ids=[0])
    y = np.asarray(r.results[0]["out_0"])
    return y.reshape(2, C, HALF, HH, WW).transpose(0, 2, 3, 4, 1).reshape(B, HH, WW, C)
```

```python
import concourse.bass as bass
from concourse import mybir
from contextlib import ExitStack
import numpy as np

F32, F16 = mybir.dt.float32, mybir.dt.float16
I32, U32 = mybir.dt.int32, mybir.dt.uint32
ALU = mybir.AluOpType
ACT = mybir.ActivationFunctionType
AX = mybir.AxisListType.X

STOP_AFTER = 5

B, HH, WW, C = 32, 16, 16, 64
HALF = B // 2
N = HH * WW
P = 2 * C
COLS = HALF * N
CHUNK = 512
NCH = COLS // CHUNK
WS, SS, HEADS, DH = 8, 4, 8, 8
WT = WS * WS
NWIN = N // WT
PAIRS = COLS // WT
HP = HEADS // 2
VW = 34
RR, KK, PH = 16, 9, HH + 2
E, FH = 8, 128
HB, NHB = 114, 6
TILES = COLS // 128
HID3 = HB * NHB
SLOTS = 256
NT = (2 * COLS + E * (SLOTS - 1)) // SLOTS

MATS = ["ident", "mean", "centre", "pair", "head", "sum", "stack",
        "wq0", "wk0", "wv0", "wo0", "wi1", "wr1", "wq2t", "wk2t", "wv2", "wo2",
        "wq4", "wk4", "wv4", "wo4", "rt3", "rt5", "before", "iota"]
VECS = (["bq0", "bk0", "bv0", "bo0", "ls0", "bi1", "br1", "ga1", "be1", "mu1", "va1",
         "bq2", "bk2", "bv2", "bo2", "ga3", "be3", "n14", "bo4", "n24", "cb1",
         "eps6", "eps5", "eps3", "tiny", "ln10", "ln20", "ln16", "guard", "one", "par0", "par1", "half0", "half1"]
        + [f"w2c{h}" for h in range(HEADS)] + [f"b1_{e}" for e in range(E)]
        + [f"b2_{e}" for e in range(E)] + [f"brr{k}" for k in range(2 * E)]
        + [f"rank{e}" for e in range(E)])
M = {n: i for i, n in enumerate(MATS)}
V = {n: i for i, n in enumerate(VECS)}

STEPS = {
    "pe_projected": [("q_proj", 8), ("k_proj", 8), ("v_proj", 16), ("l0_wo", 8), ("r_proj", 8), ("xi_proj", 8),
                     ("w2_centred", 5), ("k2_proj", 8), ("v2_proj", 8), ("q2_proj", 8), ("t2", 8), ("o2_proj", 8),
                     ("k4_proj", 8), ("v4_proj", 8), ("q4_proj", 8), ("o4_proj", 8)],
    "pe_summed": [("bias_hid", 16), ("bias_z", 1), ("g0_grp", 1), ("q_ssq", 8), ("k_ssq", 8), ("g1_grp", 1),
                  ("k2_norm", 1), ("kv2", 16), ("q2_s1", 8), ("r3_logits", 1), ("r3_load", 1), ("r3_gates", 1),
                  ("kv4", 16), ("ks4", 1), ("num4", 8)],
    "pe_mean": [("q2_s2", 8), ("n4_ms", 8), ("den4", 8), ("m4_ms", 8)],
    "ln_centred": [("a2_cen", 8), ("a3_cen", 8), ("l3_cen", 8), ("a4_cen", 8), ("a5_cen", 8)],
    "ln_variance": [("a2_var", 8), ("a3_var", 8), ("l3_var", 8), ("a4_var", 8), ("a5_var", 8)],
    "act_first": [("bias_relu", 16), ("q_sq", 8), ("k_sq", 8), ("r_ready", 8), ("xi_kept", 8), ("a2_sq", 8),
                  ("k2_sq", 8), ("k2_fourth", 8), ("k2_ln", 1), ("k2_rs", 1), ("q2_sq", 8), ("t2_kept", 8),
                  ("a3_sq", 8), ("l3_sq", 8), ("a4_sq", 8), ("n4_sq", 8), ("k4_exp", 8), ("q4_exp", 8),
                  ("z4_ln", 8), ("m4_sq", 8), ("a5_sq", 8)],
    "act_second": [("bias_exp", 1), ("qscale", 1), ("g0_sd", 1), ("q_len", 8), ("k_len", 8), ("g1_sd", 1),
                   ("bn_sd", 1), ("a2_ln", 8), ("q2_ln", 8), ("a3_ln", 8), ("sm1_exp", 1), ("sm2_exp", 1),
                   ("sm3_exp", 1), ("l3_ln", 8), ("a4_ln", 8), ("n4_ln", 8), ("z4", 8), ("m4_ln", 8), ("a5_ln", 8)],
    "act_rstd": [("a2_rstd", 8), ("q2_rs", 8), ("a3_rstd", 8), ("l3_rstd", 8), ("a4_rstd", 8), ("n4_rstd", 8),
                 ("m4_rstd", 8), ("a5_rstd", 8)],
    "l0_vector": [("hmask", 1), ("lsc", 1), ("vx_ones", 2), ("g0_stats", 16), ("g0_aggr", 16)],
    "l0_norms": [("bias_v", 3), ("bm_ready", 4), ("q_biased", 8), ("q_clip", 8), ("q_norm", 8),
                 ("k_biased", 8), ("k_clip", 8), ("k_norm", 8), ("v_ready", 32)],
    "l1_vector": [("l0_res", 8), ("x1_ready", 9), ("g1_stats", 16), ("g1_aggr", 16)],
    "l2_vector": [("a2", 8), ("w2_kept", 5), ("k2_biased", 8), ("v2_kept", 8), ("k2_sum", 9), ("k2_inv", 1),
                  ("k2_ready", 8), ("k2_clip", 1), ("kv2_kept", 16), ("q2_clip", 8), ("x3_ready", 8),
                  ("a3", 8), ("r3_mean", 8), ("sm1_in", 1), ("r3_rw", 1), ("sm2_in", 1), ("sm3_in", 1),
                  ("r3_diag", 1), ("gates2", 1), ("b2_prod", 2), ("y3_kept", 16), ("l3", 8), ("x4_part", 8),
                  ("x4_ready", 8)],
    "l3_vector": [("a4", 8), ("n4", 8), ("k4_neg", 8), ("v4_kept", 8), ("q4_neg", 8),
                  ("o4", 8), ("h4", 8), ("x5_part", 8), ("m4", 8), ("x5_ready", 8), ("a5", 8)],
    "vector_second": [("q2_ready", 8), ("k4_elu", 8), ("kv4_kept", 8), ("q4_elu", 8)],
}
PLACE = {}
for _group, _steps in STEPS.items():
    _base = 0
    for _step, _n in _steps:
        PLACE[_step] = _group, _base
        _base += _n


def network(nc, xw_d, xi_d, mats_d, vecs_d, feats_d, cw1_d, wmask_d, taps_d, wexp_d,
            w1l2_d, w2l2_d, w1l3_d, w3l3_d, w2l3_d, out_d, slots_d, results_d, stop):
    with ExitStack() as ctx:
        def sb(name, shape):
            return ctx.enter_context(nc.sbuf_tensor(name, shape, F32))

        sems = {}

        def S(step):
            name = PLACE.get(step, (step, 0))[0]
            if name not in sems:
                sems[name] = nc.alloc_semaphore(name)
            return sems[name]

        def when(step, n):
            return S(step), PLACE.get(step, (step, 0))[1] + n

        X = sb("X", [P, COLS])
        A = sb("A", [P, COLS])
        T1 = sb("T1", [P, COLS])
        T2 = sb("T2", [P, COLS])
        T34 = sb("T34", [P, 2 * COLS])
        T3, T4 = T34[:, 0:COLS], T34[:, COLS:2 * COLS]
        big = sb("big", [P, 11264])
        KVS = sb("KVS", [P, HALF, 128])
        KSS = sb("KSS", [P, HALF, 128])
        l2w = sb("l2w", [P, 2 * E * FH + 2 * E * C])
        up2 = l2w[:, 0:2 * E * FH].rearrange("p (h e n) -> p h e n", h=2, e=E)
        w2l2 = l2w[:, 2 * E * FH:2 * E * FH + E * C].rearrange("p (e c) -> p e c", e=E)
        index = ctx.enter_context(nc.sbuf_tensor("index", [P, 2, 2 * TILES], U32))
        ident16 = ctx.enter_context(nc.sbuf_tensor("ident16", [P, 128], F16))
        expert = ctx.enter_context(nc.sbuf_tensor("expert", [1, 2, NT], I32))
        rows = sb("rows", [P, 2, 128])
        mats = sb("mats", [P, len(MATS), 128])
        vecs = sb("vecs", [P, len(VECS)])
        small = sb("small", [P, 1024])
        bank = [ctx.enter_context(nc.psum_tensor(f"bank{i}", [P, CHUNK], F32)) for i in range(NCH)]

        def mat(name):
            return mats[:, M[name], :]

        def vec(name, n=1):
            return vecs[:, V[name]:V[name] + n]

        def ch(t, c, p0=0, p1=P):
            return t[p0:p1, c * CHUNK:(c + 1) * CHUNK]

        VX = big[:, 0:PAIRS * HP * VW].rearrange("p (n w) -> p n w", w=VW)
        o = PAIRS * HP * VW
        BM = big[:, o:o + NWIN * 512].rearrange("p (w h k) -> p w h k", w=NWIN, h=HEADS)
        o += NWIN * 512
        wmask = big[:, o:o + NWIN * WT].rearrange("p (w k) -> p w k", w=NWIN)
        o += NWIN * WT
        cw1 = big[0:2, o:o + 128]
        PAD = big[:, 0:HALF * PH * PH].rearrange("p (b r c) -> p b r c", b=HALF, r=PH)
        o = HALF * PH * PH
        taps = big[:, o:o + KK * 128].rearrange("p (t n) -> p t n", t=KK)
        o += KK * 128
        wexp = big[0:33, o:o + KK * 128].rearrange("p (t n) -> p t n", t=KK)
        o += KK * 128
        stage = sb("stage", [P, 4608])
        QB = [stage[:, s * 128:(s + 1) * 128] for s in range(2)]
        OB = [stage[:, 256 + s * 128:256 + (s + 1) * 128] for s in range(2)]
        KX = [stage[:, 512 + s * 512:1024 + s * 512] for s in range(2)]
        SC = [stage[:, 1536 + s * 512:2048 + s * 512] for s in range(2)]
        PR = [stage[:, 2560 + s * 512:3072 + s * 512] for s in range(2)]
        PT = [stage[:, 3584 + s * 512:4096 + s * 512] for s in range(2)]
        PROD = [stage[:, s * 512:(s + 1) * 512] for s in range(4)]
        stats = small[:, 0:96].rearrange("p (b s) -> p b s", s=6)
        mv = small[:, 96:128].rearrange("p (b s) -> p b s", s=2)
        gst = small[:, 128:160]
        grp = small[:, 160:192]
        gvar = small[:, 192:208]
        gsq = small[:, 208:224]
        gsd = small[:, 224:240]
        grs = small[:, 240:256]
        qscale = small[:, 256:257]
        lsc = small[:, 257:258]
        rowmax = [small[:, 272 + 8 * s:280 + 8 * s] for s in range(2)]
        rden = [small[:, 288 + 8 * s:296 + 8 * s] for s in range(2)]
        rmask = [small[:, 304 + 16 * s:320 + 16 * s] for s in range(2)]
        ksum = small[:, 368:432]
        kinv = small[:, 432:496]
        knorm = small[:, 496:512]
        kln = small[:, 512:528]
        krs = small[:, 528:544]
        bqc = small[:, 544:545]
        xmean = small[:, 552:568]
        y2b = small[:, 568:584]
        gates2 = small[:, 600:856]
        bnv = small[:, 336:344]

        hmask = small[:, 352:360]
        ident2 = mats[:, M["stack"], 0:64]
        pmask = mats[:, M["stack"], 64:96]

        xw3 = T1[:, :].rearrange("p (b n) -> p b n", n=N)
        X3 = X[:, :].rearrange("p (b n) -> p b n", n=N)
        A3 = A[:, :].rearrange("p (b n) -> p b n", n=N)


        def gn_vector(dve, t, src, src_sem, src_val):
            for b in range(HALF):
                if b % 2 == 0:
                    dve.wait_ge(*when(src_sem, src_val(b // 2)))
                nc.vector.bn_stats(stats[:, b, :], src[:, b, :]).then_inc(S(t + "_stats"), 1)
            for b in range(HALF):
                dve.wait_ge(*when(t + "_stats", b + 1))
                nc.vector.bn_aggr(mv[:, b, :], stats[:, b, :]).then_inc(S(t + "_aggr"), 1)
            dve.wait_ge(*when(t + "_aggr", HALF))
            nc.vector.tensor_copy(gst[:, 0:16], mv[:, :, 0]).then_inc(S(t + "_gst"), 1)
            nc.vector.tensor_tensor(gsq, mv[:, :, 0], mv[:, :, 0], ALU.mult).then_inc(S(t + "_sq"), 1)
            dve.wait_ge(*when(t + "_sq", 1))
            nc.vector.tensor_tensor(gst[:, 16:32], gsq, mv[:, :, 1], ALU.add).then_inc(S(t + "_gst"), 1)
            dve.wait_ge(*when(t + "_grp", 1))
            nc.vector.tensor_copy(grp, bank[0][:, 0:32]).then_inc(S(t + "_grpc"), 1)
            dve.wait_ge(*when(t + "_grpc", 1))
            nc.vector.tensor_tensor(gsq, grp[:, 0:16], grp[:, 0:16], ALU.mult).then_inc(S(t + "_grpc"), 1)
            dve.wait_ge(*when(t + "_grpc", 2))
            nc.vector.tensor_tensor(gvar, grp[:, 16:32], gsq, ALU.subtract).then_inc(S(t + "_var"), 1)
            dve.wait_ge(*when(t + "_rs", 1))
            for b in range(HALF):
                nc.vector.tensor_scalar(A3[:, b, :], src[:, b, :], grp[:, b:b + 1], grs[:, b:b + 1],
                                        ALU.subtract, ALU.mult).then_inc(S(t + "_norm"), 1)

        def gn_tensor(pe, t):
            pe.wait_ge(*when(t + "_gst", 2))
            nc.tensor.matmul(bank[0][:, 0:32], mat("pair"), gst, start=True, stop=True).then_inc(S(t + "_grp"), 1)

        def gn_scalar(act, t):
            act.wait_ge(*when(t + "_var", 1))
            nc.scalar.activation(gsd, gvar, ACT.Ln, bias=vec("eps5")).then_inc(S(t + "_sd"), 1)
            act.wait_ge(*when(t + "_sd", 1))
            nc.scalar.activation(grs, gsd, ACT.Exp, scale=-0.5).then_inc(S(t + "_rs"), 1)

        def ln_tensor(pe, t, src, ready, val, left=None):
            def var(c):
                pe.wait_ge(*when(t + "_sq", c + 1))
                if c >= 4:
                    pe.wait_ge(*when(t + "_ln", c - 3))
                else:
                    pe.wait_ge(*when(ready, left or val(4 + c)))
                nc.tensor.matmul(bank[4 + c % 4][:, :], mat("mean"), ch(T2, c), start=True, stop=True) \
                    .then_inc(S(t + "_var"), 1)

            for c in range(NCH):
                pe.wait_ge(*when(ready, val(c)))
                if c >= 4:
                    pe.wait_ge(*when(t, c - 3))
                nc.tensor.matmul(bank[c % 4][:, :], mat("centre"), ch(src, c), start=True, stop=True) \
                    .then_inc(S(t + "_cen"), 1)
                if c >= 2:
                    var(c - 2)
            var(NCH - 2)
            var(NCH - 1)

        def ln_scalar(act, t, eps):
            act.preload_act_table_set("natural_log_exp_and_others")

            def rstd(c):
                act.wait_ge(*when(t + "_var", c + 1))
                nc.scalar.activation(ch(T2, c), bank[4 + c % 4][:, :], ACT.Ln, bias=vec(eps)).then_inc(S(t + "_ln"), 1)
                act.wait_ge(*when(t + "_ln", c + 1))
                nc.scalar.activation(ch(T2, c), ch(T2, c), ACT.Exp, scale=-0.5).then_inc(S(t + "_rstd"), 1)

            for c in range(NCH):
                act.wait_ge(*when(t + "_cen", c + 1))
                nc.scalar.activation(ch(T2, c), bank[c % 4][:, :], ACT.Square).then_inc(S(t + "_sq"), 1)
                if c >= 3:
                    rstd(c - 3)
            for c in range(NCH - 3, NCH):
                rstd(c)

        def ln_vector(dve, t, dst):
            for c in range(NCH):
                dve.wait_ge(*when(t + "_rstd", c + 1))
                nc.vector.tensor_tensor(ch(dst, c), bank[c % 4][:, :], ch(T2, c), ALU.mult).then_inc(S(t), 1)

        def rms_scalar(act, t, src, ready, eps):
            for c in range(NCH):
                act.wait_ge(*when(ready, c + 1))
                nc.scalar.activation(ch(T2, c), ch(src, c), ACT.Square).then_inc(S(t + "_sq"), 1)
            for c in range(NCH):
                act.wait_ge(*when(t + "_ms", c + 1))
                nc.scalar.activation(ch(T2, c), bank[c][:, :], ACT.Ln, bias=vec(eps)).then_inc(S(t + "_ln"), 1)
                act.wait_ge(*when(t + "_ln", c + 1))
                nc.scalar.activation(ch(T2, c), ch(T2, c), ACT.Exp, scale=-0.5).then_inc(S(t + "_rstd"), 1)

        def rms_tensor(pe, t):
            for c in range(NCH):
                pe.wait_ge(*when(t + "_sq", c + 1))
                nc.tensor.matmul(bank[c][:, :], mat("mean"), ch(T2, c), start=True, stop=True) \
                    .then_inc(S(t + "_ms"), 1)

        def steps(eng, f, last):
            for k in range(NWIN):
                f(k, k)
            with eng.Fori(1, HALF) as b:
                for w in range(NWIN):
                    f(b * NWIN + w, w)
            for k in range(PAIRS, PAIRS + last):
                f(k, k % NWIN)

        def at(k, lag):
            n = k - lag
            return n if not isinstance(k, int) or 0 <= n < PAIRS else None

        def reused(eng, name, n, per=1):
            if not isinstance(n, int) or n >= 2:
                eng.wait_ge(*when(name, (n - 1) * per))

        def steps2(eng, f, last):
            for k in range(2):
                f(k, k)
            with eng.Fori(1, HALF // 2) as b:
                for p in range(2):
                    f(b * 2 + p, p)
            for k in range(HALF, HALF + last):
                f(k, k % 2)

        def at2(k, lag):
            n = k - lag
            return n if not isinstance(k, int) or 0 <= n < HALF else None

        def steps3(eng, f):
            for r in range(3):
                f(0, r)
            with eng.Fori(1, 2 * NT // 3) as b:
                for r in range(3):
                    f(b, r)

        def later(n, k):
            return not isinstance(n, int) or n >= k

        def finish(dve, ready):
            dve.wait_ge(*when(ready, NCH))
            for c in range(NCH):
                nc.vector.tensor_copy(ch(X, c), ch(X, c)).then_inc(S("final"), 1)

        route = sb("route", [HALF, 512])
        lg, lc, ld, wk, o1, o2 = (route[:, 16 * i:16 * i + 16] for i in range(6))
        lg3, wk3, o13, o23 = (v.rearrange("p (h e) -> p h e", e=E) for v in (lg, wk, o1, o2))
        s2a, s2b, s2f = route[:, 96:98], route[:, 98:100], route[:, 100:102]
        gdiag = route[:, 256:512]
        lg5, wk5, o15, o25 = (ch(T1, i).rearrange("p (n e) -> p n e", e=E) for i in range(4))
        s5a, s5b, s5f = (T1[:, 2048 + 64 * i:2112 + 64 * i] for i in range(3))
        sel5, tot5, pre5a, pre5b, pos5, prod5 = (ch(T3, i) for i in range(6))
        nt5, end5, end5b, start5 = (T3[:, 3072 + 16 * i:3088 + 16 * i] for i in range(4))
        slot5 = T3[:, 3200:3328]
        cmp5 = T3[0:1, 3328:3328 + 2 * NT * E]
        exp5 = T3[0:1, 4000:4000 + 2 * NT]
        big16 = big[:, :].bitcast(F16)
        ups = big16[:, 0:E * 4 * HID3].rearrange("p (e v n) -> p e v n", e=E, v=4)
        downs = l2w[:, :].bitcast(F16)[0:HB, 0:E * NHB * 2 * C].rearrange("p (n) -> p n")
        w2v = downs.rearrange("p (e k v c) -> p e k v c", e=E, k=NHB, v=2)
        WS5 = [stage[:, HID3 * i:HID3 * i + HID3] for i in range(2)]
        zeros5 = stage[:, 2560:4608]
        rows5 = T2[:, :].bitcast(F16)
        rows5v = rows5.rearrange("p (j h v) -> p j h v", h=2, v=128)
        xtok = T4.rearrange("p (j h c) -> p j h c", h=2, c=C)
        G5 = [t.rearrange("p (j k c) -> p j k c", k=2, c=C) for t in (A[:, :], X[:, :])]
        s16 = stage[:, :].bitcast(F16)
        XS = [s16[:, 256 * i:256 * i + 256].rearrange("p (i v) -> p i v", v=128) for i in range(3)]
        XT = [s16[:, 768 + 256 * i:1024 + 256 * i] for i in range(3)]
        HI5 = [s16[0:HB, 1536 + 256 * i:1792 + 256 * i] for i in range(3)]
        LO5 = [s16[0:HB, 2304 + 256 * i:2560 + 256 * i] for i in range(3)]
        S5 = [stage[0:HB, 1536 + 256 * i:1792 + 256 * i] for i in range(3)]
        H5 = [stage[0:HB, 2304 + 256 * i:2560 + 256 * i] for i in range(3)]
        Y5 = [stage[:, 3072 + 128 * i:3200 + 128 * i].rearrange("p (i c) -> p i c", c=C) for i in range(3)]
        M5 = stage[:, 3456:3968].rearrange("p (j k c) -> p j k c", k=2, c=C)
        HID = [stage[:, 512 * i:512 * i + 512] for i in range(4)]
        W2G = [stage[:, 2048 + 1024 * i:3072 + 1024 * i] for i in range(2)]
        CAPACITY = float(-(-B * N * 5 // 4 // E))

        block = ctx.enter_context(nc.Block())

        @block.sync
        def _(sp):
            sp.dma_start(T1[:, :], xw_d).then_inc(S("loaded_xw"), 16)
            sp.dma_start(mats[:, :, :], mats_d).then_inc(S("loaded_mats"), 16)
            sp.dma_start(vecs[:, :], vecs_d).then_inc(S("loaded_vecs"), 16)
            sp.dma_start(T2[0:2, :], feats_d).then_inc(S("loaded_feats"), 16)
            sp.dma_start(cw1, cw1_d).then_inc(S("loaded_feats"), 16)
            sp.dma_start(wmask, wmask_d).then_inc(S("loaded_wmask"), 16)
            sp.dma_start(X[:, :], xi_d).then_inc(S("loaded_xi"), 16)
            sp.wait_ge(*when("l0_obd", PAIRS))
            sp.wait_ge(*when("l0_pv", PAIRS))
            sp.dma_start(taps, taps_d).then_inc(S("loaded_taps"), 16)
            sp.dma_start(wexp, wexp_d).then_inc(S("loaded_taps"), 16)
            sp.wait_ge(*when("loaded_taps", 32))
            sp.dma_start(up2[:, :, :, :], w1l2_d).then_inc(S("loaded_l2"), 16)
            sp.dma_start(w2l2[:, :, :], w2l2_d).then_inc(S("loaded_l2"), 16)
            sp.wait_ge(*when("loaded_l2", 32))
            if stop == 5:
                sp.wait_ge(*when("zeros5", 1))
                for h in range(2):
                    flat = slots_d[h].rearrange("(p a) v -> p (a v)", p=128)
                    n = NT * SLOTS
                    for i in range(3):
                        sp.dma_start(flat[:, i * n // 3:(i + 1) * n // 3],
                                     zeros5.bitcast(F16)[:, 0:n // 3]).then_inc(S("slots_zero"), 16)
                sp.wait_ge(*when("slots_zero", 96))
                for i in range(2 * E):
                    if i >= 2:
                        sp.wait_ge(*when("ups_split", 2 * (i - 1)))
                    sp.dma_start(WS5[i % 2], (w1l3_d, w3l3_d)[i % 2][:, i // 2, :]).then_inc(S(f"loaded_l3_{i % 2}"), 16)
                for e in range(E):
                    i = 2 * E + e
                    sp.wait_ge(*when("ups_split", 2 * (i - 1)))
                    sp.dma_start(WS5[i % 2][0:HB, 0:NHB * C], w2l3_d[:, e, :, :].rearrange("p k c -> p (k c)")) \
                        .then_inc(S(f"loaded_l3_{i % 2}"), 16)

                def load5(t, s, h):
                    if later(t, 3):
                        sp.wait_ge(*when("turned5", t - 2))
                    rows = slots_d[h][bass.ds((t - h * NT) * SLOTS, SLOTS), :]
                    sp.dma_start(XS[s], rows.rearrange("(p i) v -> p i v", i=2)).then_inc(S(f"loaded_xs_{s}"), 16)

                def store5(t, s, h):
                    sp.wait_ge(*when("y5", t + 1))
                    rows = results_d[h][bass.ds((t - h * NT) * SLOTS, SLOTS), :]
                    sp.dma_start(rows.rearrange("(p i) c -> p i c", i=2), Y5[s]).then_inc(S(f"stored_y_{s}"), 16)

                sp.wait_ge(*when("scattered_0", 16 * 2 * TILES))
                for t in range(3):
                    load5(t, t, 0)
                with sp.Fori(0, NT // 3 - 1) as b:
                    for r in range(3):
                        load5(b * 3 + (r + 3), r, 0)
                        store5(b * 3 + r, r, 0)
                sp.wait_ge(*when("scattered_1", 16 * 2 * TILES))
                for r in range(3):
                    load5(NT + r, r, 1)
                    store5(NT - 3 + r, r, 0)
                with sp.Fori(NT // 3, 2 * NT // 3 - 1) as b:
                    for r in range(3):
                        load5(b * 3 + (r + 3), r, 1)
                        store5(b * 3 + r, r, 1)
                for r in range(3):
                    store5(2 * NT - 3 + r, r, 1)
                out5 = out_d.rearrange("p (j h c) -> p j h c", h=2, c=C)
                for h in range(2):
                    for c in range(NCH):
                        sp.wait_ge(*when("mixed5", h * NCH + c + 1))
                        sp.dma_start(out5[:, 4 * c:4 * c + 4, h, :], xtok[:, 4 * c:4 * c + 4, h, :]) \
                            .then_inc(S("stored"), 16)
                sp.wait_ge(*when("stored", 16 * 2 * NCH))
                return
            for c in range(NCH):
                sp.wait_ge(*when("final", c + 1))
                sp.dma_start(ch(out_d, c), ch(X, c)).then_inc(S("stored"), 16)
            sp.wait_ge(*when("stored", 16 * NCH))

        @block.gpsimd
        def _(pool):
            nc.gpsimd.memset(big[:, 0:PAIRS * HP * VW], 0.0).then_inc(S("vx_zero"), 1)
            def stage_keys(k, w):
                n, s = at(k, 0), w % 2
                if n is None:
                    return
                pool.wait_ge(*when("q_norm", (NCH if not isinstance(n, int) else n // NWIN // 2 + 1)))
                pool.wait_ge(*when("k_norm", (NCH if not isinstance(n, int) else n // NWIN // 2 + 1)))
                reused(pool, "l0_scores", n)
                nc.gpsimd.tensor_tensor(QB[s].rearrange("p (h q) -> p h q", h=2),
                                        T1[:, bass.ds(n * WT, WT)].unsqueeze(1).broadcast_to([P, 2, WT]),
                                        vec("half0", 2).unsqueeze(2).broadcast_to([P, 2, WT]),
                                        ALU.mult).then_inc(S("l0_staged"), 1)
                nc.gpsimd.tensor_tensor(KX[s].rearrange("p (h k) -> p h k", h=HEADS),
                                        T2[:, bass.ds(n * WT, WT)].unsqueeze(1).broadcast_to([P, HEADS, WT]),
                                        hmask.unsqueeze(2).broadcast_to([P, HEADS, WT]),
                                        ALU.mult).then_inc(S("l0_staged"), 1)

            pool.wait_ge(*when("hmask", 1))
            steps(pool, stage_keys, 0)

            pool.wait_ge(*when("l0_pv", PAIRS))
            nc.gpsimd.memset(big[:, 0:HALF * PH * PH], 0.0).then_inc(S("pad_zero"), 1)

            if stop < 3:
                return
            pool.wait_ge(*when("gates2", 1))
            pool.wait_ge(*when("loaded_l2", 32))

            def gate_w2(k, p):
                b = at2(k, 0)
                if b is None:
                    return
                if not isinstance(b, int) or b >= 2:
                    pool.wait_ge(*when("down3", E * (b - 1)))
                for h in range(2):
                    nc.gpsimd.tensor_tensor(
                        W2G[p][:, 512 * h:512 * h + 512].rearrange("p (e c) -> p e c", e=E), w2l2[:, :, :],
                        gates2[:, bass.ds(b * 16 + 8 * h, E)].unsqueeze(2).broadcast_to([P, E, C]), ALU.mult) \
                        .then_inc(S("w2_gated"), 1)

            steps2(pool, gate_w2, 0)
            if stop < 5:
                return
            pool.wait_ge(*when("down3", E * HALF))
            nc.gpsimd.memset(zeros5, 0.0).then_inc(S("zeros5"), 1)
            for i in range(3 * E):
                pool.wait_ge(*when(f"loaded_l3_{i % 2}", 16 * (i // 2 + 1)))
                if i < 2 * E:
                    src, hi, lo = WS5[i % 2], ups[:, i // 2, 2 * (i % 2), :], ups[:, i // 2, 2 * (i % 2) + 1, :]
                else:
                    src = WS5[i % 2][0:HB, 0:NHB * C].rearrange("p (k c) -> p k c", c=C)
                    hi, lo = w2v[:, i - 2 * E, :, 0, :], w2v[:, i - 2 * E, :, 1, :]
                nc.gpsimd.tensor_copy(hi, src).then_inc(S("ups_split"), 1)
                pool.wait_ge(*when("ups_split", 2 * i + 1))
                nc.gpsimd.tensor_tensor(lo, src, hi, ALU.subtract).then_inc(S("ups_split"), 1)
            pool.wait_ge(*when("index5", 2))
            pool.wait_ge(*when("rows5_low", NCH))
            pool.wait_ge(*when("slots_zero", 96))
            for h in range(2):
                for j in range(TILES):
                    for k in range(2):
                        n = 2 * j + h
                        pool.indirect_dma_start(
                            slots_d[h], bass.IndirectOffsetOnAxis(ap=index[:, k, n:n + 1], axis=0),
                            rows5[:, n * 128:(n + 1) * 128], None).then_inc(S(f"scattered_{h}"), 16)
            for h in range(2):
                for s in range(3):
                    pool.wait_ge(*when(f"stored_y_{s}", 16 * NT // 3 * (h + 1)))
                for j in range(TILES):
                    for k in range(2):
                        n = 2 * j + h
                        pool.indirect_dma_start(
                            G5[h][:, j, k, :], None, results_d[h],
                            bass.IndirectOffsetOnAxis(ap=index[:, k, n:n + 1], axis=0)).then_inc(S(f"gathered_{h}_{j // 4}"), 16)

        @block.vector
        def _(dve):
            dve.wait_ge(*when("loaded_mats", 16))
            dve.wait_ge(*when("loaded_vecs", 16))
            nc.vector.tensor_tensor(hmask, mats[:, M["head"], 0:64:8], mats[:, M["head"], 64:128:8],
                                    ALU.add).then_inc(S("hmask"), 1)
            nc.vector.tensor_copy(ident16[:, :], mat("ident")).then_inc(S("ident16"), 1)
            nc.vector.tensor_scalar(lsc, vec("ls0"), float(np.log(np.float32(100.0))), None, ALU.min) \
                .then_inc(S("lsc"), 1)
            dve.wait_ge(*when("vx_zero", 1))
            for j in range(2):
                nc.vector.tensor_copy(VX[:, :, 32 + j], vec(f"par{j}").broadcast_to([P, PAIRS * HP])) \
                    .then_inc(S("vx_ones"), 1)
            gn_vector(dve, "g0", xw3, "loaded_xw", lambda c: 16)
            dve.wait_ge(*when("bias_exp", 1))
            bz = ch(T3, 1)
            nc.vector.tensor_scalar(bz, ch(T3, 0), 1.0, None, ALU.add).then_inc(S("bias_v"), 1)
            dve.wait_ge(*when("bias_v", 1))
            nc.vector.reciprocal(ch(T3, 2), bz).then_inc(S("bias_v"), 1)
            dve.wait_ge(*when("bias_v", 2))
            nc.vector.tensor_scalar(ch(T3, 3).rearrange("p (h k) -> p k h", h=HEADS),
                                    ch(T3, 2).rearrange("p (k h) -> p k h", h=HEADS), 16.0, None, ALU.mult) \
                .then_inc(S("bias_v"), 1)
            dve.wait_ge(*when("bias_v", 3))
            dve.wait_ge(*when("loaded_wmask", 16))
            for w in range(NWIN):
                nc.vector.tensor_tensor(BM[:, w, :, :], ch(T3, 3).rearrange("p (h k) -> p h k", h=HEADS),
                                        wmask[:, w, :].unsqueeze(1).broadcast_to([P, HEADS, WT]),
                                        ALU.add).then_inc(S("bm_ready"), 1)
            dve.wait_ge(*when("bm_ready", NWIN))
            for t, T in (("q", T1), ("k", T2)):
                for c in range(NCH):
                    dve.wait_ge(*when(t + "_proj", c + 1))
                    nc.vector.tensor_scalar(ch(T, c), bank[c][:, :], vec(f"b{t}0"), None, ALU.add) \
                        .then_inc(S(t + "_biased"), 1)
                for c in range(NCH):
                    dve.wait_ge(*when(t + "_ssq", c + 1))
                    nc.vector.tensor_scalar(ch(T3, c), bank[c][:, :], 1e-24, 2.0 ** 20, ALU.max, ALU.mult) \
                        .then_inc(S(t + "_clip"), 1)
                if t == "q":
                    dve.wait_ge(*when("qscale", 1))
                for c in range(NCH):
                    dve.wait_ge(*when(t + "_rlen", c + 1))
                    nc.vector.scalar_tensor_tensor(ch(T, c), ch(T3, c), qscale if t == "q" else 1.0, ch(T, c),
                                                   ALU.mult, ALU.mult).then_inc(S(t + "_norm"), 1)
            dve.wait_ge(*when("vx_zero", 1))
            for g in range(PAIRS // 4):
                dve.wait_ge(*when("v_proj", g + 1))
                for x in range(2):
                    nc.vector.tensor_copy(
                        VX[64 * x:64 * x + 64, g * 16:g * 16 + 16, 0:32]
                        .rearrange("p n (h x d) -> p n h x d", h=2, x=2)[:, :, :, x, :],
                        bank[g % NCH][64 * x:64 * x + 64, 0:256].rearrange("p (n h d) -> p n h d", h=2, d=DH)) \
                        .then_inc(S("v_ready"), 1)

            def softmax_and_out(k, w):
                n, s = at(k, 0), w % 2
                if n is not None:
                    sc = SC[s].rearrange("p (h k) -> p h k", h=HEADS)
                    dve.wait_ge(*when("l0_scores", n + 1))
                    reused(dve, "l0_exp", n)
                    nc.vector.tensor_tensor(sc, bank[s][:, :].rearrange("p (h k) -> p h k", h=HEADS),
                                            BM[:, w, :, :], ALU.add).then_inc(S("l0_biased"), 1)
                    dve.wait_ge(*when("l0_biased", n + 1))
                    nc.vector.tensor_reduce(rowmax[s], sc, AX, ALU.max).then_inc(S("l0_max"), 1)
                    dve.wait_ge(*when("l0_max", n + 1))
                    nc.vector.tensor_tensor(sc, sc, rowmax[s].unsqueeze(2).broadcast_to([P, HEADS, WT]),
                                            ALU.subtract).then_inc(S("l0_shifted"), 1)
                n = at(k, 2)
                if n is not None:
                    ob = bank[4 + s][:, 0:HP * VW].rearrange("p (g v) -> p g v", v=VW)
                    dve.wait_ge(*when("l0_pv", n + 1))
                    nc.vector.reciprocal(rden[s].rearrange("p (g x) -> p g x", x=2), ob[:, :, 32:34]) \
                        .then_inc(S("l0_rden"), 1)
                    dve.wait_ge(*when("l0_rden", n + 1))
                    rd = rden[s].rearrange("p (g x) -> p g x", x=2)
                    for h in range(2):
                        nc.vector.tensor_scalar(rmask[s].rearrange("p (g h x) -> p g h x", h=2, x=2)[:, :, h, :],
                                                rd, vec(f"half{h}"), None, ALU.mult).then_inc(S("l0_rmask"), 1)
                    dve.wait_ge(*when("l0_rmask", (n + 1) * 2))
                    reused(dve, "l0_ot", n)
                    nc.vector.tensor_tensor(OB[s].rearrange("p (g y d) -> p g y d", g=HP, d=DH),
                                            ob[:, :, 0:32].rearrange("p g (y d) -> p g y d", d=DH),
                                            rmask[s].rearrange("p (g y) -> p g y", g=HP).unsqueeze(3)
                                            .broadcast_to([P, HP, 4, DH]), ALU.mult).then_inc(S("l0_obd"), 1)

            dve.wait_ge(*when("v_ready", PAIRS // 2))
            steps(dve, softmax_and_out, 2)
            for c in range(NCH):
                dve.wait_ge(*when("l0_wo", c + 1))
                nc.vector.tensor_scalar(ch(T4, c), bank[c][:, :], vec("bo0"), None, ALU.add) \
                    .then_inc(S("l0_res"), 1)
            dve.wait_ge(*when("l0_res", NCH))
            dve.wait_ge(*when("loaded_xi", 16))
            Xi = X[:, :].rearrange("p (b r c) -> p b r c", r=HH, c=WW)
            Tw = T4[:, :].rearrange("p (b w i j) -> p b w i j", w=NWIN, i=WS, j=WS)
            runs = [(0, 0, SS, WS), (1, 0, SS + WS, WS - SS), (1, WS - SS, 0, SS)]
            for wy, iy, r, nr in runs:
                for wx, ix, q, nq in runs:
                    xv = Xi[:, :, r:r + nr, q:q + nq]
                    nc.vector.tensor_tensor(xv, xv, Tw[:, :, 2 * wy + wx, iy:iy + nr, ix:ix + nq], ALU.add) \
                        .then_inc(S("x1_ready"), 1)
            if stop == 0:
                dve.wait_ge(*when("x1_ready", 9))
                for c in range(NCH):
                    nc.vector.tensor_copy(ch(X, c), ch(X, c)).then_inc(S("final"), 1)
                return

            gn_vector(dve, "g1", X3, "x1_ready", lambda c: 9)
            sc_, sh_ = bnv[:, 3:4], bnv[:, 5:6]
            dve.wait_ge(*when("bn_rs", 1))
            nc.vector.tensor_tensor(bnv[:, 4:5], vec("br1"), vec("mu1"), ALU.subtract).then_inc(S("bn_v"), 1)
            dve.wait_ge(*when("bn_v", 1))
            nc.vector.tensor_tensor(sc_, bnv[:, 2:3], vec("ga1"), ALU.mult).then_inc(S("bn_v"), 1)
            dve.wait_ge(*when("bn_v", 2))
            nc.vector.scalar_tensor_tensor(sh_, bnv[:, 4:5], sc_, vec("be1"), ALU.mult, ALU.add) \
                .then_inc(S("bn_v"), 1)
            nc.vector.memset(T1[32:33, :], 1.0).then_inc(S("r_one"), 1)
            for c in range(NCH):
                dve.wait_ge(*when("xi_kept", min(c + 1, NCH)))
                for t in range(KK):
                    k, i, j = c * KK + t, t // 3, t % 3
                    dve.wait_ge(*when("tap_w", k + 1))
                    if k >= 4:
                        dve.wait_ge(*when("tap_summed", k - 3))
                    nc.vector.tensor_tensor(
                        PROD[k % 4].rearrange("p (b r c) -> p b r c", r=HH, c=WW),
                        bank[k % 4][:, :].rearrange("p (b r c) -> p b r c", r=HH, c=WW),
                        PAD[:, 2 * c:2 * c + 2, i:i + HH, j:j + WW], ALU.mult).then_inc(S("tap_prod"), 1)
                    if t == 3 and c:
                        dve.wait_ge(*when("tap_summed", c * KK))
                        nc.vector.tensor_tensor(ch(X, c - 1), ch(X, c - 1), bank[4 + (c - 1) % 2][:, :], ALU.add) \
                            .then_inc(S("x2_ready"), 1)
            dve.wait_ge(*when("tap_summed", NCH * KK))
            nc.vector.tensor_tensor(ch(X, NCH - 1), ch(X, NCH - 1), bank[4 + (NCH - 1) % 2][:, :], ALU.add) \
                .then_inc(S("x2_ready"), 1)
            if stop == 1:
                finish(dve, "x2_ready")
                return

            ln_vector(dve, "a2", A)
            for i in range(2):
                dve.wait_ge(*when("w2_centred", i + 1))
                nc.vector.tensor_copy(mat(("wq2t", "wk2t")[i]), bank[i][:, 0:128]).then_inc(S("w2_kept"), 1)
            for i in range(2):
                dve.wait_ge(*when("w2_centred", i + 3))
                nc.vector.tensor_copy(rows[:, i, :], bank[2 + i][:, 0:128]).then_inc(S("w2_kept"), 1)
            dve.wait_ge(*when("w2_centred", 5))
            nc.vector.tensor_copy(bqc, bank[4][:, 0:1]).then_inc(S("w2_kept"), 1)
            dve.wait_ge(*when("w2_kept", 5))
            for c in range(NCH):
                dve.wait_ge(*when("k2_proj", c + 1))
                nc.vector.tensor_tensor(ch(T1, c).rearrange("p (j n) -> p j n", n=128),
                                        bank[c][:, :].rearrange("p (j n) -> p j n", n=128),
                                        rows[:, 0, :].unsqueeze(1).broadcast_to([P, 4, 128]), ALU.add) \
                    .then_inc(S("k2_biased"), 1)
            for c in range(NCH):
                dve.wait_ge(*when("v2_proj", c + 1))
                nc.vector.tensor_tensor(ch(T3, c).rearrange("p (j n) -> p j n", n=128),
                                        bank[c][:, :].rearrange("p (j n) -> p j n", n=128),
                                        rows[:, 1, :].unsqueeze(1).broadcast_to([P, 4, 128]), ALU.add) \
                    .then_inc(S("v2_kept"), 1)
            for c in range(NCH):
                dve.wait_ge(*when("k2_sq", c + 1))
                nc.vector.tensor_reduce(ksum[:, 8 * c:8 * c + 8], ch(T1, c).rearrange("p (j n) -> p j n", n=64),
                                        AX, ALU.add).then_inc(S("k2_sum"), 1)
            dve.wait_ge(*when("k2_sum", NCH))
            nc.vector.tensor_scalar(ksum, ksum, 1e-7, None, ALU.add).then_inc(S("k2_sum"), 1)
            dve.wait_ge(*when("k2_sum", NCH + 1))
            nc.vector.reciprocal(kinv, ksum).then_inc(S("k2_inv"), 1)
            dve.wait_ge(*when("k2_inv", 1))
            for c in range(NCH):
                k = ch(T1, c).rearrange("p (j n) -> p j n", n=64)
                nc.vector.tensor_tensor(k, k, kinv[:, 8 * c:8 * c + 8].unsqueeze(2).broadcast_to([P, 8, 64]),
                                        ALU.mult).then_inc(S("k2_ready"), 1)
            dve.wait_ge(*when("k2_norm", 1))
            nc.vector.tensor_scalar(knorm, bank[4][:, 0:HALF], 1e-24, 2.0 ** 40, ALU.max, ALU.mult) \
                .then_inc(S("k2_clip"), 1)
            dve.wait_ge(*when("k2_rs", 1))
            for b in range(HALF):
                dve.wait_ge(*when("kv2", 4 * (b // 4 + 1)))
                nc.vector.scalar_tensor_tensor(KVS[:, b, :], bank[b // 4][:, (b % 4) * 128:(b % 4 + 1) * 128],
                                               krs[:, b:b + 1], mat("sum"), ALU.mult, ALU.mult) \
                    .then_inc(S("kv2_kept"), 1)
            for c in range(NCH):
                dve.wait_ge(*when("q2_guard", c + 1))
                dve.wait_ge(*when("q2_s2", c + 1))
                nc.vector.scalar_tensor_tensor(ch(T1, c), bank[4 + c % 4][:, :], 2.0 ** 40, ch(T1, c),
                                               ALU.mult, ALU.max).then_inc(S("q2_clip"), 1)
                if c >= 2:
                    dve.wait_ge(*when("q2_rs", c - 1))
                    nc.vector.tensor_tensor(ch(T2, c - 2), ch(T2, c - 2), ch(T1, c - 2), ALU.mult) \
                        .then_inc(S("q2_ready"), 1)
            for c in range(NCH - 2, NCH):
                dve.wait_ge(*when("q2_rs", c + 1))
                nc.vector.tensor_tensor(ch(T2, c), ch(T2, c), ch(T1, c), ALU.mult).then_inc(S("q2_ready"), 1)
            for c in range(NCH):
                dve.wait_ge(*when("o2_proj", c + 1))
                nc.vector.scalar_tensor_tensor(ch(X, c), bank[c][:, :], vec("bo2"), ch(X, c), ALU.add, ALU.add) \
                    .then_inc(S("x3_ready"), 1)
            if stop == 2:
                finish(dve, "x3_ready")
                return

            ln_vector(dve, "a3", A)
            for c in range(NCH):
                dve.wait_ge(*when("a3", c + 1))
                nc.vector.tensor_reduce(xmean[:, 2 * c:2 * c + 2], ch(A, c).rearrange("p (b n) -> p b n", n=N),
                                        AX, ALU.add).then_inc(S("r3_mean"), 1)
            links = [0]

            def link(instruction):
                links[0] += 1
                instruction.then_inc(S("link"), 1)
                dve.wait_ge(*when("link", links[0]))

            def top2(p, n, probs, work, one1, one2, max1, max2, first):
                def spread(v):
                    return v.unsqueeze(2).broadcast_to([p, n, E])
                rank = vec("rank0", E)[0:p, :].unsqueeze(1).broadcast_to([p, n, E])
                for one, best, src in ((one1, max1, probs), (one2, max2, work)):
                    link(nc.vector.tensor_reduce(best, src, AX, ALU.max))
                    link(nc.vector.tensor_tensor(one, src, spread(best), ALU.is_ge))
                    link(nc.vector.tensor_tensor(one, one, rank, ALU.mult))
                    link(nc.vector.tensor_reduce(first, one, AX, ALU.max))
                    link(nc.vector.tensor_tensor(one, rank, spread(first), ALU.is_equal))
                    if one is one1:
                        link(nc.vector.scalar_tensor_tensor(work, one, -4.0, probs, ALU.mult, ALU.add))

            def softmax_vector(p, n, z, m, t):
                link(nc.vector.tensor_reduce(m, z, AX, ALU.max))
                nc.vector.tensor_tensor(z, z, m.unsqueeze(2).broadcast_to([p, n, E]), ALU.subtract) \
                    .then_inc(S(t + "_in"), 1)
                dve.wait_ge(*when(t + "_exp", 1))
                link(nc.vector.tensor_reduce(m, z, AX, ALU.add))
                link(nc.vector.reciprocal(m, m))
                link(nc.vector.tensor_tensor(z, z, m.unsqueeze(2).broadcast_to([p, n, E]), ALU.mult))

            dve.wait_ge(*when("r3_logits", 1))
            link(nc.vector.scalar_tensor_tensor(lg, bank[0][0:HALF, 0:16], 1.0 / N,
                                                vecs[0:HALF, V["brr0"]:V["brr0"] + 16], ALU.mult, ALU.add))
            softmax_vector(HALF, 2, lg3, s2a, "sm1")
            nc.vector.tensor_copy(lc, lg).then_inc(S("r3_rw"), 1)
            dve.wait_ge(*when("r3_load", 1))
            link(nc.vector.tensor_copy(ld, bank[1][0:HALF, 0:16]))
            link(nc.vector.tensor_tensor(ld[:, 0:8], ld[:, 0:8], ld[:, 8:16], ALU.add))
            link(nc.vector.reciprocal(ld[:, 8:16], ld[:, 0:8]))
            link(nc.vector.tensor_scalar(ld[:, 8:16], ld[:, 8:16], CAPACITY / N, 1.0, ALU.mult, ALU.min))
            link(nc.vector.tensor_tensor(lg3, lg3, ld[:, 8:16].unsqueeze(1).broadcast_to([HALF, 2, E]), ALU.mult))
            softmax_vector(HALF, 2, lg3, s2a, "sm2")
            top2(HALF, 2, lg3, wk3, o13, o23, s2a, s2b, s2f)
            nc.vector.tensor_tensor(s2b, s2b, s2a, ALU.subtract).then_inc(S("sm3_in"), 1)
            dve.wait_ge(*when("sm3_exp", 1))
            link(nc.vector.tensor_scalar(s2a, s2b, 1.0, None, ALU.add))
            link(nc.vector.reciprocal(s2a, s2a))
            link(nc.vector.tensor_tensor(s2b, s2a, s2b, ALU.mult))
            link(nc.vector.tensor_tensor(o13, o13, s2a.unsqueeze(2).broadcast_to([HALF, 2, E]), ALU.mult))
            link(nc.vector.tensor_tensor(o23, o23, s2b.unsqueeze(2).broadcast_to([HALF, 2, E]), ALU.mult))
            link(nc.vector.tensor_tensor(o13, o13, o23, ALU.add))
            nc.vector.tensor_tensor(gdiag.rearrange("p (b g) -> p b g", g=16),
                                    mats[0:HALF, M["ident"], 0:HALF].unsqueeze(2).broadcast_to([HALF, HALF, 16]),
                                    o1.unsqueeze(1).broadcast_to([HALF, HALF, 16]), ALU.mult) \
                .then_inc(S("r3_diag"), 1)
            dve.wait_ge(*when("r3_gates", 1))
            nc.vector.tensor_copy(gates2, bank[2][:, 0:256]).then_inc(S("gates2"), 1)
            dve.wait_ge(*when("gates2", 1))
            g4 = gates2.rearrange("p (b h e) -> p b h e", h=2, e=E)
            tb = ch(T4, 0)[:, 0:128].rearrange("p (b e) -> p b e", e=E)
            for h in range(2):
                q = slice(64 * h, 64 * h + 64)
                nc.vector.tensor_tensor(tb[q], g4[q, :, h, :],
                                        vec("b2_0", E)[q, :].unsqueeze(1).broadcast_to([64, HALF, E]), ALU.mult) \
                    .then_inc(S("b2_prod"), 1)
            dve.wait_ge(*when("b2_prod", 2))
            link(nc.vector.tensor_reduce(y2b, tb, AX, ALU.add))

            def mix2(k, p):
                b = at2(k, 1)
                if b is not None:
                    dve.wait_ge(*when("down3", E * (b + 1)))
                    nc.vector.scalar_tensor_tensor(T1[:, bass.ds(b * N, N)], bank[4 + (p + 1) % 2][:, 0:N],
                                                   y2b[:, bass.ds(b, 1)], A[:, bass.ds(b * N, N)], ALU.add, ALU.add) \
                        .then_inc(S("y3_kept"), 1)

            steps2(dve, mix2, 1)
            ln_vector(dve, "l3", T3)
            for c in range(NCH):
                dve.wait_ge(*when("l3", c + 1))
                nc.vector.scalar_tensor_tensor(ch(X, c), ch(T3, c), vec("ga3"), ch(X, c), ALU.mult, ALU.add) \
                    .then_inc(S("x4_part"), 1)
            for c in range(NCH):
                dve.wait_ge(*when("x4_part", c + 1))
                nc.vector.tensor_scalar(ch(X, c), ch(X, c), vec("be3"), None, ALU.add).then_inc(S("x4_ready"), 1)
            if stop == 3:
                finish(dve, "x4_ready")
                return

            ln_vector(dve, "a4", A)
            for c in range(NCH):
                dve.wait_ge(*when("n4_rstd", c + 1))
                nc.vector.scalar_tensor_tensor(ch(T1, c), ch(T2, c), vec("n14"), ch(A, c), ALU.mult, ALU.mult) \
                    .then_inc(S("n4"), 1)
            for t, T in (("k", T3), ("q", T2)):
                for c in range(NCH):
                    dve.wait_ge(*when(t + "4_proj", c + 1))
                    nc.vector.tensor_scalar(ch(T, c), bank[c][:, :], 0.0, None, ALU.min).then_inc(S(t + "4_neg"), 1)
                    if c >= 2:
                        dve.wait_ge(*when(t + "4_exp", c - 1))
                        nc.vector.scalar_tensor_tensor(ch(T, c - 2), bank[c - 2][:, :], 0.0, ch(T, c - 2),
                                                       ALU.max, ALU.add).then_inc(S(t + "4_elu"), 1)
                for c in range(NCH - 2, NCH):
                    dve.wait_ge(*when(t + "4_exp", c + 1))
                    nc.vector.scalar_tensor_tensor(ch(T, c), bank[c][:, :], 0.0, ch(T, c),
                                                   ALU.max, ALU.add).then_inc(S(t + "4_elu"), 1)
                if t == "k":
                    for c in range(NCH):
                        dve.wait_ge(*when("v4_proj", c + 1))
                        nc.vector.tensor_copy(ch(T4, c), bank[c][:, :]).then_inc(S("v4_kept"), 1)
                    for c in range(4):
                        dve.wait_ge(*when("kv4", 4 * (c + 1)))
                        nc.vector.tensor_tensor(KVS[:, 4 * c:4 * c + 4, :],
                                                bank[c][:, :].rearrange("p (b n) -> p b n", n=128),
                                                mat("head").unsqueeze(1).broadcast_to([P, 4, 128]), ALU.mult) \
                            .then_inc(S("kv4_kept"), 1)
                    dve.wait_ge(*when("ks4", 1))
                    nc.vector.tensor_copy(krs, bank[4][:, 0:HALF]).then_inc(S("ks4_kept"), 1)
                    dve.wait_ge(*when("ks4_kept", 1))
                    for c in range(4):
                        nc.vector.tensor_tensor(KSS[:, 4 * c:4 * c + 4, :],
                                                krs[:, 4 * c:4 * c + 4].unsqueeze(2).broadcast_to([P, 4, 128]),
                                                mat("head").unsqueeze(1).broadcast_to([P, 4, 128]), ALU.mult) \
                            .then_inc(S("kv4_kept"), 1)
            for c in range(NCH):
                dve.wait_ge(*when("z4", c + 1))
                dve.wait_ge(*when("num4", c + 1))
                nc.vector.tensor_tensor(ch(T1, c), bank[4 + c % 4][:, :], ch(T3, c), ALU.mult).then_inc(S("o4"), 1)
            for c in range(NCH):
                dve.wait_ge(*when("o4_proj", c + 1))
                nc.vector.scalar_tensor_tensor(ch(T4, c), bank[c][:, :], vec("bo4"), ch(A, c), ALU.add, ALU.add) \
                    .then_inc(S("h4"), 1)
            for c in range(NCH):
                dve.wait_ge(*when("h4", c + 1))
                nc.vector.tensor_tensor(ch(X, c), ch(X, c), ch(T4, c), ALU.add).then_inc(S("x5_part"), 1)
            for c in range(NCH):
                dve.wait_ge(*when("m4_rstd", c + 1))
                nc.vector.scalar_tensor_tensor(ch(T4, c), ch(T4, c), vec("n24"), ch(T2, c), ALU.mult, ALU.mult) \
                    .then_inc(S("m4"), 1)
            for c in range(NCH):
                dve.wait_ge(*when("m4", c + 1))
                nc.vector.tensor_tensor(ch(X, c), ch(X, c), ch(T4, c), ALU.add).then_inc(S("x5_ready"), 1)
            if stop == 4:
                finish(dve, "x5_ready")
                return

            ln_vector(dve, "a5", A)
            dve.wait_ge(*when("r5_logits", 1))
            link(nc.vector.tensor_copy(ch(T1, 0), bank[0][:, :]))
            softmax_vector(P, 2 * TILES, lg5, s5a, "sm4")
            top2(P, 2 * TILES, lg5, wk5, o15, o25, s5a, s5b, s5f)
            link(nc.vector.tensor_tensor(s5f, s5a, s5b, ALU.add))
            link(nc.vector.tensor_scalar(s5f, s5f, 1e-9, None, ALU.add))
            link(nc.vector.reciprocal(s5f, s5f))
            link(nc.vector.tensor_tensor(s5a, s5a, s5f, ALU.mult))
            link(nc.vector.tensor_tensor(s5b, s5b, s5f, ALU.mult))
            nc.vector.tensor_tensor(sel5, ch(T1, 2), ch(T1, 3), ALU.add).then_inc(S("sel5"), 1)
            dve.wait_ge(*when("counted5", 2))
            link(nc.vector.tensor_copy(tot5, bank[2][:, :]))
            src, dst = tot5, pre5a
            for d in (1, 2, 4, 8, 16):
                w = 16 * d
                nc.vector.tensor_copy(dst[:, 0:w], src[:, 0:w]).then_inc(S("pre5"), 1)
                link(nc.vector.tensor_tensor(dst[:, w:], src[:, w:], src[:, 0:CHUNK - w], ALU.add))
                src, dst = dst, (pre5b if dst is pre5a else pre5a)
                dve.wait_ge(*when("pre5", {1: 1, 2: 2, 4: 3, 8: 4, 16: 5}[d]))
            incl = src
            link(nc.vector.tensor_scalar(nt5, incl[:, CHUNK - 16:], 1.0 / SLOTS,
                                         (SLOTS - 1) / SLOTS - 0.5 + 0.5 / SLOTS, ALU.mult, ALU.add))
            link(nc.vector.tensor_scalar(nt5, nt5, 2.0 ** 23, None, ALU.add))
            link(nc.vector.tensor_scalar(nt5, nt5, -2.0 ** 23, None, ALU.add))
            src, dst = nt5, end5
            for d in (1, 2, 4):
                s3_, d3_ = (v.rearrange("p (h e) -> p h e", e=E) for v in (src, dst))
                link(nc.vector.tensor_copy(d3_[:, :, 0:d], s3_[:, :, 0:d]))
                link(nc.vector.tensor_tensor(d3_[:, :, d:], s3_[:, :, d:], s3_[:, :, 0:E - d], ALU.add))
                src, dst = dst, (end5b if dst is end5 else end5)
            ends = src
            link(nc.vector.tensor_tensor(start5, ends, nt5, ALU.subtract))
            link(nc.vector.tensor_tensor(incl, incl, tot5, ALU.subtract))
            link(nc.vector.tensor_tensor(pos5, incl, bank[1][:, :], ALU.add))
            pos5v = pos5.rearrange("p (j g) -> p j g", g=16)
            link(nc.vector.scalar_tensor_tensor(pos5v, start5.unsqueeze(1).broadcast_to([P, TILES, 16]),
                                                float(SLOTS), pos5v, ALU.mult, ALU.add))
            for k, one in enumerate((ch(T1, 2), ch(T1, 3))):
                link(nc.vector.tensor_tensor(prod5, one, pos5, ALU.mult))
                link(nc.vector.tensor_reduce(slot5[:, 64 * k:64 * k + 64],
                                             prod5.rearrange("p (n e) -> p n e", e=E), AX, ALU.add))
                nc.vector.tensor_copy(index[:, k, :], slot5[:, 64 * k:64 * k + 64]).then_inc(S("index5"), 1)
            c5 = cmp5.rearrange("p (h t e) -> p h t e", h=2, e=E)
            for h in range(2):
                link(nc.vector.tensor_tensor(
                    c5[:, h], mats[0:1, M["iota"], 0:NT].unsqueeze(2).broadcast_to([1, NT, E]),
                    ends[0:1, E * h:E * h + E].unsqueeze(1).broadcast_to([1, NT, E]), ALU.is_ge))
            link(nc.vector.tensor_reduce(exp5, cmp5.rearrange("p (t e) -> p t e", e=E), AX, ALU.add))
            link(nc.vector.tensor_scalar(exp5, exp5, float(E - 1), None, ALU.min))
            nc.vector.tensor_copy(expert[:, :, :].rearrange("p h t -> p (h t)"), exp5).then_inc(S("expert5"), 1)
            for c in range(NCH):
                dve.wait_ge(*when("rows5_high", c + 1))
                r = rows5v[:, 4 * c:4 * c + 4]
                nc.vector.tensor_tensor(r[:, :, :, C:], bank[3 + c % 4][:, :].rearrange("p (j h c) -> p j h c", h=2, c=C),
                                        r[:, :, :, 0:C], ALU.subtract).then_inc(S("rows5_low"), 1)

            def tile_vector(b, s):
                t = 3 * b + s
                for k in range(NHB):
                    n, q = t * NHB + k, k % 3
                    dve.wait_ge(*when("silu5", n + 1))
                    if later(n, 3):
                        dve.wait_ge(*when("low5", n - 2))
                    nc.vector.tensor_tensor(H5[q], bank[q][0:HB, SLOTS:], S5[q], ALU.mult).then_inc(S("hid5"), 1)
                    if later(n, 1):
                        low5(n - 1, (k - 1) % 3)
                    if k == 5 and later(t, 1):
                        sum5(t - 1, (s - 1) % 3)

            def low5(n, q):
                dve.wait_ge(*when("high5", n + 1))
                if later(n, 3):
                    dve.wait_ge(*when("down5", n - 2))
                nc.vector.tensor_tensor(LO5[q], H5[q], HI5[q], ALU.subtract).then_inc(S("low5"), 1)

            def sum5(t, s):
                dve.wait_ge(*when("y5_high", t + 1))
                y = bank[3 + s][:, 0:256].rearrange("p (i v c) -> p i v c", v=2, c=C)
                nc.vector.tensor_tensor(Y5[s], Y5[s], y[:, :, 1, :], ALU.add).then_inc(S("y5"), 1)

            steps3(dve, tile_vector)
            last = 2 * NT * NHB - 1
            low5(last, (NHB - 1) % 3)
            sum5(2 * NT - 1, 2)
            dve.wait_ge(*when("xtok", NCH))
            for h in range(2):
                for c in range(NCH):
                    n = h * NCH + c
                    dve.wait_ge(*when(f"gathered_{h}_{c}", 16 * 8))
                    g = G5[h][:, 4 * c:4 * c + 4]
                    for k, gate in enumerate((s5a, s5b)):
                        gk = gate.rearrange("p (j h) -> p j h", h=2)[:, 4 * c:4 * c + 4, h]
                        nc.vector.tensor_tensor(M5[:, :, k, :], g[:, :, k, :], gk.unsqueeze(2).broadcast_to([P, 4, C]),
                                                ALU.mult).then_inc(S("mix5"), 1)
                    dve.wait_ge(*when("mix5", 2 * n + 2))
                    link(nc.vector.tensor_tensor(M5[:, :, 0, :], M5[:, :, 0, :], M5[:, :, 1, :], ALU.add))
                    xv = xtok[:, 4 * c:4 * c + 4, h, :]
                    nc.vector.tensor_tensor(xv, xv, M5[:, :, 0, :], ALU.add).then_inc(S("mixed5"), 1)
                    dve.wait_ge(*when("mixed5", n + 1))

        @block.scalar
        def _(act):
            act.preload_act_table_set("natural_log_exp_and_others")
            act.wait_ge(*when("loaded_vecs", 16))
            for c in range(2 * NCH):
                act.wait_ge(*when("bias_hid", c + 1))
                nc.scalar.activation(ch(T34, c), bank[c % NCH][:, :], ACT.Relu, bias=vec("cb1")) \
                    .then_inc(S("bias_relu"), 1)
            act.wait_ge(*when("bias_z", 1))
            nc.scalar.activation(ch(T3, 0), bank[0][:, :], ACT.Exp, scale=-1.0).then_inc(S("bias_exp"), 1)
            act.wait_ge(*when("lsc", 1))
            nc.scalar.activation(qscale, lsc, ACT.Exp).then_inc(S("qscale"), 1)
            gn_scalar(act, "g0")
            for t, T in (("q", T1), ("k", T2)):
                for c in range(NCH):
                    act.wait_ge(*when(t + "_biased", c + 1))
                    if t == "k":
                        act.wait_ge(*when("q_norm", c + 1))
                    nc.scalar.activation(ch(T3, c), ch(T, c), ACT.Square).then_inc(S(t + "_sq"), 1)
                for c in range(NCH):
                    act.wait_ge(*when(t + "_clip", c + 1))
                    nc.scalar.activation(ch(T3, c), ch(T3, c), ACT.Ln).then_inc(S(t + "_len"), 1)
                    act.wait_ge(*when(t + "_len", c + 1))
                    nc.scalar.activation(ch(T3, c), ch(T3, c), ACT.Exp, scale=-0.5, bias=vec("ln10")) \
                        .then_inc(S(t + "_rlen"), 1)

            def exp_and_copies(k, w):
                n, s = at(k, 0), w % 2
                if n is not None:
                    act.wait_ge(*when("l0_shifted", n + 1))
                    reused(act, "l0_turned", n)
                    nc.scalar.activation(PR[s], SC[s], ACT.Exp).then_inc(S("l0_exp"), 1)
                n, s = at(k, 1), (w + 1) % 2
                if n is not None:
                    act.wait_ge(*when("l0_turned", n + 1))
                    reused(act, "l0_pv", n)
                    nc.scalar.activation(PT[s], bank[2 + s][:, :], ACT.Copy).then_inc(S("l0_pt"), 1)
                n = at(k, 3)
                if n is not None:
                    act.wait_ge(*when("l0_ot", n + 1))
                    nc.scalar.activation(T3[:, bass.ds(n * WT, WT)], bank[6 + s][:, 0:WT], ACT.Identity,
                                         bias=vec("bv0")).then_inc(S("l0_o"), 1)

            act.wait_ge(*when("k_norm", NCH))
            steps(act, exp_and_copies, 3)
            if stop == 0:
                return
            gn_scalar(act, "g1")
            nc.scalar.activation(bnv[:, 1:2], vec("va1"), ACT.Ln, bias=vec("eps3")).then_inc(S("bn_sd"), 1)
            act.wait_ge(*when("bn_sd", 1))
            nc.scalar.activation(bnv[:, 2:3], bnv[:, 1:2], ACT.Exp, scale=-0.5).then_inc(S("bn_rs"), 1)
            act.wait_ge(*when("bn_v", 3))
            for c in range(NCH):
                act.wait_ge(*when("r_proj", c + 1))
                nc.scalar.activation(ch(T1, c, 0, 32), bank[c][0:32, :], ACT.Relu, bias=bnv[0:32, 5:6],
                                     scale=bnv[0:32, 3:4]).then_inc(S("r_ready"), 1)
            act.wait_ge(*when("pad_zero", 1))
            for c in range(NCH):
                act.wait_ge(*when("xi_proj", c + 1))
                nc.scalar.activation(PAD[:, 2 * c:2 * c + 2, 1:1 + HH, 1:1 + WW],
                                     bank[c][:, :].rearrange("p (b r c) -> p b r c", r=HH, c=WW),
                                     ACT.Identity, bias=vec("bi1")).then_inc(S("xi_kept"), 1)
            if stop == 1:
                return
            ln_scalar(act, "a2", "eps5")
            for c in range(NCH):
                act.wait_ge(*when("k2_biased", c + 1))
                nc.scalar.activation(ch(T1, c), ch(T1, c), ACT.Square).then_inc(S("k2_sq"), 1)
            for c in range(NCH):
                act.wait_ge(*when("k2_ready", c + 1))
                nc.scalar.activation(ch(T2, c), ch(T1, c), ACT.Square).then_inc(S("k2_fourth"), 1)
            act.wait_ge(*when("k2_clip", 1))
            nc.scalar.activation(kln, knorm, ACT.Ln).then_inc(S("k2_ln"), 1)
            act.wait_ge(*when("k2_ln", 1))
            nc.scalar.activation(krs, kln, ACT.Exp, scale=-0.5, bias=vec("ln16")).then_inc(S("k2_rs"), 1)
            act.wait_ge(*when("kv2", HALF))
            act.wait_ge(*when("k2_norm", 1))
            act.wait_ge(*when("w2_kept", 5))

            def q_rs(c):
                act.wait_ge(*when("q2_clip", c + 1))
                nc.scalar.activation(ch(T1, c), ch(T1, c), ACT.Ln, bias=vec("tiny")).then_inc(S("q2_ln"), 1)
                act.wait_ge(*when("q2_ln", c + 1))
                nc.scalar.activation(ch(T1, c), ch(T1, c), ACT.Exp, scale=-0.5, bias=vec("ln20")) \
                    .then_inc(S("q2_rs"), 1)

            for c in range(NCH):
                act.wait_ge(*when("q2_proj", c + 1))
                nc.scalar.activation(ch(T2, c), bank[c % 4][:, :], ACT.Square, bias=bqc).then_inc(S("q2_sq"), 1)
                act.wait_ge(*when("q2_sq", c + 1))
                nc.scalar.activation(ch(T4, c), ch(T2, c), ACT.Square).then_inc(S("q2_fourth"), 1)
                act.wait_ge(*when("q2_s1", c + 1))
                nc.scalar.activation(ch(T1, c), bank[c % 4][:, :], ACT.Square, scale=1e-12 * 2.0 ** 20,
                                     bias=vec("guard")).then_inc(S("q2_guard"), 1)
                if c >= 1:
                    q_rs(c - 1)
            q_rs(NCH - 1)
            for c in range(NCH):
                act.wait_ge(*when("t2", c + 1))
                nc.scalar.activation(ch(T1, c), bank[c][:, :], ACT.Identity, bias=vec("bv2")) \
                    .then_inc(S("t2_kept"), 1)
            if stop == 2:
                return
            ln_scalar(act, "a3", "eps5")
            for t in ("sm1", "sm2"):
                act.wait_ge(*when(t + "_in", 1))
                nc.scalar.activation(lg, lg, ACT.Exp).then_inc(S(t + "_exp"), 1)
            act.wait_ge(*when("sm3_in", 1))
            nc.scalar.activation(s2b, s2b, ACT.Exp).then_inc(S("sm3_exp"), 1)

            def gelu(k, p):
                b = at2(k, 0)
                if b is None:
                    return
                for e in range(E):
                    u = b * E + e
                    act.wait_ge(*when("up3", u + 1))
                    if not isinstance(u, int) or u >= 4:
                        act.wait_ge(*when("down3", u - 3))
                    nc.scalar.activation(HID[e % 4], bank[e % 4][:, :], ACT.Gelu, bias=vec(f"b1_{e}")) \
                        .then_inc(S("hid3"), 1)

            steps2(act, gelu, 0)
            ln_scalar(act, "l3", "eps5")
            if stop == 3:
                return
            ln_scalar(act, "a4", "eps5")
            rms_scalar(act, "n4", A, "a4", "eps6")
            for t, T in (("k", T3), ("q", T2)):
                for c in range(NCH):
                    act.wait_ge(*when(t + "4_neg", c + 1))
                    nc.scalar.activation(ch(T, c), ch(T, c), ACT.Exp).then_inc(S(t + "4_exp"), 1)
            for c in range(NCH):
                act.wait_ge(*when("den4", c + 1))
                nc.scalar.activation(ch(T3, c), bank[c % 4][:, :], ACT.Ln, bias=vec("eps6")).then_inc(S("z4_ln"), 1)
                act.wait_ge(*when("z4_ln", c + 1))
                nc.scalar.activation(ch(T3, c), ch(T3, c), ACT.Exp, scale=-1.0).then_inc(S("z4"), 1)
            rms_scalar(act, "m4", T4, "h4", "eps6")
            if stop == 4:
                return
            ln_scalar(act, "a5", "eps5")
            act.wait_ge(*when("sm4_in", 1))
            nc.scalar.activation(ch(T1, 0), ch(T1, 0), ACT.Exp).then_inc(S("sm4_exp"), 1)
            for c in range(NCH):
                act.wait_ge(*when("x_turned", c + 1))
                nc.scalar.activation(ch(T4, c), bank[3 + c % 4][:, :], ACT.Copy).then_inc(S("xtok"), 1)
            for c in range(NCH):
                act.wait_ge(*when("a_turned", c + 1))
                nc.scalar.activation(rows5v[:, 4 * c:4 * c + 4, :, 0:C],
                                     bank[3 + c % 4][:, :].rearrange("p (j h c) -> p j h c", h=2, c=C), ACT.Copy) \
                    .then_inc(S("rows5_high"), 1)

            def turned_x(t, s):
                act.wait_ge(*when("turned5", t + 1))
                nc.scalar.activation(XT[s], bank[6][:, 0:SLOTS], ACT.Copy).then_inc(S("xt5"), 1)

            def high5(n, q):
                act.wait_ge(*when("hid5", n + 1))
                if later(n, 3):
                    act.wait_ge(*when("down5", n - 2))
                nc.scalar.activation(HI5[q], H5[q], ACT.Copy).then_inc(S("high5"), 1)

            def result5(t, s, b):
                act.wait_ge(*when("down5", NHB * t + NHB))
                if later(t, 3):
                    act.wait_ge(*when(f"stored_y_{s}", 16 * b))
                y = bank[3 + s][:, 0:256].rearrange("p (i v c) -> p i v c", v=2, c=C)
                nc.scalar.activation(Y5[s], y[:, :, 0, :], ACT.Copy).then_inc(S("y5_high"), 1)

            def tile_scalar(b, s, final=False):
                t = 3 * b + s
                for k in range(NHB):
                    n, q = t * NHB + k, k % 3
                    act.wait_ge(*when("up5", n + 1))
                    if later(n, 3):
                        act.wait_ge(*when("hid5", n - 2))
                    nc.scalar.activation(S5[q], bank[q][0:HB, 0:SLOTS], ACT.Silu).then_inc(S("silu5"), 1)
                    if later(n, 1):
                        high5(n - 1, (k - 1) % 3)
                    if k == 3 and not final:
                        turned_x(t + 1, (s + 1) % 3)
                    if k == 4 and later(t, 1):
                        result5(t - 1, (s - 1) % 3, b - 1 if s == 0 else b)

            turned_x(0, 0)
            for t in range(3):
                tile_scalar(0, t)
            with act.Fori(1, 2 * NT // 3 - 1) as b:
                for r in range(3):
                    tile_scalar(b, r)
            for t in range(2 * NT - 3, 2 * NT):
                tile_scalar(t // 3, t % 3, final=(t == 2 * NT - 1))
            high5(2 * NT * NHB - 1, (NHB - 1) % 3)
            result5(2 * NT - 1, 2, 2 * NT // 3 - 1)

        @block.tensor
        def _(pe):
            pe.wait_ge(*when("loaded_mats", 16))
            pe.wait_ge(*when("loaded_vecs", 16))
            pe.wait_ge(*when("loaded_feats", 32))
            for c in range(2 * NCH):
                if c >= NCH:
                    pe.wait_ge(*when("bias_relu", c - NCH + 1))
                keys = T2[0:2, c * 4 * WT:(c + 1) * 4 * WT].rearrange("p (k q) -> p k q", k=4)
                nc.tensor.matmul(bank[c % NCH][:, :], cw1, keys.unsqueeze(2).broadcast_to([2, 4, 2, WT]),
                                 start=True, stop=True).then_inc(S("bias_hid"), 1)
            pe.wait_ge(*when("bias_relu", 2 * NCH))
            for key in range(WT):
                mm = nc.tensor.matmul(bank[0][:, key * HEADS:(key + 1) * HEADS],
                                      T34[:, key * 128:(key + 1) * 128],
                                      vec("w2c0", HEADS), start=True, stop=True)
            mm.then_inc(S("bias_z"), 1)
            pe.wait_ge(*when("bias_exp", 1))
            gn_tensor(pe, "g0")
            for t in ("q", "k"):
                for c in range(NCH):
                    if t == "q":
                        pe.wait_ge(*when("g0_norm", 2 * (c + 1)))
                        if c == 0:
                            pe.wait_ge(*when("g0_grpc", 1))
                    else:
                        pe.wait_ge(*when("q_clip", c + 1))
                    nc.tensor.matmul(bank[c][:, :], mat(f"w{t}0"), ch(A, c), start=True, stop=True) \
                        .then_inc(S(t + "_proj"), 1)
                for c in range(NCH):
                    pe.wait_ge(*when(t + "_sq", c + 1))
                    nc.tensor.matmul(bank[c][:, :], mat("head"), ch(T3, c), start=True, stop=True) \
                        .then_inc(S(t + "_ssq"), 1)
            for g in range(PAIRS // 4):
                if g < NCH:
                    pe.wait_ge(*when("k_clip", g + 1))
                else:
                    pe.wait_ge(*when("v_ready", 2 * (g - NCH + 1)))
                for i in range(4):
                    n = 4 * g + i
                    for x in range(2):
                        mm = nc.tensor.matmul(
                            bank[g % NCH][64 * x:64 * x + 64, i * 64:(i + 1) * 64], A[:, n * WT:(n + 1) * WT],
                            mat("wv0").rearrange("p (g x d) -> p g x d", x=2, d=DH)[:, :, x, :],
                            start=True, stop=True)
                mm.then_inc(S("v_proj"), 1)

            def attention(k, w):
                n, s = at(k, 0), w % 2
                if n is not None:
                    pe.wait_ge(*when("l0_staged", (n + 1) * 2))
                    reused(pe, "l0_biased", n)
                    nc.tensor.matmul(bank[s][:, :], QB[s], KX[s], start=True, stop=True).then_inc(S("l0_scores"), 1)
                n, s = at(k, 1), (w + 1) % 2
                if n is not None:
                    pe.wait_ge(*when("l0_exp", n + 1))
                    reused(pe, "l0_pt", n)
                    for g in range(HP):
                        mm = nc.tensor.transpose(bank[2 + s][:, g * 128:(g + 1) * 128],
                                                 PR[s][:, g * 128:(g + 1) * 128], mat("ident"))
                    mm.then_inc(S("l0_turned"), 1)
                n, s = at(k, 2), w % 2
                if n is not None:
                    pe.wait_ge(*when("l0_pt", n + 1))
                    reused(pe, "l0_obd", n)
                    for g in range(HP):
                        mm = nc.tensor.matmul(bank[4 + s][:, g * VW:(g + 1) * VW], PT[s][:, g * 128:(g + 1) * 128],
                                              VX[:, bass.ds(n * HP + g, 1), :].rearrange("p a v -> p (a v)"),
                                              start=True, stop=True)
                    mm.then_inc(S("l0_pv"), 1)
                n, s = at(k, 3), (w + 1) % 2
                if n is not None:
                    pe.wait_ge(*when("l0_obd", n + 1))
                    reused(pe, "l0_o", n)
                    nc.tensor.matmul(bank[6 + s][:, 0:WT], OB[s], ident2, start=True, stop=True) \
                        .then_inc(S("l0_ot"), 1)

            pe.wait_ge(*when("v_ready", PAIRS // 2))
            pe.wait_ge(*when("vx_ones", 2))
            steps(pe, attention, 3)
            for c in range(NCH):
                pe.wait_ge(*when("l0_o", PAIRS))
                nc.tensor.matmul(bank[c][:, :], mat("wo0"), ch(T3, c), start=True, stop=True) \
                    .then_inc(S("l0_wo"), 1)
            if stop == 0:
                return
            gn_tensor(pe, "g1")
            for c in range(NCH):
                pe.wait_ge(*when("g1_norm", 2 * (c + 1)))
                nc.tensor.matmul(bank[c][0:32, :], mat("wr1")[:, 0:32], ch(A, c), start=True, stop=True) \
                    .then_inc(S("r_proj"), 1)
            for c in range(NCH):
                pe.wait_ge(*when("r_ready", c + 1))
                nc.tensor.matmul(bank[c][:, :], mat("wi1"), ch(A, c), start=True, stop=True) \
                    .then_inc(S("xi_proj"), 1)
            pe.wait_ge(*when("xi_kept", NCH))
            pe.wait_ge(*when("loaded_taps", 32))
            pe.wait_ge(*when("r_one", 1))

            def tap_sum(k):
                c, t = k // KK, k % KK
                pe.wait_ge(*when("tap_prod", k + 1))
                if t == 0 and c >= 2:
                    pe.wait_ge(*when("x2_ready", c - 1))
                nc.tensor.matmul(bank[4 + c % 2][:, :], taps[:, t, :], PROD[k % 4], start=(t == 0),
                                 stop=(t == KK - 1)).then_inc(S("tap_summed"), 1)

            for k in range(NCH * KK):
                if k >= 4:
                    pe.wait_ge(*when("tap_prod", k - 3))
                nc.tensor.matmul(bank[k % 4][:, :], wexp[:, k % KK, :], ch(T1, k // KK, 0, 33),
                                 start=True, stop=True).then_inc(S("tap_w"), 1)
                if k >= 2:
                    tap_sum(k - 2)
            tap_sum(NCH * KK - 2)
            tap_sum(NCH * KK - 1)
            if stop == 1:
                return
            ln_tensor(pe, "a2", X, "x2_ready", lambda c: c + 1, left=NCH)
            pe.wait_ge(*when("a2", NCH))
            for i, (left, right) in enumerate(((mat("wq2t"), mat("centre")), (mat("wk2t"), mat("centre")),
                                               (vec("bk2").broadcast_to([P, 128]), mat("centre")),
                                               (vec("bv2").broadcast_to([P, 128]), mat("ident")))):
                nc.tensor.matmul(bank[i][:, 0:128], left, right, start=True, stop=True).then_inc(S("w2_centred"), 1)
            nc.tensor.matmul(bank[4][:, 0:1], mat("centre"), vec("bq2"), start=True, stop=True) \
                .then_inc(S("w2_centred"), 1)
            pe.wait_ge(*when("w2_kept", 5))
            for c in range(NCH):
                for j in range(4):
                    mm = nc.tensor.matmul(bank[c][:, j * 128:(j + 1) * 128],
                                          A[:, (4 * c + j) * 128:(4 * c + j + 1) * 128], mat("wk2t"),
                                          start=True, stop=True)
                mm.then_inc(S("k2_proj"), 1)
            for c in range(NCH):
                pe.wait_ge(*when("k2_biased", c + 1))
                for j in range(4):
                    mm = nc.tensor.matmul(bank[c][:, j * 128:(j + 1) * 128],
                                          A[:, (4 * c + j) * 128:(4 * c + j + 1) * 128], mat("wv2"),
                                          start=True, stop=True)
                mm.then_inc(S("v2_proj"), 1)
            pe.wait_ge(*when("v2_kept", NCH))
            for b in range(HALF):
                pe.wait_ge(*when("k2_fourth", b // 2 + 1))
                for j in range(2):
                    mm = nc.tensor.matmul(bank[4][:, b:b + 1], T2[:, (2 * b + j) * 128:(2 * b + j + 1) * 128],
                                          vec("one"), start=(j == 0), stop=(j == 1))
            mm.then_inc(S("k2_norm"), 1)
            for b in range(HALF):
                pe.wait_ge(*when("k2_ready", b // 2 + 1))
                for j in range(2):
                    tile = slice((2 * b + j) * 128, (2 * b + j + 1) * 128)
                    mm = nc.tensor.matmul(bank[b // 4][:, (b % 4) * 128:(b % 4 + 1) * 128], T1[:, tile], T3[:, tile],
                                          start=(j == 0), stop=(j == 1))
                mm.then_inc(S("kv2"), 1)

            def q_sums(c):
                pe.wait_ge(*when("q2_sq", c + 1))
                nc.tensor.matmul(bank[c % 4][:, :], mat("sum"), ch(T2, c), start=True, stop=True) \
                    .then_inc(S("q2_s1"), 1)
                pe.wait_ge(*when("q2_fourth", c + 1))
                if c >= 4:
                    pe.wait_ge(*when("q2_clip", c - 3))
                nc.tensor.matmul(bank[4 + c % 4][:, :], mat("sum"), ch(T4, c), start=True, stop=True) \
                    .then_inc(S("q2_s2"), 1)

            pe.wait_ge(*when("kv2_kept", HALF))
            pe.wait_ge(*when("k2_clip", 1))
            for c in range(NCH):
                if c >= 4:
                    pe.wait_ge(*when("q2_guard", c - 3))
                nc.tensor.matmul(bank[c % 4][:, :], mat("wq2t"), ch(A, c), start=True, stop=True) \
                    .then_inc(S("q2_proj"), 1)
                if c >= 1:
                    q_sums(c - 1)
            q_sums(NCH - 1)
            pe.wait_ge(*when("q2_clip", NCH))
            for c in range(NCH):
                pe.wait_ge(*when("q2_ready", c + 1))
                for i in range(2):
                    b = 2 * c + i
                    nc.tensor.matmul(bank[c][:, i * N:(i + 1) * N], mat("wv2"), A[:, b * N:(b + 1) * N],
                                     start=True, stop=False)
                    mm = nc.tensor.matmul(bank[c][:, i * N:(i + 1) * N], KVS[:, b, :], T2[:, b * N:(b + 1) * N],
                                          start=False, stop=True)
                mm.then_inc(S("t2"), 1)
            for c in range(NCH):
                pe.wait_ge(*when("t2_kept", c + 1))
                nc.tensor.matmul(bank[c][:, :], mat("wo2"), ch(T1, c), start=True, stop=True) \
                    .then_inc(S("o2_proj"), 1)
            if stop == 2:
                return
            ln_tensor(pe, "a3", X, "x3_ready", lambda c: c + 1)
            pe.wait_ge(*when("r3_mean", NCH))
            pe.wait_ge(*when("a3", NCH))
            nc.tensor.matmul(bank[0][0:HALF, 0:16], xmean, mat("rt3")[:, 0:16], start=True, stop=True) \
                .then_inc(S("r3_logits"), 1)
            pe.wait_ge(*when("r3_rw", 1))
            nc.tensor.matmul(bank[1][0:HALF, 0:16], vec("one")[0:HALF, :].broadcast_to([HALF, HALF]), lc,
                             start=True, stop=True).then_inc(S("r3_load"), 1)
            pe.wait_ge(*when("r3_diag", 1))
            nc.tensor.matmul(bank[2][:, 0:256], vec("one")[0:HALF, :].broadcast_to([HALF, 128]), gdiag,
                             start=True, stop=True).then_inc(S("r3_gates"), 1)
            pe.wait_ge(*when("gates2", 1))
            pe.wait_ge(*when("loaded_l2", 32))

            def down3(u, e, p):
                pe.wait_ge(*when("hid3", u + 1))
                for h in range(2):
                    mm = nc.tensor.matmul(bank[4 + p][64 * h:64 * h + 64, 0:N],
                                          W2G[p][:, 512 * h + C * e:512 * h + C * e + C],
                                          HID[e % 4][:, N * h:N * h + N], start=(e == 0), stop=(e == E - 1),
                                          skip_group_check=True)
                mm.then_inc(S("down3"), 1)

            def experts(k, p):
                b, done = at2(k, 0), at2(k, 1)
                for e in range(E):
                    if b is not None:
                        u = b * E + e
                        if not isinstance(u, int) or u >= 4:
                            pe.wait_ge(*when("hid3", u - 3))
                        for h in range(2):
                            mm = nc.tensor.matmul(bank[e % 4][:, N * h:N * h + N], up2[:, h, e, :],
                                                  A[:, bass.ds(b * N, N)], start=True, stop=True)
                        mm.then_inc(S("up3"), 1)
                    if e < 2:
                        if done is not None:
                            down3(done * E + e + E - 2, e + E - 2, (p + 1) % 2)
                    elif b is not None:
                        if e == 2:
                            pe.wait_ge(*when("w2_gated", 2 * (b + 1)))
                            if not isinstance(b, int) or b >= 2:
                                pe.wait_ge(*when("y3_kept", b - 1))
                        down3(b * E + e - 2, e - 2, p)

            steps2(pe, experts, 1)
            ln_tensor(pe, "l3", T1, "y3_kept", lambda c: 2 * (c + 1), left=HALF)
            if stop == 3:
                return
            ln_tensor(pe, "a4", X, "x4_ready", lambda c: c + 1)
            pe.wait_ge(*when("a4", NCH))
            rms_tensor(pe, "n4")
            for c in range(NCH):
                pe.wait_ge(*when("n4", c + 1))
                for j in range(4):
                    mm = nc.tensor.matmul(bank[c][:, j * 128:(j + 1) * 128],
                                          T1[:, (4 * c + j) * 128:(4 * c + j + 1) * 128], mat("wk4"),
                                          start=True, stop=True)
                mm.then_inc(S("k4_proj"), 1)
            for c in range(NCH):
                pe.wait_ge(*when("k4_elu", c + 1))
                for j in range(4):
                    mm = nc.tensor.matmul(bank[c][:, j * 128:(j + 1) * 128],
                                          T1[:, (4 * c + j) * 128:(4 * c + j + 1) * 128], mat("wv4"),
                                          start=True, stop=True)
                mm.then_inc(S("v4_proj"), 1)
            pe.wait_ge(*when("v4_kept", NCH))
            for b in range(HALF):
                for j in range(2):
                    tile = slice((2 * b + j) * 128, (2 * b + j + 1) * 128)
                    mm = nc.tensor.matmul(bank[b // 4][:, (b % 4) * 128:(b % 4 + 1) * 128], T3[:, tile], T4[:, tile],
                                          start=(j == 0), stop=(j == 1))
                mm.then_inc(S("kv4"), 1)
            for b in range(HALF):
                for j in range(2):
                    mm = nc.tensor.matmul(bank[4][:, b:b + 1], T3[:, (2 * b + j) * 128:(2 * b + j + 1) * 128],
                                          vec("one"), start=(j == 0), stop=(j == 1))
            mm.then_inc(S("ks4"), 1)
            pe.wait_ge(*when("kv4_kept", 4))
            pe.wait_ge(*when("ks4_kept", 1))
            for c in range(NCH):
                nc.tensor.matmul(bank[c][:, :], mat("wq4"), ch(T1, c), start=True, stop=True) \
                    .then_inc(S("q4_proj"), 1)
            pe.wait_ge(*when("kv4_kept", 8))
            pe.wait_ge(*when("q4_elu", NCH))
            for c in range(NCH):
                if c >= 4:
                    pe.wait_ge(*when("z4", c - 3))
                    pe.wait_ge(*when("o4", c - 3))
                for t, W, k in (("den4", KSS, 0), ("num4", KVS, 4)):
                    for i in range(2):
                        b = 2 * c + i
                        mm = nc.tensor.matmul(bank[k + c % 4][:, i * N:(i + 1) * N], W[:, b, :],
                                              T2[:, b * N:(b + 1) * N], start=True, stop=True)
                    mm.then_inc(S(t), 1)
            pe.wait_ge(*when("o4", NCH))
            for c in range(NCH):
                nc.tensor.matmul(bank[c][:, :], mat("wo4"), ch(T1, c), start=True, stop=True) \
                    .then_inc(S("o4_proj"), 1)
            rms_tensor(pe, "m4")
            if stop == 4:
                return
            ln_tensor(pe, "a5", X, "x5_ready", lambda c: c + 1)
            pe.wait_ge(*when("a5", NCH))
            for j in range(TILES):
                mm = nc.tensor.matmul(bank[0][:, 16 * j:16 * j + 16], A[:, j * 128:(j + 1) * 128],
                                      mat("rt5")[:, 0:16], start=True, stop=True)
            mm.then_inc(S("r5_logits"), 1)
            for t, T, free in (("x_turned", X, "xtok"), ("a_turned", A, "rows5_low")):
                for c in range(NCH):
                    if t == "a_turned" and c < 4:
                        pe.wait_ge(*when("xtok", c + 5))
                    elif c >= 4:
                        pe.wait_ge(*when(free, c - 3))
                    for j in range(4):
                        mm = nc.tensor.transpose(bank[3 + c % 4][:, j * 128:(j + 1) * 128],
                                                 T[:, (4 * c + j) * 128:(4 * c + j + 1) * 128], mat("ident"))
                    mm.then_inc(S(t), 1)
                if t == "x_turned":
                    pe.wait_ge(*when("sel5", 1))
                    for i, w in ((1, mat("before")), (2, vec("one").broadcast_to([P, 128]))):
                        nc.tensor.matmul(bank[i][:, :], w, sel5, start=True, stop=True).then_inc(S("counted5"), 1)

            pe.wait_ge(*when("ident16", 1))
            pe.wait_ge(*when("expert5", 1))
            pe.wait_ge(*when("rows5_low", NCH))
            pe.wait_ge(*when("index5", 2))
            pe.wait_ge(*when("ups_split", 2 * 3 * E))

            def turn5(b, s):
                t = 3 * b + s
                pe.wait_ge(*when(f"loaded_xs_{s}", 16 * (b + 1)))
                if later(t, 1):
                    pe.wait_ge(*when("xt5", t))
                for i in range(2):
                    mm = nc.tensor.matmul(bank[6][:, i * 128:(i + 1) * 128], XS[s][:, i, :], ident16[:, :],
                                          start=True, stop=True)
                mm.then_inc(S("turned5"), 1)

            def down5(n, t, k, s, e):
                pe.wait_ge(*when("low5", n + 1))
                if k == 0 and later(t, 3):
                    pe.wait_ge(*when("y5", t - 2))
                q = k % 3
                w = e * (NHB * 2 * C) + k * 2 * C
                for v, H in enumerate((LO5[q], HI5[q])):
                    for i in range(2):
                        mm = nc.tensor.matmul(bank[3 + s][:, i * 128:(i + 1) * 128], H[:, i * 128:(i + 1) * 128],
                                              downs[:, bass.ds(w, 2 * C)], start=(k == 0 and v == 0 and i == 0),
                                              stop=(k == NHB - 1 and v == 1 and i == 1), skip_group_check=True)
                mm.then_inc(S("down5"), 1)

            table = expert[:, :, :].rearrange("p h t -> p (h t)")

            def expert_of(t):
                return nc.tensor.value_load(table[0:1, bass.ds(t, 1)], min_val=0, max_val=E - 1)

            def tile_tensor(b, s, e, final=False, before=None):
                t = 3 * b + s
                pe.wait_ge(*when("xt5", t + 1))
                for k in range(NHB):
                    n, q = t * NHB + k, k % 3
                    if later(n, 3):
                        pe.wait_ge(*when("hid5", n - 2))
                    for v in range(4):
                        mm = nc.tensor.matmul(bank[q][0:HB, SLOTS * (v // 2):SLOTS * (v // 2) + SLOTS],
                                              big16[:, bass.ds(e * (4 * HID3) + (v * HID3 + k * HB), HB)], XT[s],
                                              start=(v % 2 == 0), stop=(v % 2 == 1))
                    mm.then_inc(S("up5"), 1)
                    if k >= 3:
                        down5(n - 3, t, k - 3, s, e)
                    elif before is not None:
                        down5(n - 3, t - 1, k + 3, (s - 1) % 3, before)
                    if k == 2 and not final:
                        turn5(b + 1 if s == 2 else b, (s + 1) % 3)
                    if k == 4 and not final:
                        after = expert_of(t + 1)
                return None if final else after

            def three_tiles(b, before, e, final=False):
                for r in range(3):
                    before, e = e, tile_tensor(b, r, e, final and r == 2, before)
                return before, e

            turn5(0, 0)
            carried = [pe.alloc_register(name) for name in ("expert_before", "expert_next")]
            for register, value in zip(carried, three_tiles(0, None, expert_of(0))):
                pe.reg_mov(register, value)
            with pe.Fori(1, 2 * NT // 3 - 1) as b:
                before, e = (pe.snap(register, min_val=0, max_val=E - 1) for register in carried)
                for register, value in zip(carried, three_tiles(b, before, e)):
                    pe.reg_mov(register, value)
            before, e = (pe.snap(register, min_val=0, max_val=E - 1) for register in carried)
            e, _ = three_tiles(2 * NT // 3 - 1, before, e, True)
            for k in range(3, NHB):
                down5((2 * NT - 1) * NHB + k, 2 * NT - 1, k, 2, e)


def blocks(w):
    a, b = w.shape
    m = np.zeros((128, 128), np.float32)
    m[:a, :b] = w
    m[64:64 + a, b:2 * b] = w
    return m


def constants():
    eye = np.eye(128, dtype=np.float32)
    same = np.kron(np.eye(2), np.ones((64, 64))).astype(np.float32)
    pair = np.kron(np.eye(64), np.ones((2, 2))).astype(np.float32) / 2
    head = np.kron(np.eye(16), np.ones((8, 8))).astype(np.float32)
    stack = np.zeros((128, 128), np.float32)
    stack[:, 0:64] = np.concatenate([np.eye(64)] * 2, 0)
    par = (np.arange(32) // 8) % 2
    stack[:64, 64:96] = par == 0
    stack[64:, 64:96] = par == 1
    mats = {"ident": eye, "mean": same / 64, "centre": eye - same / 64, "pair": pair, "head": head,
            "sum": same, "stack": stack, "before": np.triu(np.ones((128, 128), np.float32), 1),
            "iota": np.tile(np.arange(128, dtype=np.float32), (128, 1))}
    ws = WS
    r = np.arange(-(ws - 1), ws, dtype=np.float32)
    tbl = np.stack(np.meshgrid(r, r, indexing="ij"), axis=-1)
    tbl = tbl / (ws - 1) * 8.0
    tbl = np.sign(tbl) * np.log2(np.abs(tbl) + 1.0) / np.log2(8.0)
    tbl = tbl.reshape(-1, 2).astype(np.float32)
    c = np.stack(np.meshgrid(np.arange(ws), np.arange(ws), indexing="ij")).reshape(2, -1)
    rel = c[:, :, None] - c[:, None, :] + (ws - 1)
    idx = rel[0] * (2 * ws - 1) + rel[1]
    feats = np.ascontiguousarray(tbl[idx.T].reshape(-1, 2).T)
    img = np.zeros((HH, WW), np.int32)
    cnt = 0
    for hs in (slice(0, -ws), slice(-ws, -SS), slice(-SS, None)):
        for wsl in (slice(0, -ws), slice(-ws, -SS), slice(-SS, None)):
            img[hs, wsl] = cnt
            cnt += 1
    mw = img.reshape(HH // ws, ws, WW // ws, ws).transpose(0, 2, 1, 3).reshape(-1, ws * ws)
    mask = np.where(mw[:, None, :] != mw[:, :, None], -100.0, 0.0).astype(np.float32)
    wmask = np.ascontiguousarray(np.concatenate([mask.transpose(1, 0, 2)] * 2, 0))
    taps = np.zeros((128, KK, 128), np.float32)
    m = np.arange(KK * C)
    for h in range(2):
        taps[64 * h + m % C, m // C, 64 * h + m // KK] = 1
    widx = (m // KK // 4) * KK + m % KK
    return mats, feats, wmask, taps, widx


def halves(x):
    return np.ascontiguousarray(x.reshape(2, HALF, N, C).transpose(0, 3, 1, 2).reshape(P, COLS))


_INS = ["xw", "xi", "mats", "vecs", "feats", "cw1", "wmask", "taps", "wexp", "w1l2", "w2l2", "w1l3", "w3l3", "w2l3"]
OUTPUT_NAMES = [("out_0", (P, COLS))]


def kernel(x, **w):
    import concourse.bacc as _bacc
    from concourse.bass_utils import run_bass_kernel_spmd as _run

    w = {k: np.asarray(v) for k, v in w.items()}
    x = np.asarray(x)
    mats, feats, wmask, taps, widx = constants()
    rolled = np.roll(x, (-SS, -SS), axis=(1, 2)).reshape(B, 2, WS, 2, WS, C).transpose(0, 1, 3, 2, 4, 5)
    arr = {"xw": halves(rolled.reshape(B, N, C)), "xi": halves(x.reshape(B, N, C))}
    hp, par, d = np.meshgrid(np.arange(HP), np.arange(2), np.arange(DH), indexing="ij")
    chan = (hp * 16 + par * 8 + d).ravel()
    wv0 = np.zeros((128, 128), np.float32)
    wo0 = np.zeros((128, 128), np.float32)
    bv0 = np.zeros(128, np.float32)
    for h in range(2):
        col = (hp * 32 + h * 16 + par * 8 + d).ravel()
        wv0[64 * h:64 * h + 64, col] = w["L0_conv_Wv"].T[:, chan]
        wo0[col, 64 * h:64 * h + 64] = w["L0_conv_Wo"].T[chan, :]
        bv0[col] = w["L0_conv_bv"][chan]
    qkv2, qkv4 = w["L2_attn_W_qkv"], w["L3_attn_w_qkv"]
    mats |= {"wq0": blocks(w["L0_conv_Wq"].T), "wk0": blocks(w["L0_conv_Wk"].T), "wv0": wv0, "wo0": wo0,
             "wi1": blocks(w["L1_conv_Wi"]), "wr1": blocks(w["L1_conv_Wr"]),
             "wq2t": blocks(qkv2[:, 0:64].T), "wk2t": blocks(qkv2[:, 64:128].T), "wv2": blocks(qkv2[:, 128:192]),
             "wo2": blocks(w["L2_attn_W_out"]), "wq4": blocks(qkv4[:, 0:64]), "wk4": blocks(qkv4[:, 64:128]),
             "wv4": blocks(qkv4[:, 128:192]), "wo4": blocks(w["L3_attn_w_out"]),
             "rt3": blocks(w["L2_ffn_Wr"]), "rt5": blocks(w["L3_ffn_router_w"].T)}
    arr["mats"] = np.ascontiguousarray(np.stack([mats[n] for n in MATS], 1))
    two = lambda v: np.concatenate([v, v])
    padded = lambda v: np.concatenate([v, v, np.zeros(96, np.float32)])
    vecs = {"bq0": two(w["L0_conv_bq"]), "bk0": two(w["L0_conv_bk"]), "bv0": bv0, "bo0": two(w["L0_conv_bo"]),
            "ls0": two(np.repeat(w["L0_conv_logit_scale"].reshape(-1), DH)), "bi1": two(w["L1_conv_bi"]),
            "br1": padded(w["L1_conv_br"]), "ga1": padded(w["L1_conv_gamma"]), "be1": padded(w["L1_conv_beta"]),
            "mu1": padded(w["L1_conv_mean"]), "va1": padded(w["L1_conv_var"]),
            "bq2": two(w["L2_attn_b_qkv"][0:64]), "bk2": two(w["L2_attn_b_qkv"][64:128]),
            "bv2": two(w["L2_attn_b_qkv"][128:192]), "bo2": two(w["L2_attn_b_out"]),
            "ga3": two(w["L2_ffn_gamma"]), "be3": two(w["L2_ffn_beta"]), "n14": two(w["L3_attn_w_norm1"]),
            "bo4": two(w["L3_attn_b_out"]), "n24": two(w["L3_attn_w_norm2"]), "cb1": w["L0_conv_cpb_b1"],
            "eps6": np.full(128, 1e-6), "eps5": np.full(128, 1e-5), "eps3": np.full(128, 1e-3),
            "tiny": np.full(128, 2.0 ** -60), "ln10": np.full(128, 10 * np.log(2)), "ln20": np.full(128, 20 * np.log(2)),
            "ln16": np.full(128, 20 * np.log(2) - np.log(16)), "guard": np.full(128, 1e-19 * 2.0 ** 20),
            "one": np.ones(128), "par0": np.arange(128) < 64, "par1": np.arange(128) >= 64,
            "half0": np.arange(128) < 64, "half1": np.arange(128) >= 64}
    for e in range(E):
        vecs[f"w2c{e}"] = w["L0_conv_cpb_w2"][e]
        vecs[f"b1_{e}"] = w["L2_ffn_b1"][e]
        vecs[f"b2_{e}"] = two(w["L2_ffn_b2"][e])
        vecs[f"rank{e}"] = np.full(128, E - e)
        for h in range(2):
            vecs[f"brr{h * E + e}"] = np.broadcast_to(w["L2_ffn_br"][e], (128,))
    arr["vecs"] = np.ascontiguousarray(np.stack([np.asarray(vecs[n], np.float32) for n in VECS], 1))
    arr["feats"], arr["wmask"], arr["taps"] = feats, wmask, taps
    arr["cw1"] = np.ascontiguousarray(w["L0_conv_cpb_w1"].T)
    wexp = np.zeros((33, KK, 128), np.float32)
    for h in range(2):
        for t in range(KK):
            wexp[16 * h:16 * h + 16, t, 64 * h:64 * h + 64] = w["L1_conv_Ws"][:, widx[64 * t:64 * t + 64]]
            wexp[32, t, 64 * h:64 * h + 64] = w["L1_conv_bs"][widx[64 * t:64 * t + 64]]
    arr["wexp"] = wexp
    up2 = np.zeros((128, 2, E, FH), np.float32)
    for h in range(2):
        up2[64 * h:64 * h + 64, h] = w["L2_ffn_W1"].transpose(1, 0, 2)
    arr["w1l2"] = up2
    arr["w2l2"] = np.ascontiguousarray(w["L2_ffn_W2"].transpose(1, 0, 2))
    hid = HID3
    for name, key in (("w1l3", "L3_ffn_w1"), ("w3l3", "L3_ffn_w3")):
        up = np.zeros((128, E, hid), np.float32)
        for h in range(2):
            up[64 * h:64 * h + 64, :, :w[key].shape[1]] = w[key].transpose(2, 0, 1)
        arr[name] = up
    down = np.zeros((E, hid, C), np.float32)
    down[:, :w["L3_ffn_w2"].shape[2]] = w["L3_ffn_w2"].transpose(0, 2, 1)
    arr["w2l3"] = np.ascontiguousarray(down.reshape(E, NHB, HB, C).transpose(2, 0, 1, 3))

    nc = _bacc.Bacc("TRN2", target_bir_lowering=False, num_devices=1)
    args, arrays = [], {}
    for name in _INS:
        a = arr[name]
        arrays[f"in_{name}"] = a
        args.append(nc.dram_tensor(f"in_{name}", a.shape, F32, kind="ExternalInput").ap())
    args.append(nc.dram_tensor("out_0", (P, COLS), F32, kind="ExternalOutput").ap())
    n = NT * SLOTS
    args.append([nc.dram_tensor(f"slots{h}", (n, 2 * C), F16, kind="Internal").ap() for h in range(2)])
    args.append([nc.dram_tensor(f"results{h}", (n, C), F32, kind="Internal").ap() for h in range(2)])
    network(nc, *args, STOP_AFTER)
    r = _run(nc, [arrays], core_ids=[0])
    y = np.asarray(r.results[0]["out_0"])
    if STOP_AFTER < 5:
        return y.reshape(2, C, HALF, HH, WW).transpose(0, 2, 3, 4, 1).reshape(B, HH, WW, C)
    return y.reshape(128, TILES, 2, C).transpose(2, 1, 0, 3).reshape(B, HH, WW, C)
```

```python
import concourse.bass as bass
from concourse import mybir
from contextlib import ExitStack
import numpy as np

F32, F16 = mybir.dt.float32, mybir.dt.float16
I32, U32 = mybir.dt.int32, mybir.dt.uint32
ALU = mybir.AluOpType
ACT = mybir.ActivationFunctionType
AX = mybir.AxisListType.X

B, HH, WW, C = 32, 16, 16, 64
HALF = B // 2
N = HH * WW
P = 2 * C
COLS = HALF * N
CHUNK = 512
NCH = COLS // CHUNK
WS, SS, HEADS, DH = 8, 4, 8, 8
WT = WS * WS
NWIN = N // WT
PAIRS = COLS // WT
HP = HEADS // 2
VW = 34
RR, KK, PH = 16, 9, HH + 2
E, FH = 8, 128
HB, NHB = 114, 6
TILES = COLS // 128
HID3 = HB * NHB
SLOTS = 512
SUB = SLOTS // 128
ROUND = 2
NT = (2 * COLS + E * (SLOTS - 1)) // SLOTS

MATS = ["ident", "mean", "centre", "pair", "head", "sum", "stack",
        "wq0", "wk0", "wv0", "wo0", "wi1", "wr1", "wq2t", "wk2t", "wv2", "wo2",
        "wq4", "wk4", "wv4", "wo4", "rt3", "rt5", "before", "iota", "half0", "half1"]
VECS = (["bq0", "bk0", "bv0", "bo0", "ls0", "bi1", "br1", "ga1", "be1", "mu1", "va1",
         "bq2", "bk2", "bv2", "bo2", "ga3", "be3", "n14", "bo4", "n24", "cb1",
         "eps6", "eps5", "eps3", "tiny", "ln10", "ln20", "ln16", "guard", "one", "par0", "par1", "half0", "half1"]
        + [f"w2c{h}" for h in range(HEADS)] + [f"b1_{e}" for e in range(E)]
        + [f"b2_{e}" for e in range(E)] + [f"brr{k}" for k in range(2 * E)]
        + [f"rank{e}" for e in range(E)])
M = {n: i for i, n in enumerate(MATS)}
V = {n: i for i, n in enumerate(VECS)}

STEPS = {
    "pe_projected": [("q_proj", 8), ("k_proj", 8), ("v_proj", 16), ("l0_wo", 8), ("r_proj", 8), ("xi_proj", 8),
                     ("w2_centred", 5), ("k2_proj", 8), ("v2_proj", 8), ("q2_proj", 8), ("t2", 8), ("o2_proj", 8),
                     ("k4_proj", 8), ("v4_proj", 8), ("q4_proj", 8), ("o4_proj", 8)],
    "pe_summed": [("bias_hid", 16), ("g0_grp", 1), ("q_ssq", 8), ("k_ssq", 8), ("bias_z", 1), ("g1_grp", 1),
                  ("k2_norm", 1), ("kv2", 16), ("q2_s1", 8), ("r3_logits", 1), ("r3_load", 1), ("r3_gates", 1),
                  ("kv4", 16), ("ks4", 1), ("num4", 8)],
    "pe_mean": [("q2_s2", 8), ("n4_ms", 8), ("den4", 8), ("m4_ms", 8)],
    "ln_centred": [("a2_cen", 8), ("a3_cen", 8), ("l3_cen", 8), ("a4_cen", 8), ("a5_cen", 8)],
    "ln_variance": [("a2_var", 8), ("a3_var", 8), ("l3_var", 8), ("a4_var", 8), ("a5_var", 8)],
    "act_first": [("bias_relu", 16), ("q_sq", 8), ("k_sq", 8), ("r_ready", 8), ("xi_kept", 8), ("a2_sq", 8),
                  ("k2_sq", 8), ("k2_fourth", 8), ("k2_ln", 1), ("k2_rs", 1), ("q2_sq", 8), ("t2_kept", 8),
                  ("a3_sq", 8), ("l3_sq", 8), ("a4_sq", 8), ("n4_sq", 8), ("k4_exp", 8), ("q4_exp", 8),
                  ("z4_ln", 8), ("m4_sq", 8), ("a5_sq", 8)],
    "act_second": [("qscale", 1), ("g0_sd", 1), ("q_len", 8), ("k_len", 8), ("bias_exp", 1), ("g1_sd", 1),
                   ("bn_sd", 1), ("a2_ln", 8), ("q2_ln", 8), ("a3_ln", 8), ("sm1_exp", 1), ("sm2_exp", 1),
                   ("sm3_exp", 1), ("l3_ln", 8), ("a4_ln", 8), ("n4_ln", 8), ("z4", 8), ("m4_ln", 8), ("a5_ln", 8)],
    "act_rstd": [("a2_rstd", 8), ("q2_rs", 8), ("a3_rstd", 8), ("l3_rstd", 8), ("a4_rstd", 8), ("n4_rstd", 8),
                 ("m4_rstd", 8), ("a5_rstd", 8)],
    "l0_vector": [("hmask", 1), ("lsc", 1), ("vx_ones", 2), ("g0_stats", 16), ("g0_aggr", 16)],
    "l0_norms": [("q_biased", 8), ("q_clip", 8), ("q_norm", 8), ("k_biased", 8), ("k_clip", 8), ("k_norm", 8),
                 ("bias_v", 3), ("bm_ready", 4), ("bm_high", 4), ("bm_low", 4), ("v_ready", 32)],
    "l1_vector": [("l0_res", 8), ("x1_ready", 9), ("g1_stats", 16), ("g1_aggr", 16)],
    "l2_vector": [("a2", 8), ("w2_kept", 5), ("k2_biased", 8), ("v2_kept", 8), ("k2_sum", 9), ("k2_inv", 1),
                  ("k2_ready", 8), ("k2_clip", 1), ("kv2_kept", 16), ("q2_clip", 8), ("x3_ready", 8),
                  ("a3", 8), ("r3_mean", 8), ("sm1_in", 1), ("r3_rw", 1), ("sm2_in", 1), ("sm3_in", 1),
                  ("r3_diag", 1), ("gates2", 1), ("b2_prod", 2), ("y3_kept", 16), ("l3", 8), ("x4_part", 8),
                  ("x4_ready", 8)],
    "l3_vector": [("a4", 8), ("n4", 8), ("k4_neg", 8), ("v4_kept", 8), ("q4_neg", 8),
                  ("o4", 8), ("h4", 8), ("x5_part", 8), ("m4", 8), ("x5_ready", 8), ("a5", 8)],
    "vector_second": [("q2_ready", 8), ("k4_elu", 8), ("kv4_kept", 8), ("q4_elu", 8)],
}
PLACE = {}
for _group, _steps in STEPS.items():
    _base = 0
    for _step, _n in _steps:
        PLACE[_step] = _group, _base
        _base += _n


def network(nc, xw_d, xi_d, mats_d, vecs_d, feats_d, cw1_d, wmask_d, taps_d, wexp_d,
            w1l2_d, w2l2_d, w1l3_d, w3l3_d, w2l3_d, out_d, slots_d, results_d):
    with ExitStack() as ctx:
        def sb(name, shape):
            return ctx.enter_context(nc.sbuf_tensor(name, shape, F32))

        sems = {}

        def S(step):
            name = PLACE.get(step, (step, 0))[0]
            if name not in sems:
                sems[name] = nc.alloc_semaphore(name)
            return sems[name]

        def when(step, n):
            return S(step), PLACE.get(step, (step, 0))[1] + n

        X = sb("X", [P, COLS])
        A = sb("A", [P, COLS])
        T1 = sb("T1", [P, COLS])
        T2 = sb("T2", [P, COLS])
        T34 = sb("T34", [P, 2 * COLS])
        T3, T4 = T34[:, 0:COLS], T34[:, COLS:2 * COLS]
        big = sb("big", [P, 11264])
        KVS = sb("KVS", [P, HALF, 128])
        KSS = sb("KSS", [P, HALF, 128])
        l2w = sb("l2w", [P, E * NHB * C])
        up2 = l2w[:, 0:E * FH].bitcast(F16).rearrange("p (e v n) -> p e v n", e=E, v=2)
        down2 = l2w[:, E * FH:E * FH + 3 * E * C].bitcast(F16)
        expert2 = ctx.enter_context(nc.sbuf_tensor("expert2", [1, HALF], I32))
        index = ctx.enter_context(nc.sbuf_tensor("index", [P, 2, 2 * TILES], U32))
        ident16 = ctx.enter_context(nc.sbuf_tensor("ident16", [P, 128], F16))
        expert = ctx.enter_context(nc.sbuf_tensor("expert", [1, 2 * NT // ROUND], I32))
        rows = sb("rows", [P, 2, 128])
        mats = sb("mats", [P, len(MATS), 128])
        vecs = sb("vecs", [P, len(VECS)])
        small = sb("small", [P, 1024])
        bank = [ctx.enter_context(nc.psum_tensor(f"bank{i}", [P, CHUNK], F32)) for i in range(NCH)]

        def mat(name):
            return mats[:, M[name], :]

        def vec(name, n=1):
            return vecs[:, V[name]:V[name] + n]

        def ch(t, c, p0=0, p1=P):
            return t[p0:p1, c * CHUNK:(c + 1) * CHUNK]

        VX = big[:, 0:PAIRS * HP * VW].rearrange("p (n w) -> p n w", w=VW)
        o = PAIRS * HP * VW
        BM16 = big[:, o:o + NWIN * 512].bitcast(F16).rearrange("p (w v n) -> p w v n", w=NWIN, v=2)
        o += NWIN * 512
        wmask = big[:, o:o + NWIN * WT].rearrange("p (w k) -> p w k", w=NWIN)
        o += NWIN * WT
        cw1 = big[0:2, o:o + 128]
        PAD = big[:, 0:HALF * PH * PH].rearrange("p (b r c) -> p b r c", b=HALF, r=PH)
        o = HALF * PH * PH
        taps = big[:, o:o + KK * 128].rearrange("p (t n) -> p t n", t=KK)
        o += KK * 128
        wexp = big[:, o:o + KK * 128].rearrange("p (t n) -> p t n", t=KK)
        o += KK * 128
        w1l2 = big[:, o:o + E * FH]
        o += E * FH
        w2l2 = big[:, o:o + E * C]
        o += E * C
        taps16 = big[:, o:o + KK * 64].bitcast(F16).rearrange("p (t n) -> p t n", t=KK)
        o += KK * 64
        wexp16 = big[:, o:o + KK * 128].bitcast(F16).rearrange("p (t v n) -> p t v n", t=KK, v=2)
        A16 = [t[:, :, :].rearrange("p b n -> p (b n)").bitcast(F16) for t in (KVS, KSS)]
        wv16 = l2w[:, 0:128].bitcast(F16).rearrange("p (v n) -> p v n", v=2)
        stage = sb("stage", [P, 4608])
        QB = [stage[:, s * 128:(s + 1) * 128] for s in range(2)]
        OB = [stage[:, 256 + s * 128:256 + (s + 1) * 128] for s in range(2)]
        KX = [stage[:, 512 + s * 512:1024 + s * 512] for s in range(2)]
        SC = [stage[:, 1536 + s * 512:2048 + s * 512] for s in range(2)]
        PR = [stage[:, 2560 + s * 512:3072 + s * 512] for s in range(2)]
        PT = [stage[:, 3584 + s * 512:4096 + s * 512] for s in range(2)]
        PROD = [stage[:, s * 512:(s + 1) * 512] for s in range(4)]
        PROD_HI = [stage[:, 2048 + s * 256:2304 + s * 256].bitcast(F16) for s in range(4)]
        PROD_LO = [stage[:, 3072 + s * 256:3328 + s * 256].bitcast(F16) for s in range(4)]
        R16 = T2[:, 0:COLS // 2].bitcast(F16)
        stats = small[:, 0:96].rearrange("p (b s) -> p b s", s=6)
        mv = small[:, 96:128].rearrange("p (b s) -> p b s", s=2)
        gst = small[:, 128:160]
        grp = small[:, 160:192]
        gvar = small[:, 192:208]
        gsq = small[:, 208:224]
        gsd = small[:, 224:240]
        grs = small[:, 240:256]
        qscale = small[:, 256:257]
        lsc = small[:, 257:258]
        rowmax = [small[:, 272 + 8 * s:280 + 8 * s] for s in range(2)]
        rden = [small[:, 288 + 8 * s:296 + 8 * s] for s in range(2)]
        rmask = [small[:, 304 + 16 * s:320 + 16 * s] for s in range(2)]
        ksum = small[:, 368:432]
        kinv = small[:, 432:496]
        knorm = small[:, 496:512]
        kln = small[:, 512:528]
        krs = small[:, 528:544]
        bqc = small[:, 544:545]
        xmean = small[:, 552:568]
        y2b = small[:, 568:584]
        gates2 = small[:, 600:856]
        b1sel = small[:, 856:920]
        gate2 = small[:, 920:952]
        digit2 = small[0:1, 952:952 + 68]
        bnv = small[:, 336:344]

        hmask = small[:, 352:360]
        ident2 = mats[:, M["stack"], 0:64]
        pmask = mats[:, M["stack"], 64:96]

        xw3 = T1[:, :].rearrange("p (b n) -> p b n", n=N)
        X3 = X[:, :].rearrange("p (b n) -> p b n", n=N)
        A3 = A[:, :].rearrange("p (b n) -> p b n", n=N)

        def gn_vector(dve, t, src, src_sem, src_val):
            for b in range(HALF):
                if b % 2 == 0:
                    dve.wait_ge(*when(src_sem, src_val(b // 2)))
                nc.vector.bn_stats(stats[:, b, :], src[:, b, :]).then_inc(S(t + "_stats"), 1)
            for b in range(HALF):
                dve.wait_ge(*when(t + "_stats", b + 1))
                nc.vector.bn_aggr(mv[:, b, :], stats[:, b, :]).then_inc(S(t + "_aggr"), 1)
            dve.wait_ge(*when(t + "_aggr", HALF))
            nc.vector.tensor_copy(gst[:, 0:16], mv[:, :, 0]).then_inc(S(t + "_gst"), 1)
            nc.vector.tensor_tensor(gsq, mv[:, :, 0], mv[:, :, 0], ALU.mult).then_inc(S(t + "_sq"), 1)
            dve.wait_ge(*when(t + "_sq", 1))
            nc.vector.tensor_tensor(gst[:, 16:32], gsq, mv[:, :, 1], ALU.add).then_inc(S(t + "_gst"), 1)
            dve.wait_ge(*when(t + "_grp", 1))
            nc.vector.tensor_copy(grp, bank[0][:, 0:32]).then_inc(S(t + "_grpc"), 1)
            dve.wait_ge(*when(t + "_grpc", 1))
            nc.vector.tensor_tensor(gsq, grp[:, 0:16], grp[:, 0:16], ALU.mult).then_inc(S(t + "_grpc"), 1)
            dve.wait_ge(*when(t + "_grpc", 2))
            nc.vector.tensor_tensor(gvar, grp[:, 16:32], gsq, ALU.subtract).then_inc(S(t + "_var"), 1)
            dve.wait_ge(*when(t + "_rs", 1))
            for b in range(HALF):
                nc.vector.tensor_scalar(A3[:, b, :], src[:, b, :], grp[:, b:b + 1], grs[:, b:b + 1],
                                        ALU.subtract, ALU.mult).then_inc(S(t + "_norm"), 1)

        def gn_tensor(pe, t):
            pe.wait_ge(*when(t + "_gst", 2))
            nc.tensor.matmul(bank[0][:, 0:32], mat("pair"), gst, start=True, stop=True).then_inc(S(t + "_grp"), 1)

        def gn_scalar(act, t):
            act.wait_ge(*when(t + "_var", 1))
            nc.scalar.activation(gsd, gvar, ACT.Ln, bias=vec("eps5")).then_inc(S(t + "_sd"), 1)
            act.wait_ge(*when(t + "_sd", 1))
            nc.scalar.activation(grs, gsd, ACT.Exp, scale=-0.5).then_inc(S(t + "_rs"), 1)

        def ln_tensor(pe, t, src, ready, val, left=None, also=None):
            def var(c):
                pe.wait_ge(*when(t + "_sq", c + 1))
                if c >= 3:
                    pe.wait_ge(*when(t + "_ln", c - 2))
                else:
                    pe.wait_ge(*when(ready, left or val(4 + c)))
                nc.tensor.matmul(bank[4 + c % 3][:, :], mat("mean"), ch(T2, c), start=True, stop=True) \
                    .then_inc(S(t + "_var"), 1)

            for c in range(NCH):
                pe.wait_ge(*when(ready, val(c)))
                if c >= 4:
                    pe.wait_ge(*when(t, c - 3))
                nc.tensor.matmul(bank[c % 4][:, :], mat("centre"), ch(src, c), start=True, stop=True) \
                    .then_inc(S(t + "_cen"), 1)
                if c >= 1:
                    var(c - 1)
                if also and c >= 3:
                    also(c - 3)
            var(NCH - 1)
            if also:
                for c in range(NCH - 3, NCH):
                    also(c)

        def ln_scalar(act, t, eps):
            act.preload_act_table_set("natural_log_exp_and_others")

            def rstd(c):
                act.wait_ge(*when(t + "_var", c + 1))
                nc.scalar.activation(ch(T2, c), bank[4 + c % 3][:, :], ACT.Ln, bias=vec(eps)).then_inc(S(t + "_ln"), 1)
                act.wait_ge(*when(t + "_ln", c + 1))
                nc.scalar.activation(ch(T2, c), ch(T2, c), ACT.Exp, scale=-0.5).then_inc(S(t + "_rstd"), 1)

            for c in range(NCH):
                act.wait_ge(*when(t + "_cen", c + 1))
                nc.scalar.activation(ch(T2, c), bank[c % 4][:, :], ACT.Square).then_inc(S(t + "_sq"), 1)
                if c >= 1:
                    rstd(c - 1)
            rstd(NCH - 1)

        def ln_vector(dve, t, dst):
            for c in range(NCH):
                dve.wait_ge(*when(t + "_rstd", c + 1))
                nc.vector.tensor_tensor(ch(dst, c), bank[c % 4][:, :], ch(T2, c), ALU.mult).then_inc(S(t), 1)

        def rms_scalar(act, t, src, ready, eps):
            for c in range(NCH):
                act.wait_ge(*when(ready, c + 1))
                nc.scalar.activation(ch(T2, c), ch(src, c), ACT.Square).then_inc(S(t + "_sq"), 1)
            for c in range(NCH):
                act.wait_ge(*when(t + "_ms", c + 1))
                nc.scalar.activation(ch(T2, c), bank[c][:, :], ACT.Ln, bias=vec(eps)).then_inc(S(t + "_ln"), 1)
                act.wait_ge(*when(t + "_ln", c + 1))
                nc.scalar.activation(ch(T2, c), ch(T2, c), ACT.Exp, scale=-0.5).then_inc(S(t + "_rstd"), 1)

        def rms_tensor(pe, t):
            for c in range(NCH):
                pe.wait_ge(*when(t + "_sq", c + 1))
                nc.tensor.matmul(bank[c][:, :], mat("mean"), ch(T2, c), start=True, stop=True) \
                    .then_inc(S(t + "_ms"), 1)

        def steps(eng, f, last):
            for k in range(NWIN):
                f(k, k)
            with eng.Fori(1, HALF) as b:
                for w in range(NWIN):
                    f(b * NWIN + w, w)
            for k in range(PAIRS, PAIRS + last):
                f(k, k % NWIN)

        def at(k, lag):
            n = k - lag
            return n if not isinstance(k, int) or 0 <= n < PAIRS else None

        def reused(eng, name, n, per=1):
            if not isinstance(n, int) or n >= 2:
                eng.wait_ge(*when(name, (n - 1) * per))

        def steps2(eng, f, last):
            for k in range(2):
                f(k, k)
            with eng.Fori(1, HALF // 2) as b:
                for p in range(2):
                    f(b * 2 + p, p)
            for k in range(HALF, HALF + last):
                f(k, k % 2)

        def at2(k, lag):
            n = k - lag
            return n if not isinstance(k, int) or 0 <= n < HALF else None

        def steps3(eng, f):
            for r in range(ROUND):
                f(0, r)
            with eng.Fori(1, NT) as b:
                for r in range(ROUND):
                    f(b, r)

        def later(n, k):
            return not isinstance(n, int) or n >= k

        def low_parts(k):
            return ("tap_low_odd", k // KK * (KK // 2) + k % KK // 2 + 1) if k % KK % 2 else \
                ("tap_low_even", k // KK * (KK // 2 + 1) + k % KK // 2 + 1)

        route = sb("route", [HALF, 512])
        lg, lc, ld, wk, o1, o2 = (route[:, 16 * i:16 * i + 16] for i in range(6))
        lg3, wk3, o13, o23 = (v.rearrange("p (h e) -> p h e", e=E) for v in (lg, wk, o1, o2))
        s2a, s2b, s2f = route[:, 96:98], route[:, 98:100], route[:, 100:102]
        gdiag = route[:, 256:512]
        odiag = T3[0:HALF, 512:1024]
        kdiag = route[:, 160:224]
        hot2, hotx = T3[:, 1024:1536], T3[:, 1536:2048]
        half16 = KSS[:, 0, :].bitcast(F16).rearrange("p (h n) -> p h n", h=2)
        X16 = [T2[:, 2048 * v:2048 * v + 2048].bitcast(F16) for v in range(2)]
        XS2 = [T4[:, 2048 * h:2048 * h + 2048].bitcast(F16) for h in range(2)]
        lg5, wk5, o15, o25 = (ch(T1, i).rearrange("p (n e) -> p n e", e=E) for i in range(4))
        s5a, s5b, s5f = (T1[:, 2048 + 64 * i:2112 + 64 * i] for i in range(3))
        sel5, tot5, pre5a, pre5b, pos5, prod5 = (ch(T3, i) for i in range(6))
        nt5, end5, end5b, start5 = (T3[:, 3072 + 16 * i:3088 + 16 * i] for i in range(4))
        slot5 = T3[:, 3200:3328]
        cmp5 = T3[0:1, 3328:3328 + 2 * NT * E]
        exp5 = T3[0:1, 4000:4000 + 2 * NT]
        pack5 = cmp5[:, 0:2 * NT // ROUND]
        big16 = big[:, :].bitcast(F16)
        ups = big16[:, 0:E * 4 * HID3].rearrange("p (e v n) -> p e v n", e=E, v=4)
        downs = l2w[:, :].bitcast(F16)[0:HB, 0:E * NHB * 2 * C].rearrange("p (n) -> p n")
        w2v = downs.rearrange("p (e k v c) -> p e k v c", e=E, k=NHB, v=2)
        WS5 = [stage[:, HID3 * i:HID3 * i + HID3] for i in range(2)]
        zeros5 = stage[:, 2560:4608]
        rows5 = T2[:, :].bitcast(F16)
        rows5v = rows5.rearrange("p (j h v) -> p j h v", h=2, v=128)
        xtok = T4.rearrange("p (j h c) -> p j h c", h=2, c=C)
        G5 = [t.rearrange("p (j k c) -> p j k c", k=2, c=C) for t in (A[:, :], X[:, :])]
        s16 = stage[:, :].bitcast(F16)
        XS = [s16[:, SLOTS * i:SLOTS * i + SLOTS].rearrange("p (i v) -> p i v", v=128) for i in range(2)]
        XT = [s16[:, SLOTS * (2 + i):SLOTS * (3 + i)] for i in range(2)]
        HI5 = [s16[0:HB, SLOTS * (4 + i):SLOTS * (5 + i)] for i in range(3)]
        LO5 = [s16[0:HB, SLOTS * (7 + i):SLOTS * (8 + i)] for i in range(3)]
        S5 = [T3[0:HB, SLOTS * i:SLOTS * i + SLOTS] for i in range(3)]
        H5 = [T3[0:HB, SLOTS * (3 + i):SLOTS * (4 + i)] for i in range(3)]
        Y5 = [stage[:, 2560 + 256 * i:2816 + 256 * i].rearrange("p (i c) -> p i c", c=C) for i in range(2)]
        M5 = stage[:, 3072:3584].rearrange("p (j k c) -> p j k c", k=2, c=C)
        HID = [stage[:, 256 * i:256 * i + 256] for i in range(4)]
        HID_HI = [stage[:, 1024 + 128 * i:1152 + 128 * i].bitcast(F16) for i in range(4)]
        HID_LO = [stage[:, 1536 + 128 * i:1664 + 128 * i].bitcast(F16) for i in range(4)]
        MIX = [stage[:, 2048 + 256 * i:2304 + 256 * i] for i in range(2)]
        CAPACITY = float(-(-B * N * 5 // 4 // E))

        block = ctx.enter_context(nc.Block())

        @block.sync
        def _(sp):
            sp.dma_start(T2[0:2, :], feats_d).then_inc(S("loaded_feats"), 16)
            sp.dma_start(cw1, cw1_d).then_inc(S("loaded_feats"), 16)
            sp.dma_start(vecs[:, :], vecs_d).then_inc(S("loaded_vecs"), 16)
            sp.dma_start(T1[:, :], xw_d).then_inc(S("loaded_xw"), 16)
            sp.dma_start(mats[:, :, :], mats_d).then_inc(S("loaded_mats"), 16)
            sp.dma_start(wmask, wmask_d).then_inc(S("loaded_wmask"), 16)
            sp.wait_ge(*when("bm_low", NWIN))
            sp.dma_start(X[:, :], xi_d).then_inc(S("loaded_xi"), 16)
            sp.wait_ge(*when("l0_obd", PAIRS))
            sp.wait_ge(*when("l0_pv", PAIRS))
            sp.dma_start(taps, taps_d).then_inc(S("loaded_taps"), 16)
            sp.dma_start(wexp, wexp_d).then_inc(S("loaded_taps"), 16)
            sp.wait_ge(*when("loaded_taps", 32))
            sp.dma_start(w1l2, w1l2_d).then_inc(S("loaded_l2"), 16)
            sp.dma_start(w2l2, w2l2_d).then_inc(S("loaded_l2"), 16)
            sp.wait_ge(*when("loaded_l2", 32))
            sp.wait_ge(*when("zeros5", 1))
            for h in range(2):
                flat = slots_d[h].rearrange("(p a) v -> p (a v)", p=128)
                n = NT * SLOTS
                for i in range(4):
                    sp.dma_start(flat[:, i * n // 4:(i + 1) * n // 4],
                                 zeros5.bitcast(F16)[:, 0:n // 4]).then_inc(S("slots_zero"), 16)
            sp.wait_ge(*when("slots_zero", 128))
            for i in range(2 * E):
                if i >= 2:
                    sp.wait_ge(*when("ups_split", 2 * (i - 1)))
                sp.dma_start(WS5[i % 2], (w1l3_d, w3l3_d)[i % 2][:, i // 2, :]).then_inc(S(f"loaded_l3_{i % 2}"), 16)
            for e in range(E):
                i = 2 * E + e
                sp.wait_ge(*when("ups_split", 2 * (i - 1)))
                sp.dma_start(WS5[i % 2][0:HB, 0:NHB * C], w2l3_d[:, e, :, :].rearrange("p k c -> p (k c)")) \
                    .then_inc(S(f"loaded_l3_{i % 2}"), 16)

            def load5(t, s, h):
                if later(t, 2):
                    sp.wait_ge(*when("turned5", t - 1))
                rows = slots_d[h][bass.ds((t - h * NT) * SLOTS, SLOTS), :]
                sp.dma_start(XS[s], rows.rearrange("(p i) v -> p i v", i=SUB)).then_inc(S(f"loaded_xs_{s}"), 16)

            def store5(t, s, h):
                sp.wait_ge(*when("y5", t + 1))
                rows = results_d[h][bass.ds((t - h * NT) * SLOTS, SLOTS), :]
                sp.dma_start(rows.rearrange("(p i) c -> p i c", i=SUB), Y5[s]).then_inc(S(f"stored_y_{s}"), 16)

            sp.wait_ge(*when("scattered_0", 16 * 2 * TILES))
            for t in range(2):
                load5(t, t, 0)
            with sp.Fori(0, (NT - 3) // 2) as b:
                for r in range(2):
                    load5(b * 2 + (r + 2), r, 0)
                    store5(b * 2 + r, r, 0)
            load5(NT - 1, (NT - 1) % 2, 0)
            store5(NT - 3, (NT - 3) % 2, 0)
            sp.wait_ge(*when("scattered_1", 16 * 2 * TILES))
            for t in range(NT - 2, NT):
                load5(t + 2, t % 2, 1)
                store5(t, t % 2, 0)
            with sp.Fori(0, (NT - 3) // 2) as b:
                for r in range(2):
                    load5(b * 2 + (NT + r + 2), (NT + r) % 2, 1)
                    store5(b * 2 + (NT + r), (NT + r) % 2, 1)
            load5(2 * NT - 1, 1, 1)
            store5(2 * NT - 3, 1, 1)
            for t in range(2 * NT - 2, 2 * NT):
                store5(t, t % 2, 1)
            out5 = out_d.rearrange("p (j h c) -> p j h c", h=2, c=C)
            for h in range(2):
                for c in range(NCH):
                    sp.wait_ge(*when("mixed5", h * NCH + c + 1))
                    sp.dma_start(out5[:, 4 * c:4 * c + 4, h, :], xtok[:, 4 * c:4 * c + 4, h, :]) \
                        .then_inc(S("stored"), 16)
            sp.wait_ge(*when("stored", 16 * 2 * NCH))

        @block.gpsimd
        def _(pool):
            nc.gpsimd.memset(big[:, 0:PAIRS * HP * VW], 0.0).then_inc(S("vx_zero"), 1)
            pool.wait_ge(*when("loaded_mats", 16))
            nc.gpsimd.tensor_copy(wv16[:, 0, :], mat("wv0")).then_inc(S("wv_high"), 1)
            pool.wait_ge(*when("wv_high", 1))
            nc.gpsimd.tensor_tensor(wv16[:, 1, :], mat("wv0"), wv16[:, 0, :], ALU.subtract).then_inc(S("wv_low"), 1)
            for c in range(NCH):
                pool.wait_ge(*when("g0_norm", 2 * (c + 1)))
                nc.gpsimd.tensor_copy(ch(A16[0], c), ch(A, c)).then_inc(S("a16_high"), 1)
                pool.wait_ge(*when("a16_high", c + 1))
                nc.gpsimd.tensor_tensor(ch(A16[1], c), ch(A, c), ch(A16[0], c), ALU.subtract) \
                    .then_inc(S("a16_low"), 1)

            def stage_keys(k, w):
                n, s = at(k, 0), w % 2
                if n is None:
                    return
                pool.wait_ge(*when("q_norm", (NCH if not isinstance(n, int) else n // NWIN // 2 + 1)))
                pool.wait_ge(*when("k_norm", (NCH if not isinstance(n, int) else n // NWIN // 2 + 1)))
                reused(pool, "l0_scores", n)
                nc.gpsimd.tensor_tensor(QB[s].rearrange("p (h q) -> p h q", h=2),
                                        T1[:, bass.ds(n * WT, WT)].unsqueeze(1).broadcast_to([P, 2, WT]),
                                        vec("half0", 2).unsqueeze(2).broadcast_to([P, 2, WT]),
                                        ALU.mult).then_inc(S("l0_staged"), 1)
                nc.gpsimd.tensor_tensor(KX[s].rearrange("p (h k) -> p h k", h=HEADS),
                                        T2[:, bass.ds(n * WT, WT)].unsqueeze(1).broadcast_to([P, HEADS, WT]),
                                        hmask.unsqueeze(2).broadcast_to([P, HEADS, WT]),
                                        ALU.mult).then_inc(S("l0_staged"), 1)

            pool.wait_ge(*when("hmask", 1))
            steps(pool, stage_keys, 0)

            pool.wait_ge(*when("l0_pv", PAIRS))
            nc.gpsimd.memset(big[:, 0:HALF * PH * PH], 0.0).then_inc(S("pad_zero"), 1)
            pool.wait_ge(*when("loaded_taps", 32))
            nc.gpsimd.tensor_copy(wexp16[:, :, 0, :], wexp).then_inc(S("taps16"), 1)
            nc.gpsimd.tensor_copy(taps16, taps).then_inc(S("taps16"), 1)
            pool.wait_ge(*when("taps16", 2))
            nc.gpsimd.tensor_tensor(wexp16[:, :, 1, :], wexp, wexp16[:, :, 0, :], ALU.subtract).then_inc(S("taps16"), 1)
            for k in range(NCH * KK):
                if k % KK % 2 == 1:
                    pool.wait_ge(*when("tap_high", k + 1))
                    nc.gpsimd.tensor_tensor(PROD_LO[k % 4], PROD[k % 4], PROD_HI[k % 4], ALU.subtract) \
                        .then_inc(S("tap_low_odd"), 1)

            pool.wait_ge(*when("loaded_l2", 32))
            nc.gpsimd.memset(down2, 0.0).then_inc(S("w2_zero"), 1)
            w1v = w1l2.rearrange("p (e n) -> p e n", e=E)
            w2v2 = w2l2.rearrange("p (e c) -> p e c", e=E)
            d2v = down2.rearrange("p (e v z) -> p e v z", e=E, v=2)
            nc.gpsimd.tensor_copy(up2[:, :, 0, :], w1v).then_inc(S("l2_split"), 1)
            pool.wait_ge(*when("w2_zero", 1))
            nc.gpsimd.tensor_copy(d2v[:, :, 0, C:2 * C], w2v2).then_inc(S("l2_split"), 1)
            pool.wait_ge(*when("l2_split", 2))
            nc.gpsimd.tensor_tensor(up2[:, :, 1, :], w1v, up2[:, :, 0, :], ALU.subtract).then_inc(S("l2_split"), 1)
            nc.gpsimd.tensor_tensor(d2v[:, :, 1, C:2 * C], w2v2, d2v[:, :, 0, C:2 * C], ALU.subtract) \
                .then_inc(S("l2_split"), 1)
            for c in range(NCH):
                pool.wait_ge(*when("x16_high", c + 1))
                nc.gpsimd.tensor_tensor(ch(X16[1], c), ch(A, c), ch(X16[0], c), ALU.subtract) \
                    .then_inc(S("x16_low"), 1)
            pool.wait_ge(*when("y3_kept", HALF))
            nc.gpsimd.memset(zeros5, 0.0).then_inc(S("zeros5"), 1)
            for i in range(3 * E):
                pool.wait_ge(*when(f"loaded_l3_{i % 2}", 16 * (i // 2 + 1)))
                if i < 2 * E:
                    src, hi, lo = WS5[i % 2], ups[:, i // 2, 2 * (i % 2), :], ups[:, i // 2, 2 * (i % 2) + 1, :]
                else:
                    src = WS5[i % 2][0:HB, 0:NHB * C].rearrange("p (k c) -> p k c", c=C)
                    hi, lo = w2v[:, i - 2 * E, :, 0, :], w2v[:, i - 2 * E, :, 1, :]
                nc.gpsimd.tensor_copy(hi, src).then_inc(S("ups_split"), 1)
                pool.wait_ge(*when("ups_split", 2 * i + 1))
                nc.gpsimd.tensor_tensor(lo, src, hi, ALU.subtract).then_inc(S("ups_split"), 1)
            pool.wait_ge(*when("index5", 2))
            pool.wait_ge(*when("rows5_low", NCH))
            pool.wait_ge(*when("slots_zero", 128))
            for h in range(2):
                for j in range(TILES):
                    for k in range(2):
                        n = 2 * j + h
                        pool.indirect_dma_start(
                            slots_d[h], bass.IndirectOffsetOnAxis(ap=index[:, k, n:n + 1], axis=0),
                            rows5[:, n * 128:(n + 1) * 128], None).then_inc(S(f"scattered_{h}"), 16)
            for h in range(2):
                for s in range(2):
                    pool.wait_ge(*when(f"stored_y_{s}", 16 * ((NT + 1 - s) // 2 if h == 0 else NT)))
                for j in range(TILES):
                    for k in range(2):
                        n = 2 * j + h
                        pool.indirect_dma_start(
                            G5[h][:, j, k, :], None, results_d[h],
                            bass.IndirectOffsetOnAxis(ap=index[:, k, n:n + 1], axis=0)).then_inc(S(f"gathered_{h}_{j // 4}"), 16)

        @block.vector
        def _(dve):
            dve.wait_ge(*when("loaded_mats", 16))
            dve.wait_ge(*when("loaded_vecs", 16))
            nc.vector.tensor_tensor(hmask, mats[:, M["head"], 0:64:8], mats[:, M["head"], 64:128:8],
                                    ALU.add).then_inc(S("hmask"), 1)
            nc.vector.tensor_copy(ident16[:, :], mat("ident")).then_inc(S("ident16"), 1)
            nc.vector.tensor_scalar(lsc, vec("ls0"), float(np.log(np.float32(100.0))), None, ALU.min) \
                .then_inc(S("lsc"), 1)
            dve.wait_ge(*when("vx_zero", 1))
            for j in range(2):
                nc.vector.tensor_copy(VX[:, :, 32 + j], vec(f"par{j}").broadcast_to([P, PAIRS * HP])) \
                    .then_inc(S("vx_ones"), 1)
            gn_vector(dve, "g0", xw3, "loaded_xw", lambda c: 16)
            for t, T in (("q", T1), ("k", T2)):
                for c in range(NCH):
                    dve.wait_ge(*when(t + "_proj", c + 1))
                    nc.vector.tensor_scalar(ch(T, c), bank[c][:, :], vec(f"b{t}0"), None, ALU.add) \
                        .then_inc(S(t + "_biased"), 1)
                for c in range(NCH):
                    dve.wait_ge(*when(t + "_ssq", c + 1))
                    nc.vector.tensor_scalar(ch(T3, c), bank[c][:, :], 1e-24, 2.0 ** 20, ALU.max, ALU.mult) \
                        .then_inc(S(t + "_clip"), 1)
                if t == "q":
                    dve.wait_ge(*when("qscale", 1))
                for c in range(NCH):
                    dve.wait_ge(*when(t + "_rlen", c + 1))
                    nc.vector.scalar_tensor_tensor(ch(T, c), ch(T3, c), qscale if t == "q" else 1.0, ch(T, c),
                                                   ALU.mult, ALU.mult).then_inc(S(t + "_norm"), 1)
            dve.wait_ge(*when("bias_exp", 1))
            bz = ch(T4, 5)
            nc.vector.tensor_scalar(bz, ch(T4, 4), 1.0, None, ALU.add).then_inc(S("bias_v"), 1)
            dve.wait_ge(*when("bias_v", 1))
            nc.vector.reciprocal(ch(T4, 6), bz).then_inc(S("bias_v"), 1)
            dve.wait_ge(*when("bias_v", 2))
            nc.vector.tensor_scalar(ch(T4, 7).rearrange("p (h k) -> p k h", h=HEADS),
                                    ch(T4, 6).rearrange("p (k h) -> p k h", h=HEADS), 16.0, None, ALU.mult) \
                .then_inc(S("bias_v"), 1)
            dve.wait_ge(*when("bias_v", 3))
            dve.wait_ge(*when("loaded_wmask", 16))
            for w in range(NWIN):
                nc.vector.tensor_tensor(ch(X, w).rearrange("p (h k) -> p h k", h=HEADS),
                                        ch(T4, 7).rearrange("p (h k) -> p h k", h=HEADS),
                                        wmask[:, w, :].unsqueeze(1).broadcast_to([P, HEADS, WT]),
                                        ALU.add).then_inc(S("bm_ready"), 1)
            for w in range(NWIN):
                dve.wait_ge(*when("bm_ready", w + 1))
                nc.vector.tensor_copy(BM16[:, w, 0, :], ch(X, w)).then_inc(S("bm_high"), 1)
            for w in range(NWIN):
                dve.wait_ge(*when("bm_high", w + 1))
                nc.vector.tensor_tensor(BM16[:, w, 1, :], ch(X, w), BM16[:, w, 0, :], ALU.subtract) \
                    .then_inc(S("bm_low"), 1)
            dve.wait_ge(*when("vx_zero", 1))
            for g in range(PAIRS // 4):
                dve.wait_ge(*when("v_proj", g + 1))
                for x in range(2):
                    nc.vector.tensor_copy(
                        VX[64 * x:64 * x + 64, g * 16:g * 16 + 16, 0:32]
                        .rearrange("p n (h x d) -> p n h x d", h=2, x=2)[:, :, :, x, :],
                        bank[g % NCH][64 * x:64 * x + 64, 0:256].rearrange("p (n h d) -> p n h d", h=2, d=DH)) \
                        .then_inc(S("v_ready"), 1)

            def softmax_and_out(k, w):
                n, s = at(k, 0), w % 2
                if n is not None:
                    sc = SC[s].rearrange("p (h k) -> p h k", h=HEADS)
                    biased = bank[s][:, :].rearrange("p (h k) -> p h k", h=HEADS)
                    dve.wait_ge(*when("l0_scores", n + 1))
                    nc.vector.tensor_reduce(rowmax[s], biased, AX, ALU.max).then_inc(S("l0_max"), 1)
                    dve.wait_ge(*when("l0_max", n + 1))
                    reused(dve, "l0_exp", n)
                    nc.vector.tensor_tensor(sc, biased, rowmax[s].unsqueeze(2).broadcast_to([P, HEADS, WT]),
                                            ALU.subtract).then_inc(S("l0_shifted"), 1)
                n = at(k, 2)
                if n is not None:
                    ob = bank[4 + s][:, 0:HP * VW].rearrange("p (g v) -> p g v", v=VW)
                    dve.wait_ge(*when("l0_pv", n + 1))
                    nc.vector.reciprocal(rden[s].rearrange("p (g x) -> p g x", x=2), ob[:, :, 32:34]) \
                        .then_inc(S("l0_rden"), 1)
                    dve.wait_ge(*when("l0_rden", n + 1))
                    rd = rden[s].rearrange("p (g x) -> p g x", x=2)
                    for h in range(2):
                        nc.vector.tensor_scalar(rmask[s].rearrange("p (g h x) -> p g h x", h=2, x=2)[:, :, h, :],
                                                rd, vec(f"half{h}"), None, ALU.mult).then_inc(S("l0_rmask"), 1)
                    dve.wait_ge(*when("l0_rmask", (n + 1) * 2))
                    reused(dve, "l0_ot", n)
                    nc.vector.tensor_tensor(OB[s].rearrange("p (g y d) -> p g y d", g=HP, d=DH),
                                            ob[:, :, 0:32].rearrange("p g (y d) -> p g y d", d=DH),
                                            rmask[s].rearrange("p (g y) -> p g y", g=HP).unsqueeze(3)
                                            .broadcast_to([P, HP, 4, DH]), ALU.mult).then_inc(S("l0_obd"), 1)

            dve.wait_ge(*when("v_ready", PAIRS // 2))
            steps(dve, softmax_and_out, 2)
            for c in range(NCH):
                dve.wait_ge(*when("l0_wo", c + 1))
                nc.vector.tensor_scalar(ch(T4, c), bank[c][:, :], vec("bo0"), None, ALU.add) \
                    .then_inc(S("l0_res"), 1)
            dve.wait_ge(*when("l0_res", NCH))
            dve.wait_ge(*when("loaded_xi", 16))
            Xi = X[:, :].rearrange("p (b r c) -> p b r c", r=HH, c=WW)
            Tw = T4[:, :].rearrange("p (b w i j) -> p b w i j", w=NWIN, i=WS, j=WS)
            runs = [(0, 0, SS, WS), (1, 0, SS + WS, WS - SS), (1, WS - SS, 0, SS)]
            for wy, iy, r, nr in runs:
                for wx, ix, q, nq in runs:
                    xv = Xi[:, :, r:r + nr, q:q + nq]
                    nc.vector.tensor_tensor(xv, xv, Tw[:, :, 2 * wy + wx, iy:iy + nr, ix:ix + nq], ALU.add) \
                        .then_inc(S("x1_ready"), 1)

            gn_vector(dve, "g1", X3, "x1_ready", lambda c: 9)
            sc_, sh_ = bnv[:, 3:4], bnv[:, 5:6]
            dve.wait_ge(*when("bn_rs", 1))
            nc.vector.tensor_tensor(bnv[:, 4:5], vec("br1"), vec("mu1"), ALU.subtract).then_inc(S("bn_v"), 1)
            dve.wait_ge(*when("bn_v", 1))
            nc.vector.tensor_tensor(sc_, bnv[:, 2:3], vec("ga1"), ALU.mult).then_inc(S("bn_v"), 1)
            dve.wait_ge(*when("bn_v", 2))
            nc.vector.scalar_tensor_tensor(sh_, bnv[:, 4:5], sc_, vec("be1"), ALU.mult, ALU.add) \
                .then_inc(S("bn_v"), 1)
            for c in range(NCH):
                dve.wait_ge(*when("r_ready", c + 1))
                nc.vector.tensor_copy(ch(R16, c), ch(T1, c)).then_inc(S("r_high"), 1)
            for c in range(NCH):
                dve.wait_ge(*when("r_high", c + 1))
                low = ch(R16, c, C, P)
                nc.vector.tensor_tensor(low, ch(T1, c, C, P), low, ALU.subtract).then_inc(S("r_low"), 1)

            def tap_low(k):
                if k % KK % 2 == 0:
                    dve.wait_ge(*when("tap_high", k + 1))
                    nc.vector.tensor_tensor(PROD_LO[k % 4], PROD[k % 4], PROD_HI[k % 4], ALU.subtract) \
                        .then_inc(S("tap_low_even"), 1)

            for c in range(NCH):
                dve.wait_ge(*when("xi_kept", min(c + 1, NCH)))
                for t in range(KK):
                    k, i, j = c * KK + t, t // 3, t % 3
                    dve.wait_ge(*when("tap_w", k + 1))
                    if k >= 4:
                        dve.wait_ge(*when(*low_parts(k - 4)))
                    nc.vector.tensor_tensor(
                        PROD[k % 4].rearrange("p (b r c) -> p b r c", r=HH, c=WW),
                        bank[k % 4][:, :].rearrange("p (b r c) -> p b r c", r=HH, c=WW),
                        PAD[:, 2 * c:2 * c + 2, i:i + HH, j:j + WW], ALU.mult).then_inc(S("tap_prod"), 1)
                    if k:
                        tap_low(k - 1)
                    if t == 6 and c:
                        dve.wait_ge(*when("tap_summed", c * KK))
                        nc.vector.tensor_tensor(ch(X, c - 1), ch(X, c - 1), bank[4 + (c - 1) % 2][:, :], ALU.add) \
                            .then_inc(S("x2_ready"), 1)
            tap_low(NCH * KK - 1)
            dve.wait_ge(*when("tap_summed", NCH * KK))
            nc.vector.tensor_tensor(ch(X, NCH - 1), ch(X, NCH - 1), bank[4 + (NCH - 1) % 2][:, :], ALU.add) \
                .then_inc(S("x2_ready"), 1)

            ln_vector(dve, "a2", A)
            for i in range(2):
                dve.wait_ge(*when("w2_centred", i + 1))
                nc.vector.tensor_copy(mat(("wq2t", "wk2t")[i]), bank[i][:, 0:128]).then_inc(S("w2_kept"), 1)
            for i in range(2):
                dve.wait_ge(*when("w2_centred", i + 3))
                nc.vector.tensor_copy(rows[:, i, :], bank[2 + i][:, 0:128]).then_inc(S("w2_kept"), 1)
            dve.wait_ge(*when("w2_centred", 5))
            nc.vector.tensor_copy(bqc, bank[4][:, 0:1]).then_inc(S("w2_kept"), 1)
            dve.wait_ge(*when("w2_kept", 5))
            for c in range(NCH):
                dve.wait_ge(*when("k2_proj", c + 1))
                nc.vector.tensor_tensor(ch(T1, c).rearrange("p (j n) -> p j n", n=128),
                                        bank[c][:, :].rearrange("p (j n) -> p j n", n=128),
                                        rows[:, 0, :].unsqueeze(1).broadcast_to([P, 4, 128]), ALU.add) \
                    .then_inc(S("k2_biased"), 1)
            for c in range(NCH):
                dve.wait_ge(*when("v2_proj", c + 1))
                nc.vector.tensor_tensor(ch(T3, c).rearrange("p (j n) -> p j n", n=128),
                                        bank[c][:, :].rearrange("p (j n) -> p j n", n=128),
                                        rows[:, 1, :].unsqueeze(1).broadcast_to([P, 4, 128]), ALU.add) \
                    .then_inc(S("v2_kept"), 1)
            for c in range(NCH):
                dve.wait_ge(*when("k2_sq", c + 1))
                nc.vector.tensor_reduce(ksum[:, 8 * c:8 * c + 8], ch(T1, c).rearrange("p (j n) -> p j n", n=64),
                                        AX, ALU.add).then_inc(S("k2_sum"), 1)
            dve.wait_ge(*when("k2_sum", NCH))
            nc.vector.tensor_scalar(ksum, ksum, 1e-7, None, ALU.add).then_inc(S("k2_sum"), 1)
            dve.wait_ge(*when("k2_sum", NCH + 1))
            nc.vector.reciprocal(kinv, ksum).then_inc(S("k2_inv"), 1)
            dve.wait_ge(*when("k2_inv", 1))
            for c in range(NCH):
                k = ch(T1, c).rearrange("p (j n) -> p j n", n=64)
                nc.vector.tensor_tensor(k, k, kinv[:, 8 * c:8 * c + 8].unsqueeze(2).broadcast_to([P, 8, 64]),
                                        ALU.mult).then_inc(S("k2_ready"), 1)
            dve.wait_ge(*when("k2_norm", 1))
            nc.vector.tensor_scalar(knorm, bank[4][:, 0:HALF], 1e-24, 2.0 ** 40, ALU.max, ALU.mult) \
                .then_inc(S("k2_clip"), 1)
            dve.wait_ge(*when("k2_rs", 1))
            for b in range(HALF):
                dve.wait_ge(*when("kv2", 4 * (b // 4 + 1)))
                nc.vector.scalar_tensor_tensor(KVS[:, b, :], bank[b // 4][:, (b % 4) * 128:(b % 4 + 1) * 128],
                                               krs[:, b:b + 1], mat("sum"), ALU.mult, ALU.mult) \
                    .then_inc(S("kv2_kept"), 1)
            for c in range(NCH):
                dve.wait_ge(*when("q2_guard", c + 1))
                dve.wait_ge(*when("q2_s2", c + 1))
                nc.vector.scalar_tensor_tensor(ch(T1, c), bank[4 + c % 4][:, :], 2.0 ** 40, ch(T1, c),
                                               ALU.mult, ALU.max).then_inc(S("q2_clip"), 1)
                if c >= 2:
                    dve.wait_ge(*when("q2_rs", c - 1))
                    nc.vector.tensor_tensor(ch(T2, c - 2), ch(T2, c - 2), ch(T1, c - 2), ALU.mult) \
                        .then_inc(S("q2_ready"), 1)
            for c in range(NCH - 2, NCH):
                dve.wait_ge(*when("q2_rs", c + 1))
                nc.vector.tensor_tensor(ch(T2, c), ch(T2, c), ch(T1, c), ALU.mult).then_inc(S("q2_ready"), 1)
            for c in range(NCH):
                dve.wait_ge(*when("o2_proj", c + 1))
                nc.vector.scalar_tensor_tensor(ch(X, c), bank[c][:, :], vec("bo2"), ch(X, c), ALU.add, ALU.add) \
                    .then_inc(S("x3_ready"), 1)

            nc.vector.tensor_copy(half16, mats[:, M["half0"]:M["half0"] + 2, :]).then_inc(S("half16"), 1)
            ln_vector(dve, "a3", A)
            for c in range(NCH):
                dve.wait_ge(*when("a3", c + 1))
                nc.vector.tensor_reduce(xmean[:, 2 * c:2 * c + 2], ch(A, c).rearrange("p (b n) -> p b n", n=N),
                                        AX, ALU.add).then_inc(S("r3_mean"), 1)
            links = [0]

            def link(instruction):
                links[0] += 1
                instruction.then_inc(S("link"), 1)
                dve.wait_ge(*when("link", links[0]))

            def top2(p, n, probs, work, one1, one2, max1, max2, first):
                def spread(v):
                    return v.unsqueeze(2).broadcast_to([p, n, E])
                rank = vec("rank0", E)[0:p, :].unsqueeze(1).broadcast_to([p, n, E])
                for one, best, src in ((one1, max1, probs), (one2, max2, work)):
                    link(nc.vector.tensor_reduce(best, src, AX, ALU.max))
                    link(nc.vector.tensor_tensor(one, src, spread(best), ALU.is_ge))
                    link(nc.vector.tensor_tensor(one, one, rank, ALU.mult))
                    link(nc.vector.tensor_reduce(first, one, AX, ALU.max))
                    link(nc.vector.tensor_tensor(one, rank, spread(first), ALU.is_equal))
                    if one is one1:
                        link(nc.vector.scalar_tensor_tensor(work, one, -4.0, probs, ALU.mult, ALU.add))

            def softmax_vector(p, n, z, m, t):
                link(nc.vector.tensor_reduce(m, z, AX, ALU.max))
                nc.vector.tensor_tensor(z, z, m.unsqueeze(2).broadcast_to([p, n, E]), ALU.subtract) \
                    .then_inc(S(t + "_in"), 1)
                dve.wait_ge(*when(t + "_exp", 1))
                link(nc.vector.tensor_reduce(m, z, AX, ALU.add))
                link(nc.vector.reciprocal(m, m))
                link(nc.vector.tensor_tensor(z, z, m.unsqueeze(2).broadcast_to([p, n, E]), ALU.mult))

            dve.wait_ge(*when("r3_logits", 1))
            link(nc.vector.scalar_tensor_tensor(lg, bank[0][0:HALF, 0:16], 1.0 / N,
                                                vecs[0:HALF, V["brr0"]:V["brr0"] + 16], ALU.mult, ALU.add))
            softmax_vector(HALF, 2, lg3, s2a, "sm1")
            nc.vector.tensor_copy(lc, lg).then_inc(S("r3_rw"), 1)
            dve.wait_ge(*when("r3_load", 1))
            link(nc.vector.tensor_copy(ld, bank[1][0:HALF, 0:16]))
            link(nc.vector.tensor_tensor(ld[:, 0:8], ld[:, 0:8], ld[:, 8:16], ALU.add))
            link(nc.vector.reciprocal(ld[:, 8:16], ld[:, 0:8]))
            link(nc.vector.tensor_scalar(ld[:, 8:16], ld[:, 8:16], CAPACITY / N, 1.0, ALU.mult, ALU.min))
            link(nc.vector.tensor_tensor(lg3, lg3, ld[:, 8:16].unsqueeze(1).broadcast_to([HALF, 2, E]), ALU.mult))
            softmax_vector(HALF, 2, lg3, s2a, "sm2")
            top2(HALF, 2, lg3, wk3, o13, o23, s2a, s2b, s2f)
            nc.vector.tensor_tensor(s2b, s2b, s2a, ALU.subtract).then_inc(S("sm3_in"), 1)
            dve.wait_ge(*when("sm3_exp", 1))
            link(nc.vector.tensor_scalar(s2a, s2b, 1.0, None, ALU.add))
            link(nc.vector.reciprocal(s2a, s2a))
            link(nc.vector.tensor_tensor(s2b, s2a, s2b, ALU.mult))
            eye = mats[0:HALF, M["ident"], 0:HALF]
            for k, (one, g) in enumerate(((o13, s2a), (o23, s2b))):
                for h in range(2):
                    nc.vector.tensor_tensor(
                        odiag.rearrange("p (b h k e) -> p b h k e", h=2, k=2, e=E)[:, :, h, k, :],
                        eye.unsqueeze(2).broadcast_to([HALF, HALF, E]),
                        one[:, h, :].unsqueeze(1).broadcast_to([HALF, HALF, E]), ALU.mult).then_inc(S("r3_hot"), 1)
                nc.vector.tensor_tensor(kdiag.rearrange("p (b h k) -> p b h k", h=2, k=2)[:, :, :, k],
                                        eye.unsqueeze(2).broadcast_to([HALF, HALF, 2]),
                                        g.unsqueeze(1).broadcast_to([HALF, HALF, 2]), ALU.mult).then_inc(S("r3_hot"), 1)
            dve.wait_ge(*when("r3_hot", 6))
            link(nc.vector.tensor_tensor(o13, o13, s2a.unsqueeze(2).broadcast_to([HALF, 2, E]), ALU.mult))
            link(nc.vector.tensor_tensor(o23, o23, s2b.unsqueeze(2).broadcast_to([HALF, 2, E]), ALU.mult))
            link(nc.vector.tensor_tensor(o13, o13, o23, ALU.add))
            nc.vector.tensor_tensor(gdiag.rearrange("p (b g) -> p b g", g=16),
                                    mats[0:HALF, M["ident"], 0:HALF].unsqueeze(2).broadcast_to([HALF, HALF, 16]),
                                    o1.unsqueeze(1).broadcast_to([HALF, HALF, 16]), ALU.mult) \
                .then_inc(S("r3_diag"), 1)
            dve.wait_ge(*when("r3_chosen", 2))
            g2 = bank[2][:, 256:320].rearrange("p (b h k) -> p b h k", h=2, k=2)
            for h in range(2):
                q = slice(64 * h, 64 * h + 64)
                link(nc.vector.tensor_copy(gate2[q].rearrange("p (b k) -> p b k", k=2), g2[q, :, h, :]))
            link(nc.vector.tensor_copy(hot2, bank[3][:, :]))
            hot3, hotx3 = (v.rearrange("p (n e) -> p n e", e=E) for v in (hot2, hotx))
            link(nc.vector.tensor_tensor(hotx3, hot3, vec("b1_0", E).unsqueeze(1).broadcast_to([P, 64, E]), ALU.mult))
            link(nc.vector.tensor_reduce(b1sel, hotx3, AX, ALU.add))
            link(nc.vector.tensor_tensor(hotx3[0:1], hot3[0:1],
                                         vec("rank0", E)[0:1, :].unsqueeze(1).broadcast_to([1, 64, E]), ALU.mult))
            link(nc.vector.memset(digit2[:, 0:4], 0.0))
            link(nc.vector.tensor_reduce(digit2[:, 4:68], hotx3[0:1], AX, ALU.add))
            link(nc.vector.tensor_scalar(digit2[:, 4:68], digit2[:, 4:68], -1.0, float(E), ALU.mult, ALU.add))
            own = digit2[:, 4:68].rearrange("p (b i) -> p b i", i=4)
            prev = digit2[:, 0:64].rearrange("p (b i) -> p b i", i=4)
            number = hotx[0:1, 0:HALF]
            link(nc.vector.tensor_copy(number, own[:, :, 3]))
            for d in (own[:, :, 2], own[:, :, 1], own[:, :, 0], prev[:, :, 3], prev[:, :, 2], prev[:, :, 1]):
                link(nc.vector.scalar_tensor_tensor(number, number, float(E), d, ALU.mult, ALU.add))
            nc.vector.tensor_copy(expert2[:, :], number).then_inc(S("expert2"), 1)

            dve.wait_ge(*when("r3_gates", 1))
            nc.vector.tensor_copy(gates2, bank[6][:, 0:256]).then_inc(S("gates2"), 1)
            dve.wait_ge(*when("gates2", 1))
            g4 = gates2.rearrange("p (b h e) -> p b h e", h=2, e=E)
            tb = ch(T3, 0)[:, 0:128].rearrange("p (b e) -> p b e", e=E)
            for h in range(2):
                q = slice(64 * h, 64 * h + 64)
                nc.vector.tensor_tensor(tb[q], g4[q, :, h, :],
                                        vec("b2_0", E)[q, :].unsqueeze(1).broadcast_to([64, HALF, E]), ALU.mult) \
                    .then_inc(S("b2_prod"), 1)
            dve.wait_ge(*when("b2_prod", 2))
            link(nc.vector.tensor_reduce(y2b, tb, AX, ALU.add))

            def mix3(b, p):
                dve.wait_ge(*when("down3", 4 * (b + 1)))
                at_ = bass.ds(b * N, N)
                for i in range(2):
                    nc.vector.scalar_tensor_tensor(MIX[p], bank[4 + p][:, i * N:(i + 1) * N],
                                                   gate2[:, bass.ds(b * 2 + i, 1)], MIX[p] if i else A[:, at_],
                                                   ALU.mult, ALU.add).then_inc(S("mix3"), 1)
                    dve.wait_ge(*when("mix3", 2 * b + i + 1))
                nc.vector.tensor_scalar(T1[:, at_], MIX[p], y2b[:, bass.ds(b, 1)], None, ALU.add) \
                    .then_inc(S("y3_kept"), 1)

            def image_vector(k, p):
                b = at2(k, 0)
                if b is not None:
                    for u in range(4):
                        n = 4 * b + u
                        dve.wait_ge(*when("high3", n + 1))
                        if later(n, 4):
                            dve.wait_ge(*when("down3", n - 3))
                        nc.vector.tensor_tensor(HID_LO[u], HID[u], HID_HI[u], ALU.subtract).then_inc(S("low3"), 1)
                b = at2(k, 1)
                if b is not None:
                    mix3(b, (p + 1) % 2)

            steps2(dve, image_vector, 1)
            ln_vector(dve, "l3", T3)
            for c in range(NCH):
                dve.wait_ge(*when("l3", c + 1))
                nc.vector.scalar_tensor_tensor(ch(X, c), ch(T3, c), vec("ga3"), ch(X, c), ALU.mult, ALU.add) \
                    .then_inc(S("x4_part"), 1)
            for c in range(NCH):
                dve.wait_ge(*when("x4_part", c + 1))
                nc.vector.tensor_scalar(ch(X, c), ch(X, c), vec("be3"), None, ALU.add).then_inc(S("x4_ready"), 1)

            ln_vector(dve, "a4", A)
            for c in range(NCH):
                dve.wait_ge(*when("n4_rstd", c + 1))
                nc.vector.scalar_tensor_tensor(ch(T1, c), ch(T2, c), vec("n14"), ch(A, c), ALU.mult, ALU.mult) \
                    .then_inc(S("n4"), 1)
            for t, T in (("k", T3), ("q", T2)):
                for c in range(NCH):
                    dve.wait_ge(*when(t + "4_proj", c + 1))
                    nc.vector.tensor_scalar(ch(T, c), bank[c][:, :], 0.0, None, ALU.min).then_inc(S(t + "4_neg"), 1)
                    if c >= 2:
                        dve.wait_ge(*when(t + "4_exp", c - 1))
                        nc.vector.scalar_tensor_tensor(ch(T, c - 2), bank[c - 2][:, :], 0.0, ch(T, c - 2),
                                                       ALU.max, ALU.add).then_inc(S(t + "4_elu"), 1)
                for c in range(NCH - 2, NCH):
                    dve.wait_ge(*when(t + "4_exp", c + 1))
                    nc.vector.scalar_tensor_tensor(ch(T, c), bank[c][:, :], 0.0, ch(T, c),
                                                   ALU.max, ALU.add).then_inc(S(t + "4_elu"), 1)
                if t == "k":
                    for c in range(NCH):
                        dve.wait_ge(*when("v4_proj", c + 1))
                        nc.vector.tensor_copy(ch(T4, c), bank[c][:, :]).then_inc(S("v4_kept"), 1)
                    for c in range(4):
                        dve.wait_ge(*when("kv4", 4 * (c + 1)))
                        nc.vector.tensor_tensor(KVS[:, 4 * c:4 * c + 4, :],
                                                bank[c][:, :].rearrange("p (b n) -> p b n", n=128),
                                                mat("head").unsqueeze(1).broadcast_to([P, 4, 128]), ALU.mult) \
                            .then_inc(S("kv4_kept"), 1)
                    dve.wait_ge(*when("ks4", 1))
                    nc.vector.tensor_copy(krs, bank[4][:, 0:HALF]).then_inc(S("ks4_kept"), 1)
                    dve.wait_ge(*when("ks4_kept", 1))
                    for c in range(4):
                        nc.vector.tensor_tensor(KSS[:, 4 * c:4 * c + 4, :],
                                                krs[:, 4 * c:4 * c + 4].unsqueeze(2).broadcast_to([P, 4, 128]),
                                                mat("head").unsqueeze(1).broadcast_to([P, 4, 128]), ALU.mult) \
                            .then_inc(S("kv4_kept"), 1)
            for c in range(NCH):
                dve.wait_ge(*when("z4", c + 1))
                dve.wait_ge(*when("num4", c + 1))
                nc.vector.tensor_tensor(ch(T1, c), bank[4 + c % 4][:, :], ch(T3, c), ALU.mult).then_inc(S("o4"), 1)
            for c in range(NCH):
                dve.wait_ge(*when("o4_proj", c + 1))
                nc.vector.scalar_tensor_tensor(ch(T4, c), bank[c][:, :], vec("bo4"), ch(A, c), ALU.add, ALU.add) \
                    .then_inc(S("h4"), 1)
            for c in range(NCH):
                dve.wait_ge(*when("h4", c + 1))
                nc.vector.tensor_tensor(ch(X, c), ch(X, c), ch(T4, c), ALU.add).then_inc(S("x5_part"), 1)
            for c in range(NCH):
                dve.wait_ge(*when("m4_rstd", c + 1))
                nc.vector.scalar_tensor_tensor(ch(T4, c), ch(T4, c), vec("n24"), ch(T2, c), ALU.mult, ALU.mult) \
                    .then_inc(S("m4"), 1)
            for c in range(NCH):
                dve.wait_ge(*when("m4", c + 1))
                nc.vector.tensor_tensor(ch(X, c), ch(X, c), ch(T4, c), ALU.add).then_inc(S("x5_ready"), 1)

            ln_vector(dve, "a5", A)
            dve.wait_ge(*when("r5_logits", NCH))
            link(nc.vector.tensor_copy(ch(T1, 0), bank[7][:, :]))
            softmax_vector(P, 2 * TILES, lg5, s5a, "sm4")
            top2(P, 2 * TILES, lg5, wk5, o15, o25, s5a, s5b, s5f)
            link(nc.vector.tensor_tensor(s5f, s5a, s5b, ALU.add))
            link(nc.vector.tensor_scalar(s5f, s5f, 1e-9, None, ALU.add))
            link(nc.vector.reciprocal(s5f, s5f))
            link(nc.vector.tensor_tensor(s5a, s5a, s5f, ALU.mult))
            link(nc.vector.tensor_tensor(s5b, s5b, s5f, ALU.mult))
            nc.vector.tensor_tensor(sel5, ch(T1, 2), ch(T1, 3), ALU.add).then_inc(S("sel5"), 1)
            dve.wait_ge(*when("counted5", 2))
            link(nc.vector.tensor_copy(tot5, bank[2][:, :]))
            src, dst = tot5, pre5a
            for d in (1, 2, 4, 8, 16):
                w = 16 * d
                nc.vector.tensor_copy(dst[:, 0:w], src[:, 0:w]).then_inc(S("pre5"), 1)
                link(nc.vector.tensor_tensor(dst[:, w:], src[:, w:], src[:, 0:CHUNK - w], ALU.add))
                src, dst = dst, (pre5b if dst is pre5a else pre5a)
                dve.wait_ge(*when("pre5", {1: 1, 2: 2, 4: 3, 8: 4, 16: 5}[d]))
            incl = src
            link(nc.vector.tensor_scalar(nt5, incl[:, CHUNK - 16:], 1.0 / SLOTS,
                                         (SLOTS - 1) / SLOTS - 0.5 + 0.5 / SLOTS, ALU.mult, ALU.add))
            link(nc.vector.tensor_scalar(nt5, nt5, 2.0 ** 23, None, ALU.add))
            link(nc.vector.tensor_scalar(nt5, nt5, -2.0 ** 23, None, ALU.add))
            src, dst = nt5, end5
            for d in (1, 2, 4):
                s3_, d3_ = (v.rearrange("p (h e) -> p h e", e=E) for v in (src, dst))
                link(nc.vector.tensor_copy(d3_[:, :, 0:d], s3_[:, :, 0:d]))
                link(nc.vector.tensor_tensor(d3_[:, :, d:], s3_[:, :, d:], s3_[:, :, 0:E - d], ALU.add))
                src, dst = dst, (end5b if dst is end5 else end5)
            ends = src
            link(nc.vector.tensor_tensor(start5, ends, nt5, ALU.subtract))
            link(nc.vector.tensor_tensor(incl, incl, tot5, ALU.subtract))
            link(nc.vector.tensor_tensor(pos5, incl, bank[1][:, :], ALU.add))
            pos5v = pos5.rearrange("p (j g) -> p j g", g=16)
            link(nc.vector.scalar_tensor_tensor(pos5v, start5.unsqueeze(1).broadcast_to([P, TILES, 16]),
                                                float(SLOTS), pos5v, ALU.mult, ALU.add))
            for k, one in enumerate((ch(T1, 2), ch(T1, 3))):
                link(nc.vector.tensor_tensor(prod5, one, pos5, ALU.mult))
                link(nc.vector.tensor_reduce(slot5[:, 64 * k:64 * k + 64],
                                             prod5.rearrange("p (n e) -> p n e", e=E), AX, ALU.add))
                nc.vector.tensor_copy(index[:, k, :], slot5[:, 64 * k:64 * k + 64]).then_inc(S("index5"), 1)
            for c in range(NCH):
                dve.wait_ge(*when("rows5_high", c + 1))
                r = rows5v[:, 4 * c:4 * c + 4]
                nc.vector.tensor_tensor(r[:, :, :, C:], bank[3 + c % 4][:, :].rearrange("p (j h c) -> p j h c", h=2, c=C),
                                        r[:, :, :, 0:C], ALU.subtract).then_inc(S("rows5_low"), 1)
            c5 = cmp5.rearrange("p (h t e) -> p h t e", h=2, e=E)
            for h in range(2):
                link(nc.vector.tensor_tensor(
                    c5[:, h], mats[0:1, M["iota"], 0:NT].unsqueeze(2).broadcast_to([1, NT, E]),
                    ends[0:1, E * h:E * h + E].unsqueeze(1).broadcast_to([1, NT, E]), ALU.is_ge))
            link(nc.vector.tensor_reduce(exp5, cmp5.rearrange("p (t e) -> p t e", e=E), AX, ALU.add))
            link(nc.vector.tensor_scalar(exp5, exp5, float(E - 1), None, ALU.min))
            digits = exp5[:, 0:2 * NT].rearrange("p (b r) -> p b r", r=ROUND)
            link(nc.vector.tensor_copy(pack5, digits[:, :, ROUND - 1]))
            for r in range(ROUND - 2, -1, -1):
                link(nc.vector.scalar_tensor_tensor(pack5, pack5, float(E), digits[:, :, r], ALU.mult, ALU.add))
            link(nc.vector.tensor_scalar(pack5, pack5, float(E), None, ALU.mult))
            link(nc.vector.tensor_tensor(pack5[:, 1:], pack5[:, 1:], digits[:, 0:2 * NT // ROUND - 1, ROUND - 1], ALU.add))
            nc.vector.tensor_copy(expert[:, :], pack5).then_inc(S("expert5"), 1)
            def tile_vector(b, s):
                t = 2 * b + s
                for k in range(NHB):
                    n, q = t * NHB + k, k % 3
                    dve.wait_ge(*when("silu5", n + 1))
                    if later(n, 3):
                        dve.wait_ge(*when("low5", n - 2))
                    nc.vector.tensor_tensor(H5[q], bank[3 + q][0:HB, :], S5[q], ALU.mult).then_inc(S("hid5"), 1)
                    if later(n, 1):
                        low5(n - 1, (k - 1) % 3)
                    if k == 2 and later(t, 1):
                        sum5(t - 1, (s - 1) % 2)

            def low5(n, q):
                dve.wait_ge(*when("high5", n + 1))
                if later(n, 3):
                    dve.wait_ge(*when("down5", n - 2))
                nc.vector.tensor_tensor(LO5[q], H5[q], HI5[q], ALU.subtract).then_inc(S("low5"), 1)

            def sum5(t, s):
                dve.wait_ge(*when("y5_high", t + 1))
                y = bank[6 + s][:, :].rearrange("p (i v c) -> p i v c", v=2, c=C)
                nc.vector.tensor_tensor(Y5[s], Y5[s], y[:, :, 1, :], ALU.add).then_inc(S("y5"), 1)

            steps3(dve, tile_vector)
            last = 2 * NT * NHB - 1
            low5(last, (NHB - 1) % 3)
            sum5(2 * NT - 1, 1)
            dve.wait_ge(*when("xtok", NCH))
            for h in range(2):
                for c in range(NCH):
                    n = h * NCH + c
                    dve.wait_ge(*when(f"gathered_{h}_{c}", 16 * 8))
                    g = G5[h][:, 4 * c:4 * c + 4]
                    for k, gate in enumerate((s5a, s5b)):
                        gk = gate.rearrange("p (j h) -> p j h", h=2)[:, 4 * c:4 * c + 4, h]
                        nc.vector.tensor_tensor(M5[:, :, k, :], g[:, :, k, :], gk.unsqueeze(2).broadcast_to([P, 4, C]),
                                                ALU.mult).then_inc(S("mix5"), 1)
                    dve.wait_ge(*when("mix5", 2 * n + 2))
                    link(nc.vector.tensor_tensor(M5[:, :, 0, :], M5[:, :, 0, :], M5[:, :, 1, :], ALU.add))
                    xv = xtok[:, 4 * c:4 * c + 4, h, :]
                    nc.vector.tensor_tensor(xv, xv, M5[:, :, 0, :], ALU.add).then_inc(S("mixed5"), 1)
                    dve.wait_ge(*when("mixed5", n + 1))

        @block.scalar
        def _(act):
            act.preload_act_table_set("natural_log_exp_and_others")
            act.wait_ge(*when("loaded_vecs", 16))
            for c in range(2 * NCH):
                act.wait_ge(*when("bias_hid", c + 1))
                nc.scalar.activation(ch((X, T4)[c // NCH], c % NCH), bank[c % NCH][:, :], ACT.Relu, bias=vec("cb1")) \
                    .then_inc(S("bias_relu"), 1)
            act.wait_ge(*when("lsc", 1))
            nc.scalar.activation(qscale, lsc, ACT.Exp).then_inc(S("qscale"), 1)
            gn_scalar(act, "g0")
            for t, T in (("q", T1), ("k", T2)):
                for c in range(NCH):
                    act.wait_ge(*when(t + "_biased", c + 1))
                    if t == "k":
                        act.wait_ge(*when("q_norm", c + 1))
                    nc.scalar.activation(ch(T3, c), ch(T, c), ACT.Square).then_inc(S(t + "_sq"), 1)
                for c in range(NCH):
                    act.wait_ge(*when(t + "_clip", c + 1))
                    nc.scalar.activation(ch(T3, c), ch(T3, c), ACT.Ln).then_inc(S(t + "_len"), 1)
                    act.wait_ge(*when(t + "_len", c + 1))
                    nc.scalar.activation(ch(T3, c), ch(T3, c), ACT.Exp, scale=-0.5, bias=vec("ln10")) \
                        .then_inc(S(t + "_rlen"), 1)

            def exp_and_copies(k, w):
                n, s = at(k, 0), w % 2
                if n is not None:
                    act.wait_ge(*when("l0_shifted", n + 1))
                    reused(act, "l0_turned", n)
                    nc.scalar.activation(PR[s], SC[s], ACT.Exp).then_inc(S("l0_exp"), 1)
                n, s = at(k, 1), (w + 1) % 2
                if n is not None:
                    act.wait_ge(*when("l0_turned", n + 1))
                    reused(act, "l0_pv", n)
                    nc.scalar.activation(PT[s], bank[2 + s][:, :], ACT.Copy).then_inc(S("l0_pt"), 1)
                n = at(k, 3)
                if n is not None:
                    act.wait_ge(*when("l0_ot", n + 1))
                    nc.scalar.activation(T3[:, bass.ds(n * WT, WT)], bank[6 + s][:, 0:WT], ACT.Identity,
                                         bias=vec("bv0")).then_inc(S("l0_o"), 1)

            act.wait_ge(*when("bias_z", 1))
            nc.scalar.activation(ch(T4, 4), bank[0][:, :], ACT.Exp, scale=-1.0).then_inc(S("bias_exp"), 1)
            act.wait_ge(*when("k_norm", NCH))
            steps(act, exp_and_copies, 3)
            gn_scalar(act, "g1")
            nc.scalar.activation(bnv[:, 1:2], vec("va1"), ACT.Ln, bias=vec("eps3")).then_inc(S("bn_sd"), 1)
            act.wait_ge(*when("bn_sd", 1))
            nc.scalar.activation(bnv[:, 2:3], bnv[:, 1:2], ACT.Exp, scale=-0.5).then_inc(S("bn_rs"), 1)
            act.wait_ge(*when("bn_v", 3))
            for c in range(NCH):
                act.wait_ge(*when("r_proj", c + 1))
                nc.scalar.activation(ch(T1, c), bank[c][:, :], ACT.Relu, bias=bnv[:, 5:6], scale=bnv[:, 3:4]) \
                    .then_inc(S("r_ready"), 1)
            act.wait_ge(*when("pad_zero", 1))
            for c in range(NCH):
                act.wait_ge(*when("xi_proj", c + 1))
                nc.scalar.activation(PAD[:, 2 * c:2 * c + 2, 1:1 + HH, 1:1 + WW],
                                     bank[c][:, :].rearrange("p (b r c) -> p b r c", r=HH, c=WW),
                                     ACT.Identity, bias=vec("bi1")).then_inc(S("xi_kept"), 1)
            for k in range(NCH * KK):
                act.wait_ge(*when("tap_prod", k + 1))
                if k >= 4:
                    act.wait_ge(*when("tap_summed", k - 3))
                nc.scalar.activation(PROD_HI[k % 4], PROD[k % 4], ACT.Copy).then_inc(S("tap_high"), 1)
            ln_scalar(act, "a2", "eps5")
            for c in range(NCH):
                act.wait_ge(*when("k2_biased", c + 1))
                nc.scalar.activation(ch(T1, c), ch(T1, c), ACT.Square).then_inc(S("k2_sq"), 1)
            for c in range(NCH):
                act.wait_ge(*when("k2_ready", c + 1))
                nc.scalar.activation(ch(T2, c), ch(T1, c), ACT.Square).then_inc(S("k2_fourth"), 1)
            act.wait_ge(*when("k2_clip", 1))
            nc.scalar.activation(kln, knorm, ACT.Ln).then_inc(S("k2_ln"), 1)
            act.wait_ge(*when("k2_ln", 1))
            nc.scalar.activation(krs, kln, ACT.Exp, scale=-0.5, bias=vec("ln16")).then_inc(S("k2_rs"), 1)
            act.wait_ge(*when("kv2", HALF))
            act.wait_ge(*when("k2_norm", 1))
            act.wait_ge(*when("w2_kept", 5))

            def q_rs(c):
                act.wait_ge(*when("q2_clip", c + 1))
                nc.scalar.activation(ch(T1, c), ch(T1, c), ACT.Ln, bias=vec("tiny")).then_inc(S("q2_ln"), 1)
                act.wait_ge(*when("q2_ln", c + 1))
                nc.scalar.activation(ch(T1, c), ch(T1, c), ACT.Exp, scale=-0.5, bias=vec("ln20")) \
                    .then_inc(S("q2_rs"), 1)

            for c in range(NCH):
                act.wait_ge(*when("q2_proj", c + 1))
                nc.scalar.activation(ch(T2, c), bank[c % 4][:, :], ACT.Square, bias=bqc).then_inc(S("q2_sq"), 1)
                act.wait_ge(*when("q2_sq", c + 1))
                nc.scalar.activation(ch(T4, c), ch(T2, c), ACT.Square).then_inc(S("q2_fourth"), 1)
                act.wait_ge(*when("q2_s1", c + 1))
                nc.scalar.activation(ch(T1, c), bank[c % 4][:, :], ACT.Square, scale=1e-12 * 2.0 ** 20,
                                     bias=vec("guard")).then_inc(S("q2_guard"), 1)
                if c >= 1:
                    q_rs(c - 1)
            q_rs(NCH - 1)
            for c in range(NCH):
                act.wait_ge(*when("t2", c + 1))
                nc.scalar.activation(ch(T1, c), bank[c][:, :], ACT.Identity, bias=vec("bv2")) \
                    .then_inc(S("t2_kept"), 1)
            ln_scalar(act, "a3", "eps5")
            act.wait_ge(*when("a3", NCH))
            for c in range(NCH):
                nc.scalar.activation(ch(X16[0], c), ch(A, c), ACT.Copy).then_inc(S("x16_high"), 1)

            def half_inputs(n):
                act.wait_ge(*when("xs2_sel", n + 1))
                nc.scalar.activation(ch(XS2[n % 2], n // 2), bank[4 + n % 4][:, :], ACT.Copy).then_inc(S("xs2"), 1)

            for t in ("sm1", "sm2"):
                act.wait_ge(*when(t + "_in", 1))
                nc.scalar.activation(lg, lg, ACT.Exp).then_inc(S(t + "_exp"), 1)
            for n in range(NCH):
                half_inputs(n)
            act.wait_ge(*when("sm3_in", 1))
            nc.scalar.activation(s2b, s2b, ACT.Exp).then_inc(S("sm3_exp"), 1)
            for n in range(NCH, 2 * NCH):
                half_inputs(n)

            act.preload_act_table(ACT.Gelu)

            def high3(n, u):
                act.wait_ge(*when("gelu3", n + 1))
                if later(n, 4):
                    act.wait_ge(*when("down3", n - 3))
                nc.scalar.activation(HID_HI[u], HID[u], ACT.Copy).then_inc(S("high3"), 1)

            def image_scalar(k, p):
                b = at2(k, 0)
                for u in range(4):
                    if b is not None:
                        n = 4 * b + u
                        act.wait_ge(*when("up3", n + 1))
                        if later(n, 4):
                            act.wait_ge(*when("low3", n - 3))
                        nc.scalar.activation(HID[u], bank[u][:, 0:N], ACT.Gelu, bias=b1sel[:, bass.ds(n, 1)]) \
                            .then_inc(S("gelu3"), 1)
                        if later(n, 1):
                            high3(n - 1, (u - 1) % 4)
                    elif u == 0:
                        high3(4 * HALF - 1, 3)

            act.wait_ge(*when("expert2", 1))
            steps2(act, image_scalar, 1)
            ln_scalar(act, "l3", "eps5")
            ln_scalar(act, "a4", "eps5")
            rms_scalar(act, "n4", A, "a4", "eps6")
            for t, T in (("k", T3), ("q", T2)):
                for c in range(NCH):
                    act.wait_ge(*when(t + "4_neg", c + 1))
                    nc.scalar.activation(ch(T, c), ch(T, c), ACT.Exp).then_inc(S(t + "4_exp"), 1)
            for c in range(NCH):
                act.wait_ge(*when("den4", c + 1))
                nc.scalar.activation(ch(T3, c), bank[c % 4][:, :], ACT.Ln, bias=vec("eps6")).then_inc(S("z4_ln"), 1)
                act.wait_ge(*when("z4_ln", c + 1))
                nc.scalar.activation(ch(T3, c), ch(T3, c), ACT.Exp, scale=-1.0).then_inc(S("z4"), 1)
            rms_scalar(act, "m4", T4, "h4", "eps6")
            ln_scalar(act, "a5", "eps5")
            act.wait_ge(*when("sm4_in", 1))
            nc.scalar.activation(ch(T1, 0), ch(T1, 0), ACT.Exp).then_inc(S("sm4_exp"), 1)
            for c in range(NCH):
                act.wait_ge(*when("x_turned", c + 1))
                nc.scalar.activation(ch(T4, c), bank[3 + c % 4][:, :], ACT.Copy).then_inc(S("xtok"), 1)
            for c in range(NCH):
                act.wait_ge(*when("a_turned", c + 1))
                nc.scalar.activation(rows5v[:, 4 * c:4 * c + 4, :, 0:C],
                                     bank[3 + c % 4][:, :].rearrange("p (j h c) -> p j h c", h=2, c=C), ACT.Copy) \
                    .then_inc(S("rows5_high"), 1)

            def turned_x(t, s):
                act.wait_ge(*when("turned5", t + 1))
                nc.scalar.activation(XT[s], bank[6 + s][:, :], ACT.Copy).then_inc(S("xt5"), 1)

            def high5(n, q):
                act.wait_ge(*when("hid5", n + 1))
                if later(n, 3):
                    act.wait_ge(*when("down5", n - 2))
                nc.scalar.activation(HI5[q], H5[q], ACT.Copy).then_inc(S("high5"), 1)

            def result5(t, s, b):
                act.wait_ge(*when("down5", NHB * t + NHB))
                if later(t, 2):
                    act.wait_ge(*when(f"stored_y_{s}", 16 * b))
                y = bank[6 + s][:, :].rearrange("p (i v c) -> p i v c", v=2, c=C)
                nc.scalar.activation(Y5[s], y[:, :, 0, :], ACT.Copy).then_inc(S("y5_high"), 1)

            def tile_scalar(b, s, final=False):
                t = 2 * b + s
                for k in range(NHB):
                    n, q = t * NHB + k, k % 3
                    act.wait_ge(*when("up5", n + 1))
                    if later(n, 3):
                        act.wait_ge(*when("hid5", n - 2))
                    nc.scalar.activation(S5[q], bank[q][0:HB, :], ACT.Silu).then_inc(S("silu5"), 1)
                    if later(n, 1):
                        high5(n - 1, (k - 1) % 3)
                    if k == 2 and later(t, 1):
                        result5(t - 1, (s - 1) % 2, b - 1 if s == 0 else b)
                    if k == 4 and not final:
                        turned_x(t + 1, (s + 1) % 2)

            turned_x(0, 0)
            for t in range(2):
                tile_scalar(0, t)
            with act.Fori(1, NT - 1) as b:
                for r in range(2):
                    tile_scalar(b, r)
            for r in range(2):
                tile_scalar(NT - 1, r, final=(r == 1))
            high5(2 * NT * NHB - 1, (NHB - 1) % 3)
            result5(2 * NT - 1, 1, NT - 1)

        @block.tensor
        def _(pe):
            pe.wait_ge(*when("loaded_vecs", 16))
            pe.wait_ge(*when("loaded_feats", 32))
            for c in range(2 * NCH):
                if c >= NCH:
                    pe.wait_ge(*when("bias_relu", c - NCH + 1))
                keys = T2[0:2, c * 4 * WT:(c + 1) * 4 * WT].rearrange("p (k q) -> p k q", k=4)
                nc.tensor.matmul(bank[c % NCH][:, :], cw1, keys.unsqueeze(2).broadcast_to([2, 4, 2, WT]),
                                 start=True, stop=True).then_inc(S("bias_hid"), 1)
            pe.wait_ge(*when("loaded_mats", 16))
            pe.wait_ge(*when("bias_relu", 2 * NCH))
            gn_tensor(pe, "g0")
            for t in ("q", "k"):
                for c in range(NCH):
                    if t == "q":
                        pe.wait_ge(*when("g0_norm", 2 * (c + 1)))
                        if c == 0:
                            pe.wait_ge(*when("g0_grpc", 1))
                    else:
                        pe.wait_ge(*when("q_clip", c + 1))
                    nc.tensor.matmul(bank[c][:, :], mat(f"w{t}0"), ch(A, c), start=True, stop=True) \
                        .then_inc(S(t + "_proj"), 1)
                for c in range(NCH):
                    pe.wait_ge(*when(t + "_sq", c + 1))
                    nc.tensor.matmul(bank[c][:, :], mat("head"), ch(T3, c), start=True, stop=True) \
                        .then_inc(S(t + "_ssq"), 1)
            pe.wait_ge(*when("k_clip", 1))
            for key in range(WT):
                mm = nc.tensor.matmul(bank[0][:, key * HEADS:(key + 1) * HEADS],
                                      (X, T4)[key // 32][:, (key % 32) * 128:(key % 32 + 1) * 128],
                                      vec("w2c0", HEADS), start=True, stop=True)
            mm.then_inc(S("bias_z"), 1)
            pe.wait_ge(*when("wv_low", 1))
            pe.wait_ge(*when("a16_low", NCH))
            for g in range(PAIRS // 4):
                if g == 0:
                    pe.wait_ge(*when("bias_exp", 1))
                elif g < NCH:
                    pe.wait_ge(*when("k_clip", g + 1))
                else:
                    pe.wait_ge(*when("v_ready", 2 * (g - NCH + 1)))
                for i in range(4):
                    n = 4 * g + i
                    for x in range(2):
                        for a, v in ((0, 0), (0, 1), (1, 0)):
                            mm = nc.tensor.matmul(
                                bank[g % NCH][64 * x:64 * x + 64, i * 64:(i + 1) * 64], A16[a][:, n * WT:(n + 1) * WT],
                                wv16[:, v, :].rearrange("p (g x d) -> p g x d", x=2, d=DH)[:, :, x, :],
                                start=(a + v == 0), stop=(a == 1))
                mm.then_inc(S("v_proj"), 1)

            def attention(k, w):
                n, s = at(k, 0), w % 2
                if n is not None:
                    pe.wait_ge(*when("l0_staged", (n + 1) * 2))
                    reused(pe, "l0_shifted", n)
                    nc.tensor.matmul(bank[s][:, :], QB[s], KX[s], start=True, stop=False)
                    for v in range(2):
                        mm = nc.tensor.matmul(bank[s][:, :], ident16[:, :], BM16[:, w, v, :], start=False, stop=(v == 1))
                    mm.then_inc(S("l0_scores"), 1)
                n, s = at(k, 1), (w + 1) % 2
                if n is not None:
                    pe.wait_ge(*when("l0_exp", n + 1))
                    reused(pe, "l0_pt", n)
                    for g in range(HP):
                        mm = nc.tensor.transpose(bank[2 + s][:, g * 128:(g + 1) * 128],
                                                 PR[s][:, g * 128:(g + 1) * 128], mat("ident"))
                    mm.then_inc(S("l0_turned"), 1)
                n, s = at(k, 2), w % 2
                if n is not None:
                    pe.wait_ge(*when("l0_pt", n + 1))
                    reused(pe, "l0_obd", n)
                    for g in range(HP):
                        mm = nc.tensor.matmul(bank[4 + s][:, g * VW:(g + 1) * VW], PT[s][:, g * 128:(g + 1) * 128],
                                              VX[:, bass.ds(n * HP + g, 1), :].rearrange("p a v -> p (a v)"),
                                              start=True, stop=True)
                    mm.then_inc(S("l0_pv"), 1)
                n, s = at(k, 3), (w + 1) % 2
                if n is not None:
                    pe.wait_ge(*when("l0_obd", n + 1))
                    reused(pe, "l0_o", n)
                    nc.tensor.matmul(bank[6 + s][:, 0:WT], OB[s], ident2, start=True, stop=True) \
                        .then_inc(S("l0_ot"), 1)

            pe.wait_ge(*when("v_ready", PAIRS // 2))
            pe.wait_ge(*when("vx_ones", 2))
            pe.wait_ge(*when("ident16", 1))
            steps(pe, attention, 3)
            for c in range(NCH):
                pe.wait_ge(*when("l0_o", PAIRS))
                nc.tensor.matmul(bank[c][:, :], mat("wo0"), ch(T3, c), start=True, stop=True) \
                    .then_inc(S("l0_wo"), 1)
            gn_tensor(pe, "g1")
            for c in range(NCH):
                pe.wait_ge(*when("g1_norm", 2 * (c + 1)))
                nc.tensor.matmul(bank[c][:, :], mat("wr1"), ch(A, c), start=True, stop=True) \
                    .then_inc(S("r_proj"), 1)
            for c in range(NCH):
                pe.wait_ge(*when("r_ready", c + 1))
                nc.tensor.matmul(bank[c][:, :], mat("wi1"), ch(A, c), start=True, stop=True) \
                    .then_inc(S("xi_proj"), 1)
            pe.wait_ge(*when("xi_kept", NCH))
            pe.wait_ge(*when("taps16", 3))
            pe.wait_ge(*when("r_low", NCH))

            def tap_sum(k):
                c, t = k // KK, k % KK
                pe.wait_ge(*when(*low_parts(k)))
                if t == 0 and c >= 2:
                    pe.wait_ge(*when("x2_ready", c - 1))
                nc.tensor.matmul(bank[4 + c % 2][:, :], taps16[:, t, :], PROD_HI[k % 4], start=(t == 0), stop=False)
                nc.tensor.matmul(bank[4 + c % 2][:, :], taps16[:, t, :], PROD_LO[k % 4], start=False,
                                 stop=(t == KK - 1)).then_inc(S("tap_summed"), 1)

            for k in range(NCH * KK):
                if k >= 4:
                    pe.wait_ge(*when("tap_prod", k - 3))
                for v in range(2):
                    mm = nc.tensor.matmul(bank[k % 4][:, :], wexp16[:, k % KK, v, :], ch(R16, k // KK),
                                          start=(v == 0), stop=(v == 1))
                mm.then_inc(S("tap_w"), 1)
                if k >= 4:
                    tap_sum(k - 4)
            for k in range(NCH * KK - 4, NCH * KK):
                tap_sum(k)
            ln_tensor(pe, "a2", X, "x2_ready", lambda c: c + 1, left=NCH)
            pe.wait_ge(*when("a2", NCH))
            for i, (left, right) in enumerate(((mat("wq2t"), mat("centre")), (mat("wk2t"), mat("centre")),
                                               (vec("bk2").broadcast_to([P, 128]), mat("centre")),
                                               (vec("bv2").broadcast_to([P, 128]), mat("ident")))):
                nc.tensor.matmul(bank[i][:, 0:128], left, right, start=True, stop=True).then_inc(S("w2_centred"), 1)
            nc.tensor.matmul(bank[4][:, 0:1], mat("centre"), vec("bq2"), start=True, stop=True) \
                .then_inc(S("w2_centred"), 1)
            pe.wait_ge(*when("w2_kept", 5))
            for c in range(NCH):
                for j in range(4):
                    mm = nc.tensor.matmul(bank[c][:, j * 128:(j + 1) * 128],
                                          A[:, (4 * c + j) * 128:(4 * c + j + 1) * 128], mat("wk2t"),
                                          start=True, stop=True)
                mm.then_inc(S("k2_proj"), 1)
            for c in range(NCH):
                pe.wait_ge(*when("k2_biased", c + 1))
                for j in range(4):
                    mm = nc.tensor.matmul(bank[c][:, j * 128:(j + 1) * 128],
                                          A[:, (4 * c + j) * 128:(4 * c + j + 1) * 128], mat("wv2"),
                                          start=True, stop=True)
                mm.then_inc(S("v2_proj"), 1)
            pe.wait_ge(*when("v2_kept", NCH))
            for b in range(HALF):
                pe.wait_ge(*when("k2_fourth", b // 2 + 1))
                for j in range(2):
                    mm = nc.tensor.matmul(bank[4][:, b:b + 1], T2[:, (2 * b + j) * 128:(2 * b + j + 1) * 128],
                                          vec("one"), start=(j == 0), stop=(j == 1))
            mm.then_inc(S("k2_norm"), 1)
            for b in range(HALF):
                pe.wait_ge(*when("k2_ready", b // 2 + 1))
                for j in range(2):
                    tile = slice((2 * b + j) * 128, (2 * b + j + 1) * 128)
                    mm = nc.tensor.matmul(bank[b // 4][:, (b % 4) * 128:(b % 4 + 1) * 128], T1[:, tile], T3[:, tile],
                                          start=(j == 0), stop=(j == 1))
                mm.then_inc(S("kv2"), 1)

            def q_sums(c):
                pe.wait_ge(*when("q2_sq", c + 1))
                nc.tensor.matmul(bank[c % 4][:, :], mat("sum"), ch(T2, c), start=True, stop=True) \
                    .then_inc(S("q2_s1"), 1)
                pe.wait_ge(*when("q2_fourth", c + 1))
                if c >= 4:
                    pe.wait_ge(*when("q2_clip", c - 3))
                nc.tensor.matmul(bank[4 + c % 4][:, :], mat("sum"), ch(T4, c), start=True, stop=True) \
                    .then_inc(S("q2_s2"), 1)

            pe.wait_ge(*when("kv2_kept", HALF))
            pe.wait_ge(*when("k2_clip", 1))
            for c in range(NCH):
                if c >= 4:
                    pe.wait_ge(*when("q2_guard", c - 3))
                nc.tensor.matmul(bank[c % 4][:, :], mat("wq2t"), ch(A, c), start=True, stop=True) \
                    .then_inc(S("q2_proj"), 1)
                if c >= 1:
                    q_sums(c - 1)
            q_sums(NCH - 1)
            pe.wait_ge(*when("q2_clip", NCH))
            for c in range(NCH):
                pe.wait_ge(*when("q2_ready", c + 1))
                for i in range(2):
                    b = 2 * c + i
                    nc.tensor.matmul(bank[c][:, i * N:(i + 1) * N], mat("wv2"), A[:, b * N:(b + 1) * N],
                                     start=True, stop=False)
                    mm = nc.tensor.matmul(bank[c][:, i * N:(i + 1) * N], KVS[:, b, :], T2[:, b * N:(b + 1) * N],
                                          start=False, stop=True)
                mm.then_inc(S("t2"), 1)
            for c in range(NCH):
                pe.wait_ge(*when("t2_kept", c + 1))
                nc.tensor.matmul(bank[c][:, :], mat("wo2"), ch(T1, c), start=True, stop=True) \
                    .then_inc(S("o2_proj"), 1)
            ln_tensor(pe, "a3", X, "x3_ready", lambda c: c + 1)
            pe.wait_ge(*when("a3", NCH))
            pe.wait_ge(*when("r3_mean", NCH))
            nc.tensor.matmul(bank[0][0:HALF, 0:16], xmean, mat("rt3")[:, 0:16], start=True, stop=True) \
                .then_inc(S("r3_logits"), 1)
            pe.wait_ge(*when("r3_rw", 1))
            nc.tensor.matmul(bank[1][0:HALF, 0:16], vec("one")[0:HALF, :].broadcast_to([HALF, HALF]), lc,
                             start=True, stop=True).then_inc(S("r3_load"), 1)
            pe.wait_ge(*when("half16", 1))
            for n in range(2 * NCH):
                pe.wait_ge(*when("x16_low", n // 2 + 1))
                if n >= 4:
                    pe.wait_ge(*when("xs2", n - 3))
                for v in range(2):
                    mm = nc.tensor.matmul(bank[4 + n % 4][64 * v:64 * v + 64, :], half16[:, n % 2, 64 * v:64 * v + 64],
                                          ch(X16[v], n // 2), start=True, stop=True)
                mm.then_inc(S("xs2_sel"), 1)
            pe.wait_ge(*when("r3_hot", 6))
            ones = vec("one")[0:HALF, :].broadcast_to([HALF, 128])
            nc.tensor.matmul(bank[3][:, :], ones, odiag, start=True, stop=True).then_inc(S("r3_chosen"), 1)
            nc.tensor.matmul(bank[2][:, 256:320], ones, kdiag, start=True, stop=True).then_inc(S("r3_chosen"), 1)
            pe.wait_ge(*when("r3_diag", 1))
            pe.wait_ge(*when("xs2", 2 * NCH))
            nc.tensor.matmul(bank[6][:, 0:256], vec("one")[0:HALF, :].broadcast_to([HALF, 128]), gdiag,
                             start=True, stop=True).then_inc(S("r3_gates"), 1)
            pe.wait_ge(*when("expert2", 1))
            pe.wait_ge(*when("l2_split", 4))
            pe.wait_ge(*when("xs2", 2 * NCH))

            def down3(n, i, p, e):
                h, k = i // 2, i % 2
                pe.wait_ge(*when("low3", n + 1))
                for v, H in ((0, HID_HI[i]), (1, HID_HI[i]), (0, HID_LO[i])):
                    mm = nc.tensor.matmul(bank[4 + p][:, k * N:(k + 1) * N],
                                          down2[:, bass.ds(e * (6 * C) + (v * 3 * C + (1 - h) * C), 2 * C)], H,
                                          start=(i == 0 and v == 0 and H is HID_HI[i]),
                                          stop=(i == 3 and H is HID_LO[i]), skip_group_check=True)
                mm.then_inc(S("down3"), 1)

            def image_tensor(k, p):
                b = at2(k, 0)
                v = pe.value_load(expert2[0:1, bass.ds(HALF - 1 if b is None else b, 1)], min_val=0, max_val=E ** 7 - 1)
                e = [pe.snap((v >> (3 * i)) & (E - 1), min_val=0, max_val=E - 1) for i in range(7)]
                if b is None:
                    for i in range(1, 4):
                        down3(4 * HALF - 4 + i, i, (p + 1) % 2, e[3 + i])
                    return
                for u in range(4):
                    n = 4 * b + u
                    if later(n, 4):
                        pe.wait_ge(*when("gelu3", n - 3))
                    for v in range(2):
                        mm = nc.tensor.matmul(bank[u][:, 0:N],
                                              l2w[:, 0:E * FH].bitcast(F16)[:, bass.ds(e[3 + u] * (2 * FH) + v * FH, FH)],
                                              XS2[u // 2][:, bass.ds(b * N, N)], start=(v == 0), stop=(v == 1))
                    mm.then_inc(S("up3"), 1)
                    if u == 3:
                        if later(b, 2):
                            pe.wait_ge(*when("y3_kept", b - 1))
                        down3(n - 3, 0, p, e[3])
                    elif later(b, 1):
                        down3(n - 3, u + 1, (p + 1) % 2, e[u])

            steps2(pe, image_tensor, 1)
            ln_tensor(pe, "l3", T1, "y3_kept", lambda c: 2 * (c + 1), left=HALF)
            ln_tensor(pe, "a4", X, "x4_ready", lambda c: c + 1)
            pe.wait_ge(*when("a4", NCH))
            rms_tensor(pe, "n4")
            for c in range(NCH):
                pe.wait_ge(*when("n4", c + 1))
                for j in range(4):
                    mm = nc.tensor.matmul(bank[c][:, j * 128:(j + 1) * 128],
                                          T1[:, (4 * c + j) * 128:(4 * c + j + 1) * 128], mat("wk4"),
                                          start=True, stop=True)
                mm.then_inc(S("k4_proj"), 1)
            for c in range(NCH):
                pe.wait_ge(*when("k4_elu", c + 1))
                for j in range(4):
                    mm = nc.tensor.matmul(bank[c][:, j * 128:(j + 1) * 128],
                                          T1[:, (4 * c + j) * 128:(4 * c + j + 1) * 128], mat("wv4"),
                                          start=True, stop=True)
                mm.then_inc(S("v4_proj"), 1)
            pe.wait_ge(*when("v4_kept", NCH))
            for b in range(HALF):
                for j in range(2):
                    tile = slice((2 * b + j) * 128, (2 * b + j + 1) * 128)
                    mm = nc.tensor.matmul(bank[b // 4][:, (b % 4) * 128:(b % 4 + 1) * 128], T3[:, tile], T4[:, tile],
                                          start=(j == 0), stop=(j == 1))
                mm.then_inc(S("kv4"), 1)
            for b in range(HALF):
                for j in range(2):
                    mm = nc.tensor.matmul(bank[4][:, b:b + 1], T3[:, (2 * b + j) * 128:(2 * b + j + 1) * 128],
                                          vec("one"), start=(j == 0), stop=(j == 1))
            mm.then_inc(S("ks4"), 1)
            pe.wait_ge(*when("kv4_kept", 4))
            pe.wait_ge(*when("ks4_kept", 1))
            for c in range(NCH):
                nc.tensor.matmul(bank[c][:, :], mat("wq4"), ch(T1, c), start=True, stop=True) \
                    .then_inc(S("q4_proj"), 1)
            pe.wait_ge(*when("kv4_kept", 8))
            pe.wait_ge(*when("q4_elu", NCH))
            for c in range(NCH):
                if c >= 4:
                    pe.wait_ge(*when("z4", c - 3))
                    pe.wait_ge(*when("o4", c - 3))
                for t, W, k in (("den4", KSS, 0), ("num4", KVS, 4)):
                    for i in range(2):
                        b = 2 * c + i
                        mm = nc.tensor.matmul(bank[k + c % 4][:, i * N:(i + 1) * N], W[:, b, :],
                                              T2[:, b * N:(b + 1) * N], start=True, stop=True)
                    mm.then_inc(S(t), 1)
            pe.wait_ge(*when("o4", NCH))
            for c in range(NCH):
                nc.tensor.matmul(bank[c][:, :], mat("wo4"), ch(T1, c), start=True, stop=True) \
                    .then_inc(S("o4_proj"), 1)
            rms_tensor(pe, "m4")
            def logits5(c):
                pe.wait_ge(*when("x5_ready", NCH))
                pe.wait_ge(*when("a5", c + 1))
                for j in range(4 * c, 4 * c + 4):
                    mm = nc.tensor.matmul(bank[7][:, 16 * j:16 * j + 16], A[:, j * 128:(j + 1) * 128],
                                          mat("rt5")[:, 0:16], start=True, stop=True)
                mm.then_inc(S("r5_logits"), 1)

            ln_tensor(pe, "a5", X, "x5_ready", lambda c: c + 1, also=logits5)
            for t, T, free in (("x_turned", X, "xtok"), ("a_turned", A, "rows5_low")):
                for c in range(NCH):
                    if t == "a_turned" and c < 4:
                        pe.wait_ge(*when("xtok", c + 5))
                    elif c >= 4:
                        pe.wait_ge(*when(free, c - 3))
                    for j in range(4):
                        mm = nc.tensor.transpose(bank[3 + c % 4][:, j * 128:(j + 1) * 128],
                                                 T[:, (4 * c + j) * 128:(4 * c + j + 1) * 128], mat("ident"))
                    mm.then_inc(S(t), 1)
                if t == "x_turned":
                    pe.wait_ge(*when("sel5", 1))
                    for i, w in ((1, mat("before")), (2, vec("one").broadcast_to([P, 128]))):
                        nc.tensor.matmul(bank[i][:, :], w, sel5, start=True, stop=True).then_inc(S("counted5"), 1)

            pe.wait_ge(*when("ident16", 1))
            pe.wait_ge(*when("expert5", 1))
            pe.wait_ge(*when("rows5_low", NCH))
            pe.wait_ge(*when("index5", 2))
            pe.wait_ge(*when("ups_split", 2 * 3 * E))

            def turn5(b, s):
                t = 2 * b + s
                pe.wait_ge(*when(f"loaded_xs_{s}", 16 * (b + 1)))
                if later(t, 2):
                    pe.wait_ge(*when("y5", t - 1))
                for i in range(SUB):
                    mm = nc.tensor.matmul(bank[6 + s][:, i * 128:(i + 1) * 128], XS[s][:, i, :], ident16[:, :],
                                          start=True, stop=True)
                mm.then_inc(S("turned5"), 1)

            def down5(n, t, k, s, e):
                pe.wait_ge(*when("low5", n + 1))
                q = k % 3
                w = e * (NHB * 2 * C) + k * 2 * C
                for v, H in enumerate((LO5[q], HI5[q])):
                    for i in range(SUB):
                        mm = nc.tensor.matmul(bank[6 + s][:, i * 128:(i + 1) * 128], H[:, i * 128:(i + 1) * 128],
                                              downs[:, bass.ds(w, 2 * C)], start=(k == 0 and v == 0 and i == 0),
                                              stop=(k == NHB - 1 and v == 1 and i == SUB - 1), skip_group_check=True)
                mm.then_inc(S("down5"), 1)

            def experts_of(b):
                v = pe.value_load(expert[0:1, bass.ds(b, 1)], min_val=0, max_val=E ** (ROUND + 1) - 1)
                return [pe.snap((v >> (3 * i)) & (E - 1), min_val=0, max_val=E - 1) for i in range(ROUND + 1)]

            def tile_tensor(b, s, e, final=False, before=None):
                t = 2 * b + s
                pe.wait_ge(*when("xt5", t + 1))
                for k in range(NHB):
                    n, q = t * NHB + k, k % 3
                    if later(n, 3):
                        pe.wait_ge(*when("hid5", n - 2))
                    for v in range(4):
                        mm = nc.tensor.matmul(bank[q + 3 * (v // 2)][0:HB, :],
                                              big16[:, bass.ds(e * (4 * HID3) + (v * HID3 + k * HB), HB)], XT[s],
                                              start=(v % 2 == 0), stop=(v % 2 == 1))
                    mm.then_inc(S("up5"), 1)
                    if k >= 3:
                        down5(n - 3, t, k - 3, s, e)
                    elif before is not None:
                        down5(n - 3, t - 1, k + 3, (s - 1) % 2, before)
                    if k == 4 and not final:
                        turn5(b + 1 if s == 1 else b, (s + 1) % 2)

            def tiles_of(b, first=False, final=False):
                e = experts_of(b)
                for r in range(ROUND):
                    tile_tensor(b, r, e[r + 1], final and r == ROUND - 1,
                                None if first and r == 0 else e[r])
                return e[ROUND]

            turn5(0, 0)
            tiles_of(0, first=True)
            with pe.Fori(1, 2 * NT // ROUND - 1) as b:
                tiles_of(b)
            e = tiles_of(2 * NT // ROUND - 1, final=True)
            for k in range(3, NHB):
                down5((2 * NT - 1) * NHB + k, 2 * NT - 1, k, 1, e)


def blocks(w):
    a, b = w.shape
    m = np.zeros((128, 128), np.float32)
    m[:a, :b] = w
    m[64:64 + a, b:2 * b] = w
    return m


def constants():
    eye = np.eye(128, dtype=np.float32)
    same = np.kron(np.eye(2), np.ones((64, 64))).astype(np.float32)
    pair = np.kron(np.eye(64), np.ones((2, 2))).astype(np.float32) / 2
    head = np.kron(np.eye(16), np.ones((8, 8))).astype(np.float32)
    stack = np.zeros((128, 128), np.float32)
    stack[:, 0:64] = np.concatenate([np.eye(64)] * 2, 0)
    par = (np.arange(32) // 8) % 2
    stack[:64, 64:96] = par == 0
    stack[64:, 64:96] = par == 1
    mats = {"ident": eye, "mean": same / 64, "centre": eye - same / 64, "pair": pair, "head": head,
            "sum": same, "stack": stack, "before": np.triu(np.ones((128, 128), np.float32), 1),
            "half0": np.kron([[1, 1], [0, 0]], np.eye(64)).astype(np.float32),
            "half1": np.kron([[0, 0], [1, 1]], np.eye(64)).astype(np.float32),
            "iota": np.tile(np.arange(128, dtype=np.float32), (128, 1))}
    ws = WS
    r = np.arange(-(ws - 1), ws, dtype=np.float32)
    tbl = np.stack(np.meshgrid(r, r, indexing="ij"), axis=-1)
    tbl = tbl / (ws - 1) * 8.0
    tbl = np.sign(tbl) * np.log2(np.abs(tbl) + 1.0) / np.log2(8.0)
    tbl = tbl.reshape(-1, 2).astype(np.float32)
    c = np.stack(np.meshgrid(np.arange(ws), np.arange(ws), indexing="ij")).reshape(2, -1)
    rel = c[:, :, None] - c[:, None, :] + (ws - 1)
    idx = rel[0] * (2 * ws - 1) + rel[1]
    feats = np.ascontiguousarray(tbl[idx.T].reshape(-1, 2).T)
    img = np.zeros((HH, WW), np.int32)
    cnt = 0
    for hs in (slice(0, -ws), slice(-ws, -SS), slice(-SS, None)):
        for wsl in (slice(0, -ws), slice(-ws, -SS), slice(-SS, None)):
            img[hs, wsl] = cnt
            cnt += 1
    mw = img.reshape(HH // ws, ws, WW // ws, ws).transpose(0, 2, 1, 3).reshape(-1, ws * ws)
    mask = np.where(mw[:, None, :] != mw[:, :, None], -100.0, 0.0).astype(np.float32)
    wmask = np.ascontiguousarray(np.concatenate([mask.transpose(1, 0, 2)] * 2, 0))
    taps = np.zeros((128, KK, 128), np.float32)
    m = np.arange(KK * C)
    for h in range(2):
        taps[64 * h + m % C, m // C, 64 * h + m // KK] = 1
    widx = (m // KK // 4) * KK + m % KK
    return mats, feats, wmask, taps, widx


def halves(x):
    return np.ascontiguousarray(x.reshape(2, HALF, N, C).transpose(0, 3, 1, 2).reshape(P, COLS))


_INS = ["xw", "xi", "mats", "vecs", "feats", "cw1", "wmask", "taps", "wexp", "w1l2", "w2l2", "w1l3", "w3l3", "w2l3"]
OUTPUT_NAMES = [("out_0", (P, COLS))]


def kernel(x, **w):
    import concourse.bacc as _bacc
    from concourse.bass_utils import run_bass_kernel_spmd as _run

    w = {k: np.asarray(v) for k, v in w.items()}
    x = np.asarray(x)
    mats, feats, wmask, taps, widx = constants()
    rolled = np.roll(x, (-SS, -SS), axis=(1, 2)).reshape(B, 2, WS, 2, WS, C).transpose(0, 1, 3, 2, 4, 5)
    arr = {"xw": halves(rolled.reshape(B, N, C)), "xi": halves(x.reshape(B, N, C))}
    hp, par, d = np.meshgrid(np.arange(HP), np.arange(2), np.arange(DH), indexing="ij")
    chan = (hp * 16 + par * 8 + d).ravel()
    wv0 = np.zeros((128, 128), np.float32)
    wo0 = np.zeros((128, 128), np.float32)
    bv0 = np.zeros(128, np.float32)
    for h in range(2):
        col = (hp * 32 + h * 16 + par * 8 + d).ravel()
        wv0[64 * h:64 * h + 64, col] = w["L0_conv_Wv"].T[:, chan]
        wo0[col, 64 * h:64 * h + 64] = w["L0_conv_Wo"].T[chan, :]
        bv0[col] = w["L0_conv_bv"][chan]
    def twice(v):
        m = blocks(v)
        m[:, 64:96] = m[:, 0:32]
        return m

    qkv2, qkv4 = w["L2_attn_W_qkv"], w["L3_attn_w_qkv"]
    mats |= {"wq0": blocks(w["L0_conv_Wq"].T), "wk0": blocks(w["L0_conv_Wk"].T), "wv0": wv0, "wo0": wo0,
             "wi1": blocks(w["L1_conv_Wi"]), "wr1": twice(w["L1_conv_Wr"]),
             "wq2t": blocks(qkv2[:, 0:64].T), "wk2t": blocks(qkv2[:, 64:128].T), "wv2": blocks(qkv2[:, 128:192]),
             "wo2": blocks(w["L2_attn_W_out"]), "wq4": blocks(qkv4[:, 0:64]), "wk4": blocks(qkv4[:, 64:128]),
             "wv4": blocks(qkv4[:, 128:192]), "wo4": blocks(w["L3_attn_w_out"]),
             "rt3": blocks(w["L2_ffn_Wr"]), "rt5": blocks(w["L3_ffn_router_w"].T)}
    arr["mats"] = np.ascontiguousarray(np.stack([mats[n] for n in MATS], 1))
    two = lambda v: np.concatenate([v, v])
    gap = np.zeros(32, np.float32)
    padded = lambda v: np.concatenate([v, v, gap, v, v, gap])
    shift = padded(w["L1_conv_beta"]).astype(np.float32)
    shift[32] = 1
    vecs = {"bq0": two(w["L0_conv_bq"]), "bk0": two(w["L0_conv_bk"]), "bv0": bv0, "bo0": two(w["L0_conv_bo"]),
            "ls0": two(np.repeat(w["L0_conv_logit_scale"].reshape(-1), DH)), "bi1": two(w["L1_conv_bi"]),
            "br1": padded(w["L1_conv_br"]), "ga1": padded(w["L1_conv_gamma"]), "be1": shift,
            "mu1": padded(w["L1_conv_mean"]), "va1": padded(w["L1_conv_var"]),
            "bq2": two(w["L2_attn_b_qkv"][0:64]), "bk2": two(w["L2_attn_b_qkv"][64:128]),
            "bv2": two(w["L2_attn_b_qkv"][128:192]), "bo2": two(w["L2_attn_b_out"]),
            "ga3": two(w["L2_ffn_gamma"]), "be3": two(w["L2_ffn_beta"]), "n14": two(w["L3_attn_w_norm1"]),
            "bo4": two(w["L3_attn_b_out"]), "n24": two(w["L3_attn_w_norm2"]), "cb1": w["L0_conv_cpb_b1"],
            "eps6": np.full(128, 1e-6), "eps5": np.full(128, 1e-5), "eps3": np.full(128, 1e-3),
            "tiny": np.full(128, 2.0 ** -60), "ln10": np.full(128, 10 * np.log(2)), "ln20": np.full(128, 20 * np.log(2)),
            "ln16": np.full(128, 20 * np.log(2) - np.log(16)), "guard": np.full(128, 1e-19 * 2.0 ** 20),
            "one": np.ones(128), "par0": np.arange(128) < 64, "par1": np.arange(128) >= 64,
            "half0": np.arange(128) < 64, "half1": np.arange(128) >= 64}
    for e in range(E):
        vecs[f"w2c{e}"] = w["L0_conv_cpb_w2"][e]
        vecs[f"b1_{e}"] = w["L2_ffn_b1"][e]
        vecs[f"b2_{e}"] = two(w["L2_ffn_b2"][e])
        vecs[f"rank{e}"] = np.full(128, E - e)
        for h in range(2):
            vecs[f"brr{h * E + e}"] = np.broadcast_to(w["L2_ffn_br"][e], (128,))
    arr["vecs"] = np.ascontiguousarray(np.stack([np.asarray(vecs[n], np.float32) for n in VECS], 1))
    arr["feats"], arr["wmask"], arr["taps"] = feats, wmask, taps
    arr["cw1"] = np.ascontiguousarray(w["L0_conv_cpb_w1"].T)
    wexp = np.zeros((P, KK, 128), np.float32)
    for h in range(2):
        for t in range(KK):
            wexp[16 * h:16 * h + 16, t, 64 * h:64 * h + 64] = w["L1_conv_Ws"][:, widx[64 * t:64 * t + 64]]
            wexp[64 + 16 * h:80 + 16 * h, t, 64 * h:64 * h + 64] = wexp[16 * h:16 * h + 16, t, 64 * h:64 * h + 64]
            wexp[32, t, 64 * h:64 * h + 64] = w["L1_conv_bs"][widx[64 * t:64 * t + 64]]
    arr["wexp"] = wexp
    arr["w1l2"] = np.ascontiguousarray(np.tile(w["L2_ffn_W1"].transpose(1, 0, 2).reshape(C, E * FH), (2, 1)))
    arr["w2l2"] = np.ascontiguousarray(w["L2_ffn_W2"].transpose(1, 0, 2).reshape(FH, E * C))
    hid = HID3
    for name, key in (("w1l3", "L3_ffn_w1"), ("w3l3", "L3_ffn_w3")):
        up = np.zeros((128, E, hid), np.float32)
        for h in range(2):
            up[64 * h:64 * h + 64, :, :w[key].shape[1]] = w[key].transpose(2, 0, 1)
        arr[name] = up
    down = np.zeros((E, hid, C), np.float32)
    down[:, :w["L3_ffn_w2"].shape[2]] = w["L3_ffn_w2"].transpose(0, 2, 1)
    arr["w2l3"] = np.ascontiguousarray(down.reshape(E, NHB, HB, C).transpose(2, 0, 1, 3))

    nc = _bacc.Bacc("TRN2", target_bir_lowering=False, num_devices=1)
    args, arrays = [], {}
    for name in _INS:
        a = arr[name]
        arrays[f"in_{name}"] = a
        args.append(nc.dram_tensor(f"in_{name}", a.shape, F32, kind="ExternalInput").ap())
    args.append(nc.dram_tensor("out_0", (P, COLS), F32, kind="ExternalOutput").ap())
    n = NT * SLOTS
    args.append([nc.dram_tensor(f"slots{h}", (n, 2 * C), F16, kind="Internal").ap() for h in range(2)])
    args.append([nc.dram_tensor(f"results{h}", (n, C), F32, kind="Internal").ap() for h in range(2)])
    network(nc, *args)
    r = _run(nc, [arrays], core_ids=[0])
    y = np.asarray(r.results[0]["out_0"])
    return y.reshape(128, TILES, 2, C).transpose(2, 1, 0, 3).reshape(B, HH, WW, C)
```
